# Optimizing a Trainium2 kernel written in Bass

```python
import numpy as np
import jax
import jax.numpy as jnp

def _softmax(x, axis=-1):
    return jax.nn.softmax(x, axis=axis)

def _gelu(x):
    return jax.nn.gelu(x, approximate=True)

def _silu(x):
    return jax.nn.silu(x)

def _sigmoid(x):
    return jax.nn.sigmoid(x)

def _layernorm(x, axis=-1, eps=1e-05):
    m = jnp.mean(x, axis=axis, keepdims=True)
    v = jnp.var(x, axis=axis, keepdims=True)
    return (x - m) / jnp.sqrt(v + eps)

def _scatter_add(tgt, idx, src, axis=0):
    return tgt.at[idx].add(src)

def _segment_sum(src, seg, n):
    return jax.ops.segment_sum(src, seg, n)
kernel_name = 'mk_vit_tower_cls_d2_tok_img1024_r4_85040b'

def setup_inputs(seed: int=0):
    np.random.seed(seed)
    _w = jnp.asarray

    def _rec_inputs():
        import jax
        import jax.numpy as jnp
        _rk = jax.random.key(seed)
        x = -0.00016672 + 0.999947 * jax.random.normal(jax.random.fold_in(_rk, 1), (32, 3, 96, 96), jnp.float32)
        cls_tok = 0.02 * jax.random.normal(jax.random.fold_in(_rk, 5), (1, 1, 256), jnp.float32)
        return (x, cls_tok)
    x, cls_tok = _rec_inputs()

    def _L0_tok_setup():
        import jax, jax.numpy as jnp
        import numpy as np
        DIM = 256
        IMG = 96
        P = 16
        C = 3
        TEMP = 10000.0
        EPS = 1e-05
        PATCH_DIM = C * P * P
        HP = IMG // P

        def layernorm(x, gamma, beta):
            mu = jnp.mean(x, axis=-1, keepdims=True)
            var = jnp.var(x, axis=-1, keepdims=True)
            return (x - mu) * jax.lax.rsqrt(var + EPS) * gamma + beta

        def posemb_sincos_2d(h, w, dim, dtype):
            y, x = jnp.meshgrid(jnp.arange(h), jnp.arange(w), indexing='ij')
            omega = jnp.arange(dim // 4, dtype=jnp.float32) / (dim // 4 - 1)
            omega = 1.0 / TEMP ** omega
            y = y.reshape(-1)[:, None] * omega[None, :]
            x = x.reshape(-1)[:, None] * omega[None, :]
            pe = jnp.concatenate((jnp.sin(x), jnp.cos(x), jnp.sin(y), jnp.cos(y)), axis=1)
            return pe.astype(dtype)
        key = jax.random.key(seed)
        ks = jax.random.split(key, 8)
        B = 64
        img = jax.random.normal(ks[0], (B, C, IMG, IMG), dtype=jnp.float32)
        cls_token = jax.random.normal(ks[1], (1, 1, DIM), dtype=jnp.float32)
        cls_pos_embedding = jax.random.normal(ks[2], (1, 1, DIM), dtype=jnp.float32)
        ln1_g = jnp.ones((PATCH_DIM,), jnp.float32)
        ln1_b = jnp.zeros((PATCH_DIM,), jnp.float32)
        W = jax.random.normal(ks[3], (PATCH_DIM, DIM), dtype=jnp.float32) / np.sqrt(PATCH_DIM)
        bias = jnp.zeros((DIM,), jnp.float32)
        ln2_g = jnp.ones((DIM,), jnp.float32)
        ln2_b = jnp.zeros((DIM,), jnp.float32)
        return {'img': img, 'cls_token': cls_token, 'cls_pos_embedding': cls_pos_embedding, 'ln1_g': ln1_g, 'ln1_b': ln1_b, 'W': W, 'bias': bias, 'ln2_g': ln2_g, 'ln2_b': ln2_b}
    _L0_tok_all = _L0_tok_setup()
    _L0_tok_in = {k: v for k, v in _L0_tok_all.items() if k in ('cls_token', 'cls_pos_embedding', 'ln1_g', 'ln1_b', 'W', 'bias', 'ln2_g', 'ln2_b')}
    del _L0_tok_all

    def _L0_attn_setup():
        import math
        import jax, jax.numpy as jnp
        import numpy as np
        N_HEAD = 16

        def quant_weight(w):
            scale = jnp.maximum(jnp.mean(jnp.abs(w)), 1e-08)
            w_quant = jnp.clip(jnp.round(w / scale), -2.0, 2.0)
            return jax.lax.stop_gradient(w_quant * scale - w) + w
        key = jax.random.key(seed)
        k1, k2, k3 = jax.random.split(key, 3)
        C = 256
        x = jax.random.normal(k1, (2, 512, C), dtype=jnp.float32)
        w_attn = jax.random.normal(k2, (3 * C, C), dtype=jnp.float32) * (1.0 / math.sqrt(C))
        w_proj = jax.random.normal(k3, (C, C), dtype=jnp.float32) * (1.0 / math.sqrt(C))
        return {'x': x, 'w_attn': w_attn, 'w_proj': w_proj}
    _L0_attn_all = _L0_attn_setup()
    _L0_attn_in = {k: v for k, v in _L0_attn_all.items() if k in ('w_attn', 'w_proj')}
    del _L0_attn_all

    def _L0_ffn_setup():
        import jax, jax.numpy as jnp
        import numpy as np
        D_MODEL = 256
        key = jax.random.key(seed)
        k_x, k_w, k_a1, k_a2 = jax.random.split(key, 4)
        x = jax.random.normal(k_x, (4, 512, D_MODEL), dtype=jnp.float32)
        weight = jax.random.normal(k_w, (D_MODEL, D_MODEL), dtype=jnp.float32) * 0.02
        aux_weight1 = jax.random.normal(k_a1, (D_MODEL, D_MODEL), dtype=jnp.float32) * 0.02
        aux_weight2 = jax.random.normal(k_a2, (D_MODEL, D_MODEL), dtype=jnp.float32) * 0.02
        bias = jnp.zeros((D_MODEL,), dtype=jnp.float32)
        return {'x': x, 'weight': weight, 'aux_weight1': aux_weight1, 'aux_weight2': aux_weight2, 'bias': bias}
    _L0_ffn_all = _L0_ffn_setup()
    _L0_ffn_in = {k: v for k, v in _L0_ffn_all.items() if k in ('weight', 'aux_weight1', 'aux_weight2', 'bias')}
    del _L0_ffn_all

    def _L1_attn_setup():
        import jax, jax.numpy as jnp
        import numpy as np
        HIDDEN = 256
        HEADS = 16
        HEAD_DIM = HIDDEN // HEADS
        B, S = (4, 512)
        key = jax.random.key(seed)
        ks = jax.random.split(key, 10)
        scale = 1.0 / np.sqrt(HIDDEN)

        def lin(k):
            return jax.random.uniform(k, (HIDDEN, HIDDEN), jnp.float32, -scale, scale)
        return {'x': jax.random.normal(ks[0], (B, S, HIDDEN), jnp.float32), 'Wq': lin(ks[1]), 'bq': jnp.zeros((HIDDEN,), jnp.float32), 'Wk': lin(ks[2]), 'bk': jnp.zeros((HIDDEN,), jnp.float32), 'Wv': lin(ks[3]), 'bv': jnp.zeros((HIDDEN,), jnp.float32), 'Wo': lin(ks[4]), 'bo': jnp.zeros((HIDDEN,), jnp.float32), 'head_mask': jnp.ones((HEADS,), jnp.float32)}
    _L1_attn_all = _L1_attn_setup()
    _L1_attn_in = {k: v for k, v in _L1_attn_all.items() if k in ('Wq', 'bq', 'Wk', 'bk', 'Wv', 'bv', 'Wo', 'bo', 'head_mask')}
    del _L1_attn_all

    def _L1_ffn_setup():
        import jax, jax.numpy as jnp
        import numpy as np
        B, S, D, H, E = (8, 512, 256, 1024, 16)
        key = jax.random.key(seed)
        ks = jax.random.split(key, 4)
        sd = 1.0 / np.sqrt(D).astype(np.float32)
        sh = 1.0 / np.sqrt(H).astype(np.float32)
        return {'x': jax.random.normal(ks[0], (B, S, D), jnp.float32), 'Wg': jax.random.normal(ks[1], (D, E), jnp.float32) * sd, 'bg': jnp.zeros((E,), jnp.float32), 'W1': jax.random.normal(ks[2], (E, D, H), jnp.float32) * sd, 'b1': jnp.zeros((E, H), jnp.float32), 'W2': jax.random.normal(ks[3], (E, H, D), jnp.float32) * sh, 'b2': jnp.zeros((E, D), jnp.float32)}
    _L1_ffn_all = _L1_ffn_setup()
    _L1_ffn_in = {k: v for k, v in _L1_ffn_all.items() if k in ('Wg', 'bg', 'W1', 'b1', 'W2', 'b2')}
    del _L1_ffn_all
    return {'x': x, 'cls_tok': cls_tok, 'L0_tok_cls_token': _L0_tok_in['cls_token'], 'L0_tok_cls_pos_embedding': _L0_tok_in['cls_pos_embedding'], 'L0_tok_ln1_g': _L0_tok_in['ln1_g'], 'L0_tok_ln1_b': _L0_tok_in['ln1_b'], 'L0_tok_W': _L0_tok_in['W'], 'L0_tok_bias': _L0_tok_in['bias'], 'L0_tok_ln2_g': _L0_tok_in['ln2_g'], 'L0_tok_ln2_b': _L0_tok_in['ln2_b'], 'L0_attn_w_attn': _L0_attn_in['w_attn'], 'L0_attn_w_proj': _L0_attn_in['w_proj'], 'L0_ffn_weight': _L0_ffn_in['weight'], 'L0_ffn_aux_weight1': _L0_ffn_in['aux_weight1'], 'L0_ffn_aux_weight2': _L0_ffn_in['aux_weight2'], 'L0_ffn_bias': _L0_ffn_in['bias'], 'L1_attn_Wq': _L1_attn_in['Wq'], 'L1_attn_bq': _L1_attn_in['bq'], 'L1_attn_Wk': _L1_attn_in['Wk'], 'L1_attn_bk': _L1_attn_in['bk'], 'L1_attn_Wv': _L1_attn_in['Wv'], 'L1_attn_bv': _L1_attn_in['bv'], 'L1_attn_Wo': _L1_attn_in['Wo'], 'L1_attn_bo': _L1_attn_in['bo'], 'L1_attn_head_mask': _L1_attn_in['head_mask'], 'L1_ffn_Wg': _L1_ffn_in['Wg'], 'L1_ffn_bg': _L1_ffn_in['bg'], 'L1_ffn_W1': _L1_ffn_in['W1'], 'L1_ffn_b1': _L1_ffn_in['b1'], 'L1_ffn_W2': _L1_ffn_in['W2'], 'L1_ffn_b2': _L1_ffn_in['b2']}

def reference(x, cls_tok, L0_tok_cls_token, L0_tok_cls_pos_embedding, L0_tok_ln1_g, L0_tok_ln1_b, L0_tok_W, L0_tok_bias, L0_tok_ln2_g, L0_tok_ln2_b, L0_attn_w_attn, L0_attn_w_proj, L0_ffn_weight, L0_ffn_aux_weight1, L0_ffn_aux_weight2, L0_ffn_bias, L1_attn_Wq, L1_attn_bq, L1_attn_Wk, L1_attn_bk, L1_attn_Wv, L1_attn_bv, L1_attn_Wo, L1_attn_bo, L1_attn_head_mask, L1_ffn_Wg, L1_ffn_bg, L1_ffn_W1, L1_ffn_b1, L1_ffn_W2, L1_ffn_b2):
    import jax
    import jax.numpy as jnp

    def _L0_tok_ref(img, cls_token, cls_pos_embedding, ln1_g, ln1_b, W, bias, ln2_g, ln2_b):
        import jax, jax.numpy as jnp
        import numpy as np
        DIM = 256
        IMG = 96
        P = 16
        C = 3
        TEMP = 10000.0
        EPS = 1e-05
        PATCH_DIM = C * P * P
        HP = IMG // P

        def layernorm(x, gamma, beta):
            mu = jnp.mean(x, axis=-1, keepdims=True)
            var = jnp.var(x, axis=-1, keepdims=True)
            return (x - mu) * jax.lax.rsqrt(var + EPS) * gamma + beta

        def posemb_sincos_2d(h, w, dim, dtype):
            y, x = jnp.meshgrid(jnp.arange(h), jnp.arange(w), indexing='ij')
            omega = jnp.arange(dim // 4, dtype=jnp.float32) / (dim // 4 - 1)
            omega = 1.0 / TEMP ** omega
            y = y.reshape(-1)[:, None] * omega[None, :]
            x = x.reshape(-1)[:, None] * omega[None, :]
            pe = jnp.concatenate((jnp.sin(x), jnp.cos(x), jnp.sin(y), jnp.cos(y)), axis=1)
            return pe.astype(dtype)
        b = img.shape[0]
        x = img.reshape(b, C, HP, P, HP, P)
        x = jnp.transpose(x, (0, 2, 4, 3, 5, 1))
        x = x.reshape(b, HP, HP, PATCH_DIM)
        x = layernorm(x, ln1_g, ln1_b)
        x = jnp.einsum('bhwp,pd->bhwd', x, W) + bias
        x = layernorm(x, ln2_g, ln2_b)
        pe = posemb_sincos_2d(HP, HP, DIM, x.dtype)
        x = x.reshape(b, HP * HP, DIM) + pe[None]
        cls_tokens = jnp.broadcast_to(cls_token + cls_pos_embedding, (b, 1, DIM))
        return jnp.concatenate((cls_tokens, x), axis=1)

    def _L0_attn_ref(x, w_attn, w_proj):
        import math
        import jax, jax.numpy as jnp
        import numpy as np
        N_HEAD = 16

        def quant_weight(w):
            scale = jnp.maximum(jnp.mean(jnp.abs(w)), 1e-08)
            w_quant = jnp.clip(jnp.round(w / scale), -2.0, 2.0)
            return jax.lax.stop_gradient(w_quant * scale - w) + w
        B, T, C = x.shape
        H = N_HEAD
        D = C // H
        qkv = jnp.einsum('btc,oc->bto', x, quant_weight(w_attn))
        q, k, v = jnp.split(qkv, 3, axis=-1)
        q = q.reshape(B, T, H, D).transpose(0, 2, 1, 3)
        k = k.reshape(B, T, H, D).transpose(0, 2, 1, 3)
        v = v.reshape(B, T, H, D).transpose(0, 2, 1, 3)
        att = jnp.einsum('bhqd,bhkd->bhqk', q, k) * (1.0 / math.sqrt(D))
        causal = jnp.tril(jnp.ones((T, T), dtype=bool))
        att = jnp.where(causal, att, jnp.finfo(att.dtype).min)
        att = jax.nn.softmax(att, axis=-1)
        y = jnp.einsum('bhqk,bhkd->bhqd', att, v)
        y = y.transpose(0, 2, 1, 3).reshape(B, T, C)
        return jnp.einsum('btc,oc->bto', y, quant_weight(w_proj))

    def _L0_ffn_ref(x, weight, aux_weight1, aux_weight2, bias):
        import jax, jax.numpy as jnp
        import numpy as np
        D_MODEL = 256
        h = jnp.einsum('btc,cd->btd', x, weight)
        h = jnp.einsum('btc,cd->btd', h, aux_weight1)
        h = jnp.einsum('btc,cd->btd', h, aux_weight2)
        return jnp.tanh(h + bias)

    def _L1_attn_ref(x, Wq, bq, Wk, bk, Wv, bv, Wo, bo, head_mask):
        import jax, jax.numpy as jnp
        import numpy as np
        HIDDEN = 256
        HEADS = 16
        HEAD_DIM = HIDDEN // HEADS
        B, S = (4, 512)
        b, s, _ = x.shape
        q = (x @ Wq.T + bq).reshape(b, s, HEADS, HEAD_DIM)
        k = (x @ Wk.T + bk).reshape(b, s, HEADS, HEAD_DIM)
        v = (x @ Wv.T + bv).reshape(b, s, HEADS, HEAD_DIM)
        attn = jnp.einsum('bqhd,bkhd->bhqk', q, k) / np.sqrt(HEAD_DIM).astype(np.float32)
        attn = jax.nn.softmax(attn, axis=-1)
        attn = attn * head_mask[None, :, None, None]
        out = jnp.einsum('bhqk,bkhd->bqhd', attn, v).reshape(b, s, HIDDEN)
        return out @ Wo.T + bo

    def _L1_ffn_ref(x, Wg, bg, W1, b1, W2, b2):
        import jax, jax.numpy as jnp
        import numpy as np
        B, S, D, H, E = (8, 512, 256, 1024, 16)
        d = x.shape[-1]
        xf = x.reshape(-1, d)
        n_tok = xf.shape[0]
        n_exp = Wg.shape[1]
        cap = -(-n_tok // n_exp)
        score = jax.nn.softmax(xf @ Wg + bg, axis=-1)
        gate = jnp.max(score, axis=-1)
        idx = jnp.argmax(score, axis=-1)
        onehot = jax.nn.one_hot(idx, n_exp, dtype=jnp.int32)
        pos = jnp.sum((jnp.cumsum(onehot, axis=0) - 1) * onehot, axis=-1)
        keep = pos < cap
        safe_pos = jnp.where(keep, pos, cap - 1)
        buf = jnp.zeros((n_exp, cap, d), x.dtype).at[idx, safe_pos].add(jnp.where(keep[:, None], xf, 0.0))
        h = jax.nn.relu(jnp.einsum('ecd,edh->ech', buf, W1) + b1[:, None, :])
        y = jnp.einsum('ech,ehd->ecd', h, W2) + b2[:, None, :]
        out = y[idx, safe_pos] * gate[:, None]
        out = jnp.where(keep[:, None], out, 0.0)
        return out.reshape(x.shape)
    h = _L0_tok_ref(x, L0_tok_cls_token, L0_tok_cls_pos_embedding, L0_tok_ln1_g, L0_tok_ln1_b, L0_tok_W, L0_tok_bias, L0_tok_ln2_g, L0_tok_ln2_b)
    h = jnp.concatenate([jnp.broadcast_to(cls_tok, (h.shape[0], 1, h.shape[2])), h], axis=1)
    h = h + _L0_attn_ref(_layernorm(h, axis=-1), L0_attn_w_attn, L0_attn_w_proj)
    h = h + _L0_ffn_ref(_layernorm(h, axis=-1), L0_ffn_weight, L0_ffn_aux_weight1, L0_ffn_aux_weight2, L0_ffn_bias)
    h = h + _L1_attn_ref(_layernorm(h, axis=-1), L1_attn_Wq, L1_attn_bq, L1_attn_Wk, L1_attn_bk, L1_attn_Wv, L1_attn_bv, L1_attn_Wo, L1_attn_bo, L1_attn_head_mask)
    h = h + _L1_ffn_ref(_layernorm(h, axis=-1), L1_ffn_Wg, L1_ffn_bg, L1_ffn_W1, L1_ffn_b1, L1_ffn_W2, L1_ffn_b2)
    return h

_drawn_inputs = setup_inputs


def setup_inputs(seed=0):
    import zlib

    import numpy as np

    out = dict(_drawn_inputs(seed))
    spreads = {'L0_tok_ln1_g': (1.0, 0.2),
     'L0_tok_ln1_b': (0.0, 0.1),
     'L0_tok_bias': (0.0, 0.1),
     'L0_tok_ln2_g': (1.0, 0.2),
     'L0_tok_ln2_b': (0.0, 0.1),
     'L0_ffn_bias': (0.0, 0.1),
     'L1_attn_bq': (0.0, 0.751),
     'L1_attn_bk': (0.0, 0.8),
     'L1_attn_bv': (0.0, 0.1),
     'L1_attn_bo': (0.0, 0.1),
     'L1_ffn_bg': (0.0, 0.1),
     'L1_ffn_b1': (0.0, 0.725),
     'L1_ffn_b2': (0.0, 0.516)}
    factors = {'L1_attn_Wq': 2.815, 'L1_attn_Wk': 3.017}
    for name, (base, spread) in spreads.items():
        noise = np.random.default_rng([zlib.crc32(name.encode()), seed]).standard_normal(out[name].shape)
        drawn = base * np.exp(spread * noise) if base else spread * noise
        out[name] = jnp.asarray(drawn.astype(out[name].dtype))
    for name, factor in factors.items():
        out[name] = (out[name] * factor).astype(out[name].dtype)
    return out
```

```python
from contextlib import ExitStack

import numpy as np

import concourse.bass as bass
from concourse import mybir

F32 = mybir.dt.float32
BF16 = mybir.dt.bfloat16
U32 = mybir.dt.uint32
ALU = mybir.AluOpType
ACT = mybir.ActivationFunctionType
AX = mybir.AxisListType

NIMG, CH, IMG, PATCH, DIM = 32, 3, 96, 16, 256
HP = IMG // PATCH
SEQ = HP * HP + 2
NTOK = NIMG * SEQ
HEADS, HD = 16, 16
KC = DIM // 128
PC = CH * PATCH * PATCH // 128
TILE_IMGS = 3
TROWS = TILE_IMGS * SEQ
TILES = -(-NIMG // TILE_IMGS)
GROUP_IMGS = 6
GCOLS = GROUP_IMGS * SEQ
GROUPS = -(-NIMG // GROUP_IMGS)
PAIRS = NIMG // 2
PCOLS = 2 * SEQ
BROW = 64
PROWS = BROW + SEQ
HSTART = [0, 3, 6, 9, 12, 13]
VW = HD + 1
EXP, HID = 16, 1024
HC = HID // 128
CAP = -(-NTOK // EXP)
ECOLS = 96
XNB = 4
SLOTS = 4
EPS = 1e-5
MAGIC = 12582912.0
NEG = -1.0e30
DROP = 65536.0

WEIGHTS = ["L0_ffn_weight", "L0_ffn_aux_weight1", "L1_attn_Wq", "L1_attn_Wk", "L1_attn_Wv", "L1_attn_Wo"]
INS = ["x", "cls_tok", "L0_tok_cls_token", "L0_tok_cls_pos_embedding", "L0_tok_ln1_g", "L0_tok_ln1_b",
       "L0_tok_W", "L0_tok_bias", "L0_tok_ln2_g", "L0_tok_ln2_b", "L0_attn_w_attn", "L0_attn_w_proj",
       "L0_ffn_weight", "L0_ffn_aux_weight1", "L0_ffn_aux_weight2", "L0_ffn_bias", "L1_attn_Wq",
       "L1_attn_bq", "L1_attn_Wk", "L1_attn_bk", "L1_attn_Wv", "L1_attn_bv", "L1_attn_Wo", "L1_attn_bo",
       "L1_attn_head_mask", "L1_ffn_Wg", "L1_ffn_bg", "L1_ffn_W1", "L1_ffn_b1", "L1_ffn_W2", "L1_ffn_b2"]


def constants():
    p = np.arange(128)
    head = np.zeros((128, 8), np.float32)
    head[p, p // HD] = 1.0
    block = np.zeros((TROWS, HEADS), np.float32)
    for h in range(HEADS):
        at = 2 if h == HEADS - 1 else h % 3
        block[at * SEQ:(at + 1) * SEQ, h] = 1.0
    causal = np.zeros((128, 8, SEQ), np.float32)
    q = np.where(p < SEQ, p, np.where((p >= BROW) & (p < PROWS), p - BROW, SEQ))
    for r in range(128):
        causal[r, :, :] = np.where(np.arange(SEQ) > q[r], NEG, 0.0)
    upto = (p[:TROWS, None] <= p[None, :TROWS]).astype(np.float32)
    iota = np.broadcast_to(np.arange(EXP, dtype=np.float32), (TROWS, EXP)).copy()
    omega = np.arange(DIM // 4, dtype=np.float32) / np.float32(DIM // 4 - 1)
    omega = (np.float32(1.0) / np.power(np.float32(10000.0), omega)).astype(np.float32)
    y, x = np.meshgrid(np.arange(HP, dtype=np.float32), np.arange(HP, dtype=np.float32), indexing="ij")
    y, x = y.reshape(-1)[:, None] * omega, x.reshape(-1)[:, None] * omega
    one = np.concatenate([np.zeros((2, DIM), np.float32), np.concatenate([np.sin(x), np.cos(x), np.sin(y), np.cos(y)], 1)], 0)
    pos = np.tile(one, (TILE_IMGS, 1)).astype(np.float32)
    s = np.arange(TROWS) % SEQ
    kinds = np.stack([s >= 2, s == 0, s == 1], 1).astype(np.float32)
    return {"k_ident": np.eye(128, dtype=np.float32), "k_head": head, "k_block": block,
            "k_causal": causal.reshape(128, 8 * SEQ), "k_upto": upto, "k_iota": iota, "k_pos": pos, "k_kinds": kinds}


def rows(t):
    return min(TROWS, NTOK - t * TROWS)


def cols(t):
    return slice(t * TROWS, t * TROWS + rows(t))


def gcols(g):
    return slice(g * GCOLS, min((g + 1) * GCOLS, NTOK))


def bc(ap, axis, n):
    v = ap.unsqueeze(axis)
    shape = list(v.shape)
    shape[axis] = n
    return v.to_broadcast(shape)


def order():
    at = []
    last = lambda t: min((TILE_IMGS * t + TILE_IMGS - 1) // 2, PAIRS - 1)
    for t in range(TILES):
        b = 15 * t - 70
        at += [(b, "tok", 0, t), (b + 8, "tokn", 0, t), (b + 9, "lns", 0, t), (b + 14, "lnx", 0, t), (b + 20, "lnt", 0, t)]
    for g in range(GROUPS):
        at.append((15 * min(2 * g + 1, TILES - 1) - 70 + 20.5, "qk", 0, g))
    for l in range(2):
        z = 160 * l
        for p in range(PAIRS):
            at += [(z + 10 * p - 9, "km", l, p), (z + 10 * p - 9.5, "rep", l, p), (z + 10 * p - 6, "v", l, p), (z + 10 * p, "s", l, p), (z + 10 * p + 12, "pt", l, p),
                   (z + 10 * p + 21, "pv", l, p), (z + 10 * p + 33, "ot", l, p)]
        for t in range(TILES):
            b = z + 10 * last(t) + 33.5
            at.append((b, "proj", l, t))
            if l == 0:
                at += [(b + 0.1, "lns", 1, t), (b + 4, "lnx", 1, t), (b + 9, "lnt", 1, t), (b + 13, "ffn", 0, t), (b + 20, "ffnr", 0, t),
                       (b + 20.1, "lns", 2, t), (b + 24, "lnx", 2, t), (b + 29, "lnt", 2, t)]
            else:
                at += [(b + 0.1, "lns", 3, t), (b + 4, "lnx", 3, t), (b + 9, "lnt", 3, t), (b + 13, "log", 0, t)]
        if l == 0:
            for g in range(GROUPS):
                at.append((10 * last(min(2 * g + 1, TILES - 1)) + 33.5 + 29.2, "qk", 1, g))
    at.sort(key=lambda a: a[0])
    return [a[1:] for a in at]


def tower(nc, i, k, out):
    tasks = order()
    uses = {}
    n = 0
    for task in tasks:
        if task[0] in ("tok", "lnt", "ot", "proj", "ffn", "log"):
            uses[task] = n
            n += 1
        elif task[0] == "qk":
            uses[task] = n
            n += 2
    rs_rank = {}
    for task in tasks:
        if task[0] in ("tok", "lns"):
            rs_rank[task] = len(rs_rank) + 1
    lnt_tasks = [task for task in tasks if task[0] == "lnt"]
    assert [task[1:] for task in tasks if task[0] == "lnx"] == [task[1:] for task in lnt_tasks]
    xn_rank = {task[2]: m + 1 for m, task in enumerate(lnt_tasks) if task[1] == 2}
    use_count, n = n, n + 1
    use_xe = list(range(n, n + 6))
    xbuf = nc.dram_tensor("expert_in", [NTOK, DIM], F32, kind="Internal").ap()
    ybuf = nc.dram_tensor("expert_out", [NTOK, DIM], F32, kind="Internal").ap()

    with ExitStack() as ctx:
        def sb(name, shape, dt=F32):
            return ctx.enter_context(nc.sbuf_tensor(name, shape, dt))

        def sem(name):
            return ctx.enter_context(nc.semaphore(name))

        def carve(arena, sizes):
            at, found = 0, []
            for s in sizes:
                found.append(arena[:, at:at + s])
                at += s
            return found

        XW = CH * PATCH * IMG
        early = sb("early", [128, 2 * XW + PC * NTOK + PC * DIM + 3 * KC * DIM])
        x0, xn0, xT_, tws_, temp_ = carve(early, [XW, XW, PC * NTOK, PC * DIM, 3 * KC * DIM])
        a1T, wT, fB = [v.rearrange("p (k n) -> p k n", k=KC) for v in carve(temp_, [KC * DIM] * 3)]
        xT = xT_.rearrange("p (k n) -> p k n", k=PC)
        tokWg = tws_.rearrange("p (f c n) -> p f c n", f=2, c=CH)
        slot = [early[:, 4096 * s:4096 * (s + 1)] for s in range(SLOTS)]
        w1s = [s[:, 0:2048].rearrange("p (k n) -> p k n", k=KC) for s in slot]
        w2s = [s[:, 2048:4096].rearrange("p (c n) -> p c n", c=HC) for s in slot]

        mid = sb("mid", [128, 14400])
        qT_, kT_, OT_, km_, P_, PTs_, Vb_, On_ = carve(mid, [KC * NTOK] * 3 + [2 * 2 * 8 * PCOLS, 2 * HEADS * SEQ, 2 * 6 * PROWS, 3 * 2 * HEADS * VW, 2 * DIM])
        qT, kT, OT = [v.rearrange("p (k n) -> p k n", k=KC) for v in (qT_, kT_, OT_)]
        km = km_.rearrange("p (b f h n) -> p b f h n", b=2, f=2, h=8)
        P = P_.rearrange("p (b h n) -> p b h n", b=2, h=HEADS)
        PTs = PTs_.rearrange("p (b j n) -> p b j n", b=2, j=6)
        Vb = Vb_.rearrange("p (b a h d) -> p b a h d", b=3, a=2, h=HEADS)
        On = On_.rearrange("p (b n) -> p b n", b=2)
        nat_, _ = carve(mid, [11 * KC * DIM, 0])
        attn_nat = nat_[:, 0:3 * KC * DIM].rearrange("p (o n) -> p o n", o=6)
        proj_nat = nat_[:, 3 * KC * DIM:4 * KC * DIM].rearrange("p (o n) -> p o n", o=KC)
        nat = {w: nat_[:, (4 + j) * KC * DIM:(5 + j) * KC * DIM].rearrange("p (o n) -> p o n", o=KC) for j, w in enumerate(WEIGHTS)}
        a2 = nat_[:, 10 * KC * DIM:11 * KC * DIM].rearrange("p (o n) -> p o n", o=KC)
        tokW = mid[:, 11 * KC * DIM:11 * KC * DIM + PC * DIM].rearrange("p (f c n) -> p f c n", f=2, c=CH)
        x1 = mid[:, 3 * KC * NTOK:3 * KC * NTOK + XW]
        at = 3 * KC * NTOK + XW
        clsB = mid[0:TROWS, at:at + 3 * DIM].rearrange("p (j n) -> p j n", j=3)
        l2bB = mid[0:TROWS, at + 3 * DIM:at + 4 * DIM]
        causf = mid[:, at + 4 * DIM:at + 4 * DIM + 8 * SEQ]
        xe_, xeT_, hT_, ysb_, b2B_ = carve(mid, [EXP * DIM, EXP * KC * ECOLS, 2 * HC * CAP, 2 * DIM, 2 * DIM])
        xe = xe_.rearrange("p (e n) -> p e n", e=EXP)
        xeT = xeT_.rearrange("p (e k n) -> p e k n", e=EXP, k=KC)
        hT = hT_.rearrange("p (b c n) -> p b c n", b=2, c=HC)
        ysb = ysb_.rearrange("p (b n) -> p b n", b=2)
        b2B = b2B_.rearrange("p (b n) -> p b n", b=2)

        h = sb("h", [TROWS, TILES, DIM])
        xnd = sb("xnd", [TROWS, TILES, DIM])
        xnT = sb("xnT", [128, KC, NTOK])
        xnT3 = sb("xnT3", [128, 2, 2, KC, TROWS])
        xn = sb("xn", [TROWS, XNB, DIM])
        yv = sb("yv", [TROWS, 2, DIM])
        fv = sb("fv", [TROWS, 2, DIM])
        qkvT = sb("qkvT", [128, KC, 3 * DIM])
        projT = sb("projT", [128, KC, DIM])
        ffnW = sb("ffnW", [128, KC, DIM])
        wqkvT = sb("wqkvT", [128, KC, 3 * DIM])
        woT = sb("woT", [128, KC, DIM])
        gateW = sb("gateW", [128, KC, EXP])
        b1n = sb("b1n", [128, 128])
        b1T = sb("b1T", [128, EXP * HC])
        ident = sb("ident", [128, 128])
        ones = sb("ones", [128, 128])
        headm = sb("headm", [128, 8])
        blockm = sb("blockm", [TROWS, HEADS])
        causb = sb("causb", [128, 8 * SEQ], BF16)
        identb = sb("identb", [128, PROWS], BF16)
        upto = sb("upto", [TROWS, TROWS])
        iota = sb("iota", [TROWS, EXP])
        addA = sb("addA", [TROWS, DIM])
        kinds = sb("kinds", [TROWS, 3])
        g2B = sb("g2B", [TROWS, DIM])
        biasB = sb("biasB", [TROWS, DIM])
        fbB = sb("fbB", [TROWS, DIM])
        boB = sb("boB", [TROWS, DIM])
        bvB = sb("bvB", [PROWS, DIM])
        hmB = sb("hmB", [PROWS, HEADS])
        bgB = sb("bgB", [TROWS, EXP])
        bq = sb("bq", [128, KC])
        bk = sb("bk", [128, KC])
        g1 = sb("g1", [128, 2, CH])
        be1 = sb("be1", [128, 2, CH])
        mhalf = sb("mhalf", [128, 1])
        xst = sb("xst", [96, 2, HP, 2, 6])
        xmv = sb("xmv", [96, 2, HP, 2])
        xrs = sb("xrs", [96, 2, HP])
        asum = sb("asum", [128, 2])
        qs = sb("qs", [128, 8])
        st = sb("st", [TROWS, 2, 6])
        mv = sb("mv", [TROWS, 5 * TILES, 2])
        rs = sb("rs", [TROWS, 5 * TILES, 1])
        mx = sb("mx", [PROWS, 2, HEADS])
        rec = sb("rec", [PROWS, 2, HEADS])
        lg = sb("lg", [TROWS, 2, EXP])
        top = sb("top", [TROWS, 2, 8])
        ti = sb("ti", [TROWS, 2, 8], U32)
        nmx = sb("nmx", [TROWS, 2])
        ex = sb("ex", [TROWS, EXP])
        se = sb("se", [TROWS, TILES])
        idf = sb("idf", [TROWS, TILES])
        oh = sb("oh", [TROWS, TILES, EXP])
        ohc = sb("ohc", [TROWS, TILES, EXP])
        pos = sb("pos", [TROWS, TILES])
        keep = sb("keep", [TROWS, TILES])
        slotf = sb("slotf", [TROWS, TILES])
        sloti = sb("sloti", [TROWS, TILES], U32)
        gk = sb("gk", [TROWS, TILES])

        bank = [ctx.enter_context(nc.psum_tensor(f"bank{b}", [128, 1024], F32)) for b in range(4)]
        Sp = bank[0][:, :].rearrange("p (f n) -> p f n", f=2)
        PTp = bank[1][:, :].rearrange("p (f n) -> p f n", f=2)
        Vp = bank[2][:, 0:512]
        Op = bank[2][:, 512:1024]
        G = [bank[3][:, 0:512], bank[3][:, 512:1024]]
        ring = [bank[b][:, 512 * f:512 * f + 512] for b in range(3) for f in range(2)]
        Hp = [bank[0][:, :].rearrange("p (f n) -> p f n", f=2), bank[1][:, :].rearrange("p (f n) -> p f n", f=2)]
        Yp = [Vp, Op]

        l_ident, l_tab, l_x, l_nat, l_tok, l_bias, l_zero = (
            sem("l_ident"), sem("l_tab"), [[sem(f"l_x{u}{c}") for c in range(CH)] for u in range(2)],
            [sem(f"l_nat{j}") for j in range(4)], sem("l_tok"), sem("l_bias"), sem("l_zero"))
        zeroed, consts, causal_ready, xstats, xrstd, xnorm = (sem("zeroed"), sem("consts"), sem("causal_ready"), sem("xstats"), sem("xrstd"), sem("xnorm"))
        ring_full = [sem(f"ring_full{b}") for b in range(6)]
        ring_free = [sem(f"ring_free{b}") for b in range(6)]
        asum_ready, quant_ready, tokw_ready, bias_ready, tables_ready, start_done = (
            sem("asum_ready"), sem("quant_ready"), sem("tokw_ready"), sem("bias_ready"), sem("tables_ready"), sem("start_done"))
        g_full, g_free = [sem("g_full0"), sem("g_full1")], [sem("g_free0"), sem("g_free1")]
        mv_ready, rs_ready, xn_ready = sem("mv_ready"), sem("rs_ready"), sem("xn_ready")
        rep_ready, km_ready, v_full, vb_ready = sem("rep_ready"), sem("km_ready"), sem("v_full"), sem("vb_ready")
        s_full, p_ready, p_exp, pt_full, pt_ready = sem("s_full"), sem("p_ready"), sem("p_exp"), sem("pt_full"), sem("pt_ready")
        o_full, on_ready = sem("o_full"), sem("on_ready")
        bo_added, tanh_ready, neg_ready, oh_ready, se_ready = (
            sem("bo_added"), sem("tanh_ready"), sem("neg_ready"), sem("oh_ready"), sem("se_ready"))
        slots_ready, scattered, xe_loaded, pad_zero = sem("slots_ready"), sem("scattered"), sem("xe_loaded"), sem("pad_zero")
        w1_here, w2_here = [sem(f"w1_here{s}") for s in range(SLOTS)], [sem(f"w2_here{s}") for s in range(SLOTS)]
        w1_used = [sem(f"w1_used{s}") for s in range(SLOTS)]
        hid_full, hid_act, hid_dve = [[sem(f"{n}{b}") for b in range(2)] for n in ("hid_full", "hid_act", "hid_dve")]
        y_full, y_ready, y_stored, b2_here = [[sem(f"{n}{b}") for b in range(2)] for n in ("y_full", "y_ready", "y_stored", "b2_here")]
        gathered, final_ready, stored = [sem(f"gathered{t}") for t in range(TILES)], sem("final_ready"), sem("stored")
        dve_done, act_done, pool_done = sem("dve_done"), sem("act_done"), sem("pool_done")

        def chain(eng, s):
            count = [0]

            def link(ins):
                count[0] += 1
                ins.then_inc(s, 1)
                eng.wait_ge(s, count[0])
            return link

        def x_uses():
            return [("x", u, kc, w3) for u in range(2) for kc in range(PC) for w3 in range(2)]
        start = [("T", "qkv0"), ("T", "qkv1"), ("T", "qkv2"), ("T", "proj"), ("T", WEIGHTS[1]), ("T", WEIGHTS[0]),
                 ("T", WEIGHTS[2]), ("T", WEIGHTS[3]), ("T", WEIGHTS[4]), ("T", WEIGHTS[5]), ("b1",), ("sum",), ("fB",), ("bias",), ("fW",)] + x_uses()
        start_at = {u: n for n, u in enumerate(start)}
        on_act = {u: n % 2 == 0 for n, u in enumerate(start)}
        for u in (("sum",), ("bias",)):
            on_act[u] = False
        ring_total = [len([1 for n in range(len(start)) if n % 6 == b]) for b in range(6)]

        T_dst = {"qkv0": qkvT[:, :, 0:DIM], "qkv1": qkvT[:, :, DIM:2 * DIM], "qkv2": qkvT[:, :, 2 * DIM:], "proj": projT[:, :, :],
                 WEIGHTS[1]: a1T, WEIGHTS[0]: wT, WEIGHTS[2]: wqkvT[:, :, 0:DIM], WEIGHTS[3]: wqkvT[:, :, DIM:2 * DIM],
                 WEIGHTS[4]: wqkvT[:, :, 2 * DIM:], WEIGHTS[5]: woT[:, :, :]}
        T_src = {"qkv0": attn_nat[:, 0:2, :], "qkv1": attn_nat[:, 2:4, :], "qkv2": attn_nat[:, 4:6, :], "proj": proj_nat, **nat}
        T_load = {"qkv0": 0, "qkv1": 0, "qkv2": 0, "proj": 0, WEIGHTS[0]: 1, WEIGHTS[1]: 1, WEIGHTS[2]: 2, WEIGHTS[3]: 2, WEIGHTS[4]: 3, WEIGHTS[5]: 3}
        T_count = [4 * 16, 3 * 16, 2 * 16, 2 * 16]
        xs = [x0, x1]
        xv = [v[0:96, :].rearrange("p (r w q) -> p r w q", r=CH * PATCH, w=HP) for v in xs]
        xnv = [v[0:96, :].rearrange("p (w n) -> p w n", w=HP) for v in (xn0, x0)]

        def empty_ring(eng, op, link, u):
            n = start_at[u]
            b = n % 6
            eng.wait_ge(ring_full[b], n // 6 + 1)
            if u[0] == "T":
                d = T_dst[u[1]]
                scale = 0.25 if u[1] == WEIGHTS[2] else 1.0
                ins = op(d, ring[b].rearrange("p (k n) -> p k n", k=KC), scale)
            elif u[0] == "b1":
                ins = op(b1T[:, :], ring[b][:, 0:128], 1.0)
            elif u[0] in ("fB", "fW"):
                ins = op(fB if u[0] == "fB" else ffnW[:, :, :], ring[b].rearrange("p (k n) -> p k n", k=KC), 1.0)
            elif u[0] == "x":
                _, half, kc, w3 = u
                d = xT[:, kc, half * 16 * SEQ:(half + 1) * 16 * SEQ].rearrange("p (b s) -> p b s", s=SEQ)[:, :, 2:SEQ]
                d = d.rearrange("p b (y w) -> p b y w", w=HP)[:, :, :, 3 * w3:3 * w3 + 3]
                ins = op(d, ring[b][:, 0:288].rearrange("p (w b y) -> p b y w", w=3, y=HP), 1.0)
            ins.then_inc(ring_free[b], 1)

        def g_use(n):
            return n % 2, n // 2

        def emptied(eng, n):
            b, g = g_use(n)
            eng.wait_ge(g_free[b], g + 1)

        block = ctx.enter_context(nc.Block())

        @block.sync
        def _(sp):
            sp.dma_start(ident[:, :], k["k_ident"]).then_inc(l_ident, 16)

            def images(u):
                for c in range(CH):
                    sp.dma_start(xs[u][0:96, c * PATCH * IMG:(c + 1) * PATCH * IMG],
                                 i["x"][16 * u:16 * u + 16, c].rearrange("b (y r) w -> b y (r w)", y=HP)).then_inc(l_x[u][c], 16)
            images(0)
            sp.dma_start(attn_nat, i["L0_attn_w_attn"].rearrange("(o p) n -> p o n", p=128)).then_inc(l_nat[0], 16)
            sp.dma_start(proj_nat, i["L0_attn_w_proj"].rearrange("(o p) n -> p o n", p=128)).then_inc(l_nat[0], 16)
            sp.dma_start(b1n[:, :], i["L1_ffn_b1"].rearrange("e (c p) -> (e c) p", p=128)).then_inc(l_nat[0], 16)
            sp.dma_start(causf, k["k_causal"]).then_inc(l_nat[0], 16)
            images(1)
            for j, names in ((1, ["L0_ffn_weight", "L0_ffn_aux_weight1", "L0_ffn_aux_weight2"]), (2, WEIGHTS[2:4]), (3, WEIGHTS[4:6])):
                for w in names:
                    sp.dma_start(a2 if w == "L0_ffn_aux_weight2" else nat[w], i[w].rearrange("(o p) n -> p o n", p=128)).then_inc(l_nat[j], 16)
            sp.wait_ge(zeroed, 1)
            sp.dma_start(xbuf[0:10 * TROWS, :].rearrange("(t p) n -> p t n", p=TROWS), xnd[:, 0:10, :]).then_inc(l_zero, 16)
            sp.dma_start(xbuf[10 * TROWS:NTOK, :], xnd[0:rows(10), 10, :]).then_inc(l_zero, 16)
            emptied(sp, uses[("tok", 0, TILES - 1)])
            sp.wait_ge(start_done, 2)
            for s in range(SLOTS):
                sp.dma_start(w1s[s], i["L1_ffn_W1"][s].rearrange("(k p) n -> p k n", p=128)).then_inc(w1_here[s], 16)
                sp.dma_start(w2s[s], i["L1_ffn_W2"][s].rearrange("(c p) n -> p c n", p=128)).then_inc(w2_here[s], 16)
            with sp.Fori(1, EXP // SLOTS) as it:
                for s in range(SLOTS):
                    sp.wait_ge(w1_used[s], it)
                    sp.dma_start(w1s[s], i["L1_ffn_W1"][bass.ds(it * SLOTS + s, 1)].rearrange("e (k p) n -> p (e k) n", p=128)).then_inc(w1_here[s], 16)
                    sp.wait_ge(y_full[s % 2], it * (SLOTS // 2) + s // 2 - 1)
                    sp.dma_start(w2s[s], i["L1_ffn_W2"][bass.ds(it * SLOTS + s, 1)].rearrange("e (c p) n -> p (e c) n", p=128)).then_inc(w2_here[s], 16)
            out_rows = out.rearrange("b s n -> (b s) n")
            for t in range(TILES):
                sp.wait_ge(final_ready, t + 1)
                sp.dma_start(out_rows[cols(t), :], h[0:rows(t), t, :]).then_inc(stored, 16)
            sp.wait_ge(stored, 16 * TILES)

        @block.gpsimd
        def _(pool):
            link = chain(pool, pool_done)
            eng = nc.gpsimd
            eng.memset(mhalf[:, :], -0.5)
            eng.memset(ones[:, :], 1.0).then_inc(consts, 1)
            pool.dma_start(tokW.rearrange("p f c n -> p f (c n)"), i["L0_tok_W"].rearrange("(f p c) n -> p f (c n)", f=2, c=CH)).then_inc(l_tok, 16)
            with nc.allow_non_contiguous_dma(reason="small vectors laid over partitions"):
                for d, s in ((g1, "L0_tok_ln1_g"), (be1, "L0_tok_ln1_b")):
                    pool.dma_start(d[:, :, :], i[s].rearrange("(f p c) -> p f c", f=2, c=CH)).then_inc(l_tok, 16)
                for d, s in ((bq, "L1_attn_bq"), (bk, "L1_attn_bk")):
                    pool.dma_start(d[:, :], i[s].rearrange("(k p) -> p k", p=128)).then_inc(l_bias, 16)
            for d, s in ((biasB[:, :], i["L0_tok_bias"]), (g2B[:, :], i["L0_tok_ln2_g"]), (l2bB, i["L0_tok_ln2_b"]),
                         (clsB[:, 0, :], i["cls_tok"].rearrange("a b n -> (a b n)")),
                         (clsB[:, 1, :], i["L0_tok_cls_token"].rearrange("a b n -> (a b n)")),
                         (clsB[:, 2, :], i["L0_tok_cls_pos_embedding"].rearrange("a b n -> (a b n)")),
                         (fbB[:, :], i["L0_ffn_bias"]), (boB[:, :], i["L1_attn_bo"]), (bvB[:, :], i["L1_attn_bv"]),
                         (hmB[:, :], i["L1_attn_head_mask"]), (bgB[:, :], i["L1_ffn_bg"])):
                pool.dma_start(d, s.partition_broadcast(d.shape[0])).then_inc(l_bias, 16)
            for d, s in ((headm, "k_head"), (blockm, "k_block"), (upto, "k_upto"), (iota, "k_iota"), (addA, "k_pos"), (kinds, "k_kinds")):
                pool.dma_start(d[:, :], k[s]).then_inc(l_bias, 16)
            pool.dma_start(gateW[:, :, :], i["L1_ffn_Wg"].rearrange("(k p) n -> p k n", p=128)).then_inc(l_bias, 16)
            eng.memset(xnd[:, :, :], 0.0).then_inc(zeroed, 1)
            eng.memset(oh[:, :, :], 0.0)
            eng.memset(idf[:, :], 0.0)
            eng.memset(se[:, :], 1.0)
            link(eng.memset(xT.rearrange("p k (b s) -> p k b s", s=SEQ)[:, :, :, 0:2], 0.0))
            for u in range(2):
                pool.wait_ge(xstats, u + 1)
                link(eng.tensor_scalar(xrs[:, u, :], xmv[:, u, :, 1], EPS, None, ALU.add))
                link(eng.tensor_tensor(xrs[:, u, :], xrs[:, u, :], mhalf[0:96, :].to_broadcast([96, HP]), ALU.pow))
                for w in range(HP):
                    eng.tensor_scalar(xnv[u][:, w, :].rearrange("p (r q) -> p r q", q=PATCH), xv[u][:, :, w, :], xmv[:, u, w, 0:1], xrs[:, u, w:w + 1], ALU.subtract, ALU.mult).then_inc(xnorm, 1)
                if u == 0:
                    pool.wait_ge(l_tok, 48)
                    eng.tensor_tensor(tokWg, tokW, bc(g1[:, :, :], 3, DIM), ALU.mult).then_inc(tokw_ready, 1)
            pool.wait_ge(l_bias, 16 * 20)
            link(eng.tensor_tensor(clsB[:, 1, :], clsB[:, 1, :], clsB[:, 2, :], ALU.add))
            for v, c in ((l2bB, 0), (clsB[:, 0, :], 1), (clsB[:, 1, :], 2)):
                link(eng.tensor_scalar(v, v, kinds[:, c:c + 1], None, ALU.mult))
                link(eng.tensor_tensor(addA[:, :], addA[:, :], v, ALU.add))
            link(eng.tensor_tensor(bvB[:, :].rearrange("p (h d) -> p h d", h=HEADS), bvB[:, :].rearrange("p (h d) -> p h d", h=HEADS),
                                   bc(hmB[:, :], 2, HD), ALU.mult))
            eng.tensor_scalar(bq[:, :], bq[:, :], 0.25, None, ALU.mult).then_inc(tables_ready, 1)

            counts = {"mv": 0, "km": 0, "rep": 0}
            for kind, l, n in tasks:
                if kind in ("tok", "lns"):
                    r, j = rows(n), (n if kind == "tok" else (l + 1) * TILES + n)
                    counts["mv"] += 1
                    pool.wait_ge(mv_ready, counts["mv"])
                    link(eng.tensor_scalar(rs[0:r, j, :], mv[0:r, j, 1:2], EPS, None, ALU.add))
                    ins = eng.tensor_tensor(rs[0:r, j, :], rs[0:r, j, :], mhalf[0:r, :], ALU.pow)
                    if kind == "tok":
                        link(ins)
                        ins = eng.tensor_scalar(rs[0:r, j, :], rs[0:r, j, :], kinds[0:r, 0:1], None, ALU.mult)
                    ins.then_inc(rs_ready, 1)
                elif kind == "km":
                    emptied(pool, uses[("qk", l, 2 * n // GROUP_IMGS)] + 1)
                    counts["km"] += 1
                    if counts["km"] > 2:
                        pool.wait_ge(s_full, counts["km"] - 2)
                    for f in range(2):
                        ins = eng.tensor_tensor(km[:, n % 2, f], bc(kT[:, f, n * PCOLS:(n + 1) * PCOLS], 1, 8), bc(headm[:, :], 2, PCOLS), ALU.mult)
                    ins.then_inc(km_ready, 1)
                elif kind == "rep":
                    emptied(pool, uses[("qk", l, 2 * n // GROUP_IMGS)] + 1)
                    counts["rep"] += 1
                    if counts["rep"] > 2:
                        pool.wait_ge(v_full, counts["rep"] - 2)
                    for a in range(2):
                        at = (2 * n + a) * SEQ
                        ins = eng.tensor_copy(xnT3[:, n % 2, a].rearrange("p k (j n) -> p k j n", j=3), bc(xnT[:, :, at:at + SEQ], 2, 3))
                    ins.then_inc(rep_ready, 1)
                elif kind == "lnx" and l == 2:
                    pool.wait_ge(xn_ready, xn_rank[n])
                    eng.tensor_tensor(h[0:rows(n), n, :], h[0:rows(n), n, :], boB[0:rows(n), :], ALU.add).then_inc(bo_added, 1)

            pool.wait_ge(slots_ready, 1)
            pool.wait_ge(l_zero, 32)
            for t in range(TILES):
                eng.indirect_dma_start(out=xbuf, out_offset=bass.IndirectOffsetOnAxis(ap=sloti[0:rows(t), t:t + 1], axis=0),
                                       in_=xnd[0:rows(t), t, :], in_offset=None, bounds_check=NTOK - 1, oob_is_err=False).then_inc(scattered, 16)
            eng.memset(xeT[:, :, :, CAP:ECOLS], 0.0).then_inc(pad_zero, 1)
            pool.wait_ge(scattered, 16 * TILES)
            for q in range(4):
                pool.dma_start(xe[0:CAP, 4 * q:4 * q + 4, :], xbuf[4 * q * CAP:(4 * q + 4) * CAP, :].rearrange("(e p) n -> p e n", p=CAP)).then_inc(xe_loaded, 16)
            pool.wait_ge(xe_loaded, 64)
            for b in range(2):
                pool.dma_start(b2B[0:CAP, b, :], i["L1_ffn_b2"][b, :].partition_broadcast(CAP)).then_inc(b2_here[b], 16)
            with pool.Fori(0, EXP // 2 - 1) as it:
                for b in range(2):
                    pool.wait_ge(y_ready[b], it + 1)
                    pool.dma_start(ybuf[bass.ds((it * 2 + b) * CAP, CAP), :], ysb[0:CAP, b, :]).then_inc(y_stored[b], 16)
                    pool.dma_start(b2B[0:CAP, b, :], i["L1_ffn_b2"][bass.ds(it * 2 + b + 2, 1), :].rearrange("e n -> (e n)").partition_broadcast(CAP)
                                   ).then_inc(b2_here[b], 16)
            for b in range(2):
                pool.wait_ge(y_ready[b], EXP // 2)
                pool.dma_start(ybuf[(EXP - 2 + b) * CAP:(EXP - 1 + b) * CAP, :], ysb[0:CAP, b, :]).then_inc(y_stored[b], 16)
            for b in range(2):
                pool.wait_ge(y_stored[b], 16 * EXP // 2)
            for t in range(TILES):
                eng.indirect_dma_start(out=xnd[0:rows(t), t, :], out_offset=None, in_=ybuf,
                                       in_offset=bass.IndirectOffsetOnAxis(ap=sloti[0:rows(t), t:t + 1], axis=0),
                                       bounds_check=NTOK - 1, oob_is_err=False).then_inc(gathered[t], 16)

        @block.tensor
        def _(pe):
            mm, tr = nc.tensor.matmul, nc.tensor.transpose
            pe.wait_ge(l_ident, 16)
            for u in start:
                n = start_at[u]
                b = n % 6
                if n >= 6:
                    pe.wait_ge(ring_free[b], n // 6)
                if u[0] == "T":
                    pe.wait_ge(l_nat[T_load[u[1]]], T_count[T_load[u[1]]])
                    for kc in range(KC):
                        for oc in range(KC):
                            ins = tr(ring[b][:, kc * DIM + oc * 128:kc * DIM + oc * 128 + 128], T_src[u[1]][:, oc, kc * 128:kc * 128 + 128], ident[:, :])
                elif u[0] == "b1":
                    ins = tr(ring[b][:, 0:128], b1n[:, :], ident[:, :])
                elif u[0] == "sum":
                    pe.wait_ge(asum_ready, 1)
                    pe.wait_ge(consts, 1)
                    ins = mm(ring[b][:, 0:2], ones[:, :], asum[:, :], start=True, stop=True)
                elif u[0] == "fB":
                    pe.wait_ge(ring_free[start_at[("T", WEIGHTS[1])] % 6], start_at[("T", WEIGHTS[1])] // 6 + 1)
                    for ic in range(KC):
                        for kc in range(KC):
                            ins = mm(ring[b][:, ic * DIM:(ic + 1) * DIM], a1T[:, kc, ic * 128:ic * 128 + 128], a2[:, kc, :], start=kc == 0, stop=kc == KC - 1)
                elif u[0] == "fW":
                    for d in (("fB",), ("T", WEIGHTS[0])):
                        pe.wait_ge(ring_free[start_at[d] % 6], start_at[d] // 6 + 1)
                    for ic in range(KC):
                        for kc in range(KC):
                            ins = mm(ring[b][:, ic * DIM:(ic + 1) * DIM], wT[:, kc, ic * 128:ic * 128 + 128], fB[:, kc, :], start=kc == 0, stop=kc == KC - 1)
                elif u[0] == "bias":
                    pe.wait_ge(l_tok, 48)
                    for j in range(PC):
                        f, c = j % 2, j // 2
                        ins = mm(ring[b][0:TROWS, 0:DIM], be1[:, f, c:c + 1].to_broadcast([128, TROWS]), tokW[:, f, c, :], start=j == 0, stop=j == PC - 1)
                elif u[0] == "x":
                    _, half, kc, w3 = u
                    pe.wait_ge(xnorm, HP * half + 3 * w3 + 3)
                    for w in range(3):
                        ins = tr(ring[b][:, w * 96:(w + 1) * 96], xnv[half][:, 3 * w3 + w, kc * 128:kc * 128 + 128], ident[0:96, 0:96])
                ins.then_inc(ring_full[b], 1)

            def take(n):
                b, m = g_use(n)
                if m:
                    pe.wait_ge(g_free[b], m)
                return G[b], g_full[b]

            done = {"v": 0, "s": 0, "pt": 0, "pv": 0, "ot": 0, "lnt": 0}
            for kind, l, n in tasks:
                done[kind] = done.get(kind, 0) + 1
                m = done[kind]
                if kind == "tok":
                    if n == 0:
                        pe.wait_ge(tokw_ready, 1)
                        for b in range(6):
                            pe.wait_ge(ring_free[b], ring_total[b])
                    ps, full = take(uses[(kind, l, n)])
                    for j in range(PC):
                        mm_ = mm(ps[0:rows(n), 0:DIM], xT[:, j, cols(n)], tokWg[:, j % 2, j // 2, :], start=j == 0, stop=j == PC - 1)
                    mm_.then_inc(full, 1)
                elif kind == "lnt":
                    pe.wait_ge(xn_ready, m)
                    ps, full = take(uses[(kind, l, n)])
                    src = xnd[:, n, :] if l == 3 else xn[:, (m - 1) % XNB, :]
                    for kc in range(KC):
                        ins = tr(ps[:, kc * TROWS:kc * TROWS + rows(n)], src[0:rows(n), kc * 128:kc * 128 + 128], ident[0:rows(n), 0:rows(n)])
                    ins.then_inc(full, 1)
                elif kind == "qk":
                    for t in range(2 * n, min(2 * n + 2, TILES)):
                        emptied(pe, uses[("lnt", 2 * l, t)])
                    if m == 1:
                        pe.wait_ge(quant_ready, 1)
                    w = wqkvT if l else qkvT
                    width = gcols(n).stop - gcols(n).start
                    for j in range(2):
                        ps, full = take(uses[(kind, l, n)] + j)
                        for oc in range(KC):
                            for kc in range(KC):
                                ins = mm(ps[:, oc * width:(oc + 1) * width], w[:, kc, j * DIM + oc * 128:j * DIM + oc * 128 + 128], xnT[:, kc, gcols(n)],
                                         start=kc == 0, stop=kc == KC - 1)
                        ins.then_inc(full, 1)
                elif kind == "v":
                    pe.wait_ge(rep_ready, m)
                    if m > 1:
                        pe.wait_ge(vb_ready, m - 1)
                    w = wqkvT if l else qkvT
                    for a in range(2):
                        for kc in range(KC):
                            ins = mm(Vp[0:TROWS, a * DIM:(a + 1) * DIM], xnT3[:, n % 2, a, kc, :], w[:, kc, 2 * DIM:3 * DIM],
                                     start=kc == 0, stop=kc == KC - 1)
                    ins.then_inc(v_full, 1)
                elif kind == "s":
                    pe.wait_ge(km_ready, m)
                    if m > 1:
                        pe.wait_ge(p_ready, m - 1)
                    if m == 1:
                        pe.wait_ge(causal_ready, 1)
                    for f in range(2):
                        o = Sp[:, f, 0:8 * SEQ]
                        if l == 0:
                            mm(o[0:PROWS, :], identb[:, :], causb[:, :], start=True, stop=False, skip_group_check=True)
                        at = n * PCOLS
                        mm(o[0:BROW, :], qT[:, f, at:at + BROW], km[:, n % 2, f, :, 0:SEQ], start=l == 1, stop=True, skip_group_check=True)
                        ins = mm(o[BROW:PROWS, :], qT[:, f, at + SEQ:at + PCOLS], km[:, n % 2, f, :, SEQ:PCOLS], start=l == 1, stop=True, skip_group_check=True)
                    ins.then_inc(s_full, 1)
                elif kind == "pt":
                    pe.wait_ge(p_exp, m)
                    if m > 1:
                        pe.wait_ge(pt_ready, m - 1)
                    for j in range(6):
                        ins = tr(PTp[0:TROWS, j // 3, (j % 3) * PROWS:(j % 3 + 1) * PROWS], P[0:PROWS, n % 2, HSTART[j]:HSTART[j] + 3, :], ident[0:PROWS, 0:PROWS])
                    ins.then_inc(pt_full, 1)
                elif kind == "pv":
                    pe.wait_ge(pt_ready, m)
                    pe.wait_ge(vb_ready, m)
                    if m > 1:
                        pe.wait_ge(on_ready, m - 1)
                    for j in range(6):
                        h0 = 3 * j
                        h1 = min(h0 + 3, HEADS)
                        for a, (r0, r1) in enumerate(((0, BROW), (BROW, PROWS))):
                            ins = mm(Op[r0:r1, h0 * VW:h1 * VW], PTs[0:TROWS, n % 2, j, r0:r1], Vb[0:TROWS, (m - 1) % 3, a, h0:h1, :], start=True, stop=True)
                    ins.then_inc(o_full, 1)
                elif kind == "ot":
                    pe.wait_ge(on_ready, m)
                    ps, full = take(uses[(kind, l, n)])
                    for f in range(2):
                        ins = tr(ps[:, f * PROWS:(f + 1) * PROWS], On[0:PROWS, n % 2, f * 128:f * 128 + 128], ident[0:PROWS, 0:PROWS])
                    ins.then_inc(full, 1)
                elif kind == "proj":
                    for p in range(TILE_IMGS * n // 2, min((TILE_IMGS * n + 2) // 2, PAIRS - 1) + 1):
                        emptied(pe, uses[("ot", l, p)])
                    ps, full = take(uses[(kind, l, n)])
                    w = woT if l else projT
                    for kc in range(KC):
                        ins = mm(ps[0:rows(n), 0:DIM], OT[:, kc, cols(n)], w[:, kc, :], start=kc == 0, stop=kc == KC - 1)
                    ins.then_inc(full, 1)
                elif kind in ("ffn", "log"):
                    emptied(pe, uses[("lnt", 1 if kind == "ffn" else 3, n)])
                    ps, full = take(uses[(kind, l, n)])
                    w, width = (ffnW, DIM) if kind == "ffn" else (gateW, EXP)
                    for kc in range(KC):
                        ins = mm(ps[0:rows(n), 0:width], xnT[:, kc, cols(n)], w[:, kc, :], start=kc == 0, stop=kc == KC - 1)
                    ins.then_inc(full, 1)

            pe.wait_ge(oh_ready, TILES)
            ps, full = take(use_count)
            mm(ps[0:TROWS, 0:TILES * EXP], upto[:, :], oh[:, :, :], start=True, stop=False, skip_group_check=True)
            for t in range(TILES - 1):
                ins = mm(ps[0:TROWS, (t + 1) * EXP:TILES * EXP], ones[0:TROWS, 0:TROWS], bc(oh[:, t, :], 1, TILES - 1 - t), start=False, stop=t == TILES - 2,
                         skip_group_check=True)
            ins.then_inc(full, 1)
            for j in range(6):
                es = range(3 * j, min(3 * j + 3, EXP))
                if j == 0:
                    pe.wait_ge(xe_loaded, 64)
                ps, full = take(use_xe[j])
                for e in es:
                    for kc in range(KC):
                        at = ((e - 3 * j) * KC + kc) * CAP
                        ins = tr(ps[:, at:at + CAP], xe[0:CAP, e, kc * 128:kc * 128 + 128], ident[0:CAP, 0:CAP])
                ins.then_inc(full, 1)
            for j in (4, 5):
                emptied(pe, use_xe[j])
            pe.wait_ge(pad_zero, 1)
            def experts(it, first=False):
                for s in range(SLOTS):
                    b = s % 2
                    pe.wait_ge(w1_here[s], it * 16 + 16)
                    if not first or s >= 2:
                        pe.wait_ge(hid_act[b], it * 2 + s // 2)
                        pe.wait_ge(hid_dve[b], it * 2 + s // 2)
                    for c in range(HC):
                        for kc in range(KC):
                            ins = mm(Hp[b][:, c // 4, (c % 4) * ECOLS:(c % 4 + 1) * ECOLS], w1s[s][:, kc, c * 128:c * 128 + 128],
                                     xeT[:, bass.ds(it * SLOTS + s, 1), kc, :].rearrange("p e n -> p (e n)"), start=kc == 0, stop=kc == KC - 1)
                        if c == HC // 2 - 1:
                            ins.then_inc(hid_full[b], 1)
                    ins.then_inc(hid_full[b], 1)
                    pe.wait_ge(w2_here[s], it * 16 + 16)
                    if not first or s >= 2:
                        pe.wait_ge(y_ready[b], it * 2 + s // 2)
                    for c in range(HC):
                        if c == 0:
                            pe.wait_ge(hid_act[b], it * 2 + s // 2 + 1)
                        if c == HC // 2:
                            pe.wait_ge(hid_dve[b], it * 2 + s // 2 + 1)
                        ins = mm(Yp[b][0:CAP, 0:DIM], hT[:, b, c, :], w2s[s][:, c, :], start=c == 0, stop=c == HC - 1)
                        if c == 0:
                            ins.then_inc(w1_used[s], 1)
                    ins.then_inc(y_full[b], 1)

            experts(0, first=True)
            with pe.Fori(1, EXP // SLOTS) as it:
                experts(it)

        @block.scalar
        def _(act):
            link = chain(act, act_done)
            eng = nc.scalar

            def copy(d, s, scale):
                return eng.activation(d, s, ACT.Copy, scale=scale)

            for u in start:
                if on_act[u]:
                    empty_ring(act, copy, link, u)
            act.wait_ge(ring_free[0], 1)
            eng.copy(nmx[0:1, 1:2], ident[0:1, 0:1]).then_inc(start_done, 1)
            done = {}
            act.wait_ge(tables_ready, 1)
            for kind, l, n in tasks:
                done[kind] = done.get(kind, 0) + 1
                m = done[kind]
                if (kind, l, n) in uses:
                    b, g = g_use(uses[(kind, l, n)])
                if kind == "lnt":
                    act.wait_ge(g_full[b], g + 1)
                    eng.copy(xnT[:, :, cols(n)], G[b][:, 0:2 * TROWS].rearrange("p (k n) -> p k n", k=KC)[:, :, 0:rows(n)]).then_inc(g_free[b], 1)
                elif kind == "qk":
                    width = gcols(n).stop - gcols(n).start
                    for j, d in ((0, qT), (1, kT)):
                        b, g = g_use(uses[(kind, l, n)] + j)
                        act.wait_ge(g_full[b], g + 1)
                        if l == 0:
                            ins = eng.copy(d[:, :, gcols(n)], G[b][:, 0:2 * width].rearrange("p (k n) -> p k n", k=KC))
                        else:
                            for oc in range(KC):
                                ins = eng.activation(d[:, oc, gcols(n)], G[b][:, oc * width:(oc + 1) * width], ACT.Identity, bias=(bk if j else bq)[:, oc:oc + 1])
                        ins.then_inc(g_free[b], 1)
                elif kind == "s":
                    act.wait_ge(p_ready, m)
                    eng.activation(P[0:PROWS, n % 2], P[0:PROWS, n % 2], ACT.Exp).then_inc(p_exp, 1)
                elif kind == "pt":
                    act.wait_ge(pt_full, m)
                    if m > 2:
                        act.wait_ge(o_full, m - 2)
                    eng.copy(PTs[0:TROWS, n % 2].rearrange("p (f j) n -> p f (j n)", f=2), PTp[0:TROWS, :, 0:3 * PROWS]).then_inc(pt_ready, 1)
                elif kind == "ot":
                    act.wait_ge(g_full[b], g + 1)
                    s = G[b][:, 0:2 * PROWS].rearrange("p (f n) -> p f n", f=2)
                    for a, r0 in ((0, 0), (1, BROW)):
                        ins = eng.copy(OT[:, :, n * PCOLS + a * SEQ:n * PCOLS + (a + 1) * SEQ], s[:, :, r0:r0 + SEQ])
                    ins.then_inc(g_free[b], 1)
                elif kind == "ffn":
                    emptied(act, uses[(kind, l, n)])
                    eng.activation(fv[0:rows(n), n % 2, :], fv[0:rows(n), n % 2, :], ACT.Tanh).then_inc(tanh_ready, 1)
                elif kind == "log":
                    act.wait_ge(neg_ready, n + 1)
                    eng.activation(ex[0:rows(n), :], lg[0:rows(n), n % 2, :], ACT.Exp, bias=nmx[0:rows(n), n % 2:n % 2 + 1],
                                   accum_out=se[0:rows(n), n:n + 1]).then_inc(se_ready, 1)
            for j in range(0, 6, 2):
                b, g = g_use(use_xe[j])
                act.wait_ge(g_full[b], g + 1)
                ne = min(3, EXP - 3 * j)
                eng.copy(xeT[:, 3 * j:3 * j + ne, :, 0:CAP], G[b][:, 0:ne * KC * CAP].rearrange("p (e k n) -> p e k n", k=KC, n=CAP)).then_inc(g_free[b], 1)

            def hidden(it, first=False):
                for b in range(2):
                    act.wait_ge(hid_full[b], it * 2 + 1)
                    if not first:
                        act.wait_ge(y_full[b], it)
                    for c in range(HC // 2):
                        ins = eng.activation(hT[:, b, c, :], Hp[b][:, 0, c * ECOLS:c * ECOLS + CAP], ACT.Relu, bias=b1T[:, bass.ds((it * 2 + b) * HC + c, 1)])
                    ins.then_inc(hid_act[b], 1)

            hidden(0, first=True)
            with act.Fori(1, EXP // 2) as it:
                hidden(it)

        @block.vector
        def _(dve):
            link = chain(dve, dve_done)
            eng = nc.vector

            def copy(d, s, scale):
                return eng.tensor_copy(d, s) if scale == 1.0 else eng.tensor_scalar(d, s, scale, None, ALU.mult)

            def patch_stats(u):
                for w in range(HP):
                    for f in range(2):
                        dve.wait_ge(l_x[u][1], 16)
                        if w == 0:
                            dve.wait_ge(l_x[u][0], 16)
                            dve.wait_ge(l_x[u][2], 16)
                        ins = eng.bn_stats(xst[:, u, w, f, :], xv[u][:, 24 * f:24 * f + 24, w, :])
                link(ins)
                for w in range(HP):
                    ins = eng.bn_aggr(xmv[:, u, w, :], xst[:, u, w].rearrange("p f s -> p (f s)"))
                ins.then_inc(xstats, 1)

            patch_stats(0)
            dve.wait_ge(l_nat[0], 64)
            eng.tensor_copy(causb[:, :], causf)
            dve.wait_ge(l_ident, 16)
            eng.tensor_copy(identb[:, :], ident[:, 0:PROWS]).then_inc(causal_ready, 1)
            eng.tensor_reduce(asum[:, 0:1], attn_nat, AX.XY, ALU.add, apply_absolute_value=True)
            eng.tensor_reduce(asum[:, 1:2], proj_nat, AX.XY, ALU.add, apply_absolute_value=True).then_inc(asum_ready, 1)
            patch_stats(1)
            for u in start:
                if u[0] == "sum":
                    n = start_at[u]
                    b = n % 6
                    dve.wait_ge(ring_full[b], n // 6 + 1)
                    for c, size in ((0, 3 * DIM * DIM), (1, DIM * DIM)):
                        ins = eng.tensor_scalar(qs[:, c:c + 1], ring[b][:, c:c + 1], 1.0 / size, 1e-8, ALU.mult, ALU.max)
                    link(ins)
                    eng.tensor_scalar(qs[:, 4:5], qs[:, 0:1], 0.25, None, ALU.mult)
                    link(eng.reciprocal(qs[:, 2:4], qs[:, 0:2]))
                    eng.tensor_copy(qs[:, 6:8], ring[b][:, 0:2]).then_inc(ring_free[b], 1)
                elif u[0] == "bias":
                    n = start_at[u]
                    b = n % 6
                    dve.wait_ge(ring_full[b], n // 6 + 1)
                    dve.wait_ge(l_bias, 16 * 20)
                    eng.tensor_tensor(biasB[:, :], ring[b][0:TROWS, 0:DIM], biasB[:, :], ALU.add).then_inc(ring_free[b], 1)
                elif not on_act[u]:
                    empty_ring(dve, copy, link, u)
            for name in ("qkv0", "qkv1", "qkv2", "proj"):
                n = start_at[("T", name)]
                dve.wait_ge(ring_free[n % 6], n // 6 + 1)
            for w, inv in ((qkvT[:, :, :], 2), (projT[:, :, :], 3)):
                ins = eng.tensor_scalar(w, w, qs[:, inv:inv + 1], MAGIC, ALU.mult, ALU.add)
            link(ins)
            for w in (qkvT[:, :, :], projT[:, :, :]):
                ins = eng.tensor_scalar(w, w, MAGIC, -2.0, ALU.subtract, ALU.max)
            link(ins)
            for w, c in ((qkvT[:, :, 0:DIM], 4), (qkvT[:, :, DIM:], 0), (projT[:, :, :], 1)):
                ins = eng.tensor_scalar(w, w, 2.0, qs[:, c:c + 1], ALU.min, ALU.mult)
            ins.then_inc(quant_ready, 1)
            link(eng.memset(nmx[:, 0:1], 0.0))
            eng.tensor_copy(nmx[0:1, 0:1], nmx[0:1, 0:1]).then_inc(start_done, 1)
            dve.wait_ge(tables_ready, 1)

            normed = [0]

            def stats(src, r, j):
                q = normed[0] % 2
                normed[0] += 1
                if normed[0] > 2:
                    dve.wait_ge(mv_ready, normed[0] - 2)
                link(eng.bn_stats(st[0:r, q, :], src))
                eng.bn_aggr(mv[0:r, j, :], st[0:r, q, :]).then_inc(mv_ready, 1)

            done = {}
            for kind, l, n in tasks:
                done[kind] = done.get(kind, 0) + 1
                m = done[kind]
                r = rows(n)
                if (kind, l, n) in uses:
                    b, g = g_use(uses[(kind, l, n)])
                if kind == "tok":
                    dve.wait_ge(g_full[b], g + 1)
                    eng.tensor_tensor(yv[0:r, n % 2, :], G[b][0:r, 0:DIM], biasB[0:r, :], ALU.add).then_inc(g_free[b], 1)
                    dve.wait_ge(g_free[b], g + 1)
                    stats(yv[0:r, n % 2, :], r, n)
                elif kind == "tokn":
                    dve.wait_ge(rs_ready, rs_rank[("tok", 0, n)])
                    link(eng.scalar_tensor_tensor(out=h[0:r, n, :], in0=yv[0:r, n % 2, :], scalar=mv[0:r, n, 0:1], in1=g2B[0:r, :], op0=ALU.subtract, op1=ALU.mult))
                    link(eng.scalar_tensor_tensor(out=h[0:r, n, :], in0=h[0:r, n, :], scalar=rs[0:r, n, :], in1=addA[0:r, :], op0=ALU.mult, op1=ALU.add))
                elif kind == "lns":
                    stats(h[0:r, n, :], r, (l + 1) * TILES + n)
                elif kind == "lnx":
                    dve.wait_ge(rs_ready, rs_rank[("lns", l, n)])
                    if m > XNB:
                        emptied(dve, uses[lnt_tasks[m - 1 - XNB]])
                    if l == 3:
                        dve.wait_ge(l_zero, 32)
                    j = (l + 1) * TILES + n
                    d = xnd[0:r, n, :] if l == 3 else xn[0:r, (m - 1) % XNB, :]
                    eng.tensor_scalar(d, h[0:r, n, :], mv[0:r, j, 0:1], rs[0:r, j, :], ALU.subtract, ALU.mult).then_inc(xn_ready, 1)
                elif kind == "v":
                    dve.wait_ge(v_full, m)
                    if m > 3:
                        dve.wait_ge(o_full, m - 3)
                    else:
                        dve.wait_ge(tables_ready, 1)
                        eng.tensor_copy(Vb[0:TROWS, (m - 1) % 3, :, :, HD:VW], bc(bc(blockm[:, :], 1, 2), 3, 1))
                    eng.tensor_tensor(Vb[0:TROWS, (m - 1) % 3, :, :, 0:HD], Vp[0:TROWS, :].rearrange("p (a h d) -> p a h d", a=2, h=HEADS),
                                      bc(bc(blockm[:, :], 1, 2), 3, HD), ALU.mult).then_inc(vb_ready, 1)
                elif kind == "s":
                    dve.wait_ge(s_full, m)
                    sv = Sp[0:PROWS, :, 0:8 * SEQ].rearrange("p f (h n) -> p f h n", h=8)
                    mxv = mx[:, n % 2, :].rearrange("p (f h) -> p f h", f=2)
                    link(eng.tensor_reduce(mxv, sv, AX.X, ALU.max))
                    if m > 2:
                        dve.wait_ge(pt_full, m - 2)
                    eng.tensor_tensor(P[0:PROWS, n % 2].rearrange("p (f h) n -> p f h n", f=2), sv, bc(mxv, 3, SEQ), ALU.subtract).then_inc(p_ready, 1)
                elif kind == "pv":
                    dve.wait_ge(o_full, m)
                    if m > 2:
                        emptied(dve, uses[("ot",) + divmod(m - 3, PAIRS)])
                    ov = Op[0:PROWS, 0:HEADS * VW].rearrange("p (h d) -> p h d", h=HEADS)
                    link(eng.reciprocal(rec[:, n % 2, :], ov[:, :, HD]))
                    if l == 1:
                        link(eng.tensor_tensor(rec[:, n % 2, :], rec[:, n % 2, :], hmB[:, :], ALU.mult))
                    d = On[0:PROWS, n % 2, :]
                    ins = eng.tensor_tensor(d.rearrange("p (h d) -> p h d", h=HEADS), ov[:, :, 0:HD], bc(rec[:, n % 2, :], 2, HD), ALU.mult)
                    if l == 1:
                        link(ins)
                        ins = eng.tensor_tensor(d, d, bvB[:, :], ALU.add)
                    ins.then_inc(on_ready, 1)
                elif kind == "proj":
                    dve.wait_ge(g_full[b], g + 1)
                    if l == 1:
                        dve.wait_ge(bo_added, n + 1)
                    eng.tensor_tensor(h[0:r, n, :], h[0:r, n, :], G[b][0:r, 0:DIM], ALU.add).then_inc(g_free[b], 1)
                    dve.wait_ge(g_free[b], g + 1)
                elif kind == "ffn":
                    dve.wait_ge(g_full[b], g + 1)
                    eng.tensor_tensor(fv[0:r, n % 2, :], G[b][0:r, 0:DIM], fbB[0:r, :], ALU.add).then_inc(g_free[b], 1)
                elif kind == "ffnr":
                    dve.wait_ge(tanh_ready, n + 1)
                    link(eng.tensor_tensor(h[0:r, n, :], h[0:r, n, :], fv[0:r, n % 2, :], ALU.add))
                elif kind == "log":
                    q = n % 2
                    dve.wait_ge(g_full[b], g + 1)
                    if n >= 2:
                        dve.wait_ge(se_ready, n - 1)
                    eng.tensor_tensor(lg[0:r, q, :], G[b][0:r, 0:EXP], bgB[0:r, :], ALU.add).then_inc(g_free[b], 1)
                    dve.wait_ge(g_free[b], g + 1)
                    link(eng.max(top[0:r, q, :], lg[0:r, q, :]))
                    eng.tensor_scalar(nmx[0:r, q:q + 1], top[0:r, q, 0:1], -1.0, None, ALU.mult).then_inc(neg_ready, 1)
                    link(eng.max_index(ti[0:r, q, :], top[0:r, q, :], lg[0:r, q, :]))
                    link(eng.tensor_copy(idf[0:r, n:n + 1], ti[0:r, q, 0:1]))
                    eng.tensor_scalar(oh[0:r, n, :], iota[0:r, :], idf[0:r, n:n + 1], None, ALU.is_equal).then_inc(oh_ready, 1)

            b, g = g_use(use_count)
            dve.wait_ge(g_full[b], g + 1)
            eng.tensor_tensor(ohc[:, :, :], oh[:, :, :], G[b][0:TROWS, 0:TILES * EXP].rearrange("p (t e) -> p t e", e=EXP), ALU.mult).then_inc(g_free[b], 1)
            dve.wait_ge(g_free[b], g + 1)
            link(eng.tensor_reduce(pos[:, :], ohc[:, :, :], AX.X, ALU.add))
            eng.tensor_scalar(slotf[:, :], idf[:, :], float(CAP), -1.0, ALU.mult, ALU.add)
            link(eng.tensor_scalar(keep[:, :], pos[:, :], CAP + 0.5, None, ALU.is_lt))
            link(eng.tensor_tensor(slotf[:, :], slotf[:, :], pos[:, :], ALU.add))
            link(eng.tensor_scalar(pos[:, :], keep[:, :], -DROP, DROP, ALU.mult, ALU.add))
            link(eng.tensor_tensor(slotf[:, :], slotf[:, :], pos[:, :], ALU.add))
            eng.tensor_copy(sloti[:, :], slotf[:, :]).then_inc(slots_ready, 1)
            dve.wait_ge(se_ready, TILES)
            link(eng.reciprocal(gk[:, :], se[:, :]))
            link(eng.tensor_tensor(gk[:, :], gk[:, :], keep[:, :], ALU.mult))
            for j in range(1, 6, 2):
                b, g = g_use(use_xe[j])
                dve.wait_ge(g_full[b], g + 1)
                ne = min(3, EXP - 3 * j)
                eng.tensor_copy(xeT[:, 3 * j:3 * j + ne, :, 0:CAP], G[b][:, 0:ne * KC * CAP].rearrange("p (e k n) -> p e k n", k=KC, n=CAP)).then_inc(g_free[b], 1)

            def hidden(it, first=False):
                for b in range(2):
                    dve.wait_ge(hid_full[b], it * 2 + 2)
                    if not first:
                        dve.wait_ge(y_full[b], it)
                    for c in range(HC // 2, HC):
                        ins = eng.tensor_scalar(hT[:, b, c, :], Hp[b][:, 1, (c - 4) * ECOLS:(c - 4) * ECOLS + CAP], b1T[:, bass.ds((it * 2 + b) * HC + c, 1)], 0.0,
                                                ALU.add, ALU.max)
                    ins.then_inc(hid_dve[b], 1)
                    dve.wait_ge(y_full[b], it + 1)
                    dve.wait_ge(b2_here[b], it * 16 + 16)
                    if not first:
                        dve.wait_ge(y_stored[b], it * 16)
                    eng.tensor_tensor(ysb[0:CAP, b, :], Yp[b][0:CAP, 0:DIM], b2B[0:CAP, b, :], ALU.add).then_inc(y_ready[b], 1)

            hidden(0, first=True)
            with dve.Fori(1, EXP // 2) as it:
                hidden(it)
            for t in range(TILES):
                r = rows(t)
                dve.wait_ge(gathered[t], 16)
                eng.scalar_tensor_tensor(out=h[0:r, t, :], in0=xnd[0:r, t, :], scalar=gk[0:r, t:t + 1], in1=h[0:r, t, :], op0=ALU.mult, op1=ALU.add).then_inc(final_ready, 1)


def kernel(**inputs):
    import numpy as _np
    import concourse.bacc as _bacc
    from concourse.bass_utils import run_bass_kernel_spmd as _run

    nc = _bacc.Bacc("TRN2", target_bir_lowering=False, num_devices=1)
    arrays, args, tables = {}, {}, {}
    for name in INS:
        arrays[f"in_{name}"] = a = _np.ascontiguousarray(inputs[name])
        args[name] = nc.dram_tensor(f"in_{name}", a.shape, mybir.dt.from_np(a.dtype), kind="ExternalInput").ap()
    for name, a in constants().items():
        arrays[name] = a
        tables[name] = nc.dram_tensor(name, a.shape, mybir.dt.from_np(a.dtype), kind="ExternalInput").ap()
    out = nc.dram_tensor("out", (NIMG, SEQ, DIM), F32, kind="ExternalOutput").ap()
    tower(nc, args, tables, out)
    r = _run(nc, [arrays], core_ids=[0])
    return r.results[0]["out"]
```

```python
from contextlib import ExitStack

import numpy as np

import concourse.bass as bass
from concourse import mybir

F32 = mybir.dt.float32
BF16 = mybir.dt.bfloat16
U32 = mybir.dt.uint32
ALU = mybir.AluOpType
ACT = mybir.ActivationFunctionType
AX = mybir.AxisListType

NIMG, CH, IMG, PATCH, DIM = 32, 3, 96, 16, 256
HP = IMG // PATCH
SEQ = HP * HP + 2
NTOK = NIMG * SEQ
HEADS, HD = 16, 16
KC = DIM // 128
PC = CH * PATCH * PATCH // 128
TILE_IMGS = 3
TROWS = TILE_IMGS * SEQ
TILES = -(-NIMG // TILE_IMGS)
GROUP_IMGS = 6
GCOLS = GROUP_IMGS * SEQ
GROUPS = -(-NIMG // GROUP_IMGS)
PAIRS = NIMG // 2
PCOLS = 2 * SEQ
BROW = 64
PROWS = BROW + SEQ
HSTART = [0, 3, 6, 9, 12, 13]
VW = HD + 1
EXP, HID = 16, 1024
ROW = 2 * DIM + 2
HC = HID // 128
CAP = -(-NTOK // EXP)
ECOLS = 96
XNB = 3
SLOTS = 4
EPS = 1e-5
MAGIC = 12582912.0
NEG = -1.0e30
DROP = 65536.0

WEIGHTS = ["L0_ffn_weight", "L0_ffn_aux_weight1", "L1_attn_Wq", "L1_attn_Wk", "L1_attn_Wv", "L1_attn_Wo"]
INS = ["x", "cls_tok", "L0_tok_cls_token", "L0_tok_cls_pos_embedding", "L0_tok_ln1_g", "L0_tok_ln1_b",
       "L0_tok_W", "L0_tok_bias", "L0_tok_ln2_g", "L0_tok_ln2_b", "L0_attn_w_attn", "L0_attn_w_proj",
       "L0_ffn_weight", "L0_ffn_aux_weight1", "L0_ffn_aux_weight2", "L0_ffn_bias", "L1_attn_Wq",
       "L1_attn_bq", "L1_attn_Wk", "L1_attn_bk", "L1_attn_Wv", "L1_attn_bv", "L1_attn_Wo", "L1_attn_bo",
       "L1_attn_head_mask", "L1_ffn_Wg", "L1_ffn_bg", "L1_ffn_W1", "L1_ffn_b1", "L1_ffn_W2", "L1_ffn_b2"]


def constants():
    p = np.arange(128)
    head = np.zeros((128, 8), np.float32)
    head[p, p // HD] = 1.0
    block = np.zeros((TROWS, HEADS), np.float32)
    for h in range(HEADS):
        at = 2 if h == HEADS - 1 else h % 3
        block[at * SEQ:(at + 1) * SEQ, h] = 1.0
    causal = np.zeros((128, 8, SEQ), np.float32)
    q = np.where(p < SEQ, p, np.where((p >= BROW) & (p < PROWS), p - BROW, SEQ))
    for r in range(128):
        causal[r, :, :] = np.where(np.arange(SEQ) > q[r], NEG, 0.0)
    upto = (p[:TROWS, None] <= p[None, :TROWS]).astype(np.float32)
    ids = (np.arange(TILES)[None, :] * TROWS + p[:TROWS, None]).astype(np.float32)
    iota = np.broadcast_to(np.arange(EXP, dtype=np.float32), (TROWS, EXP)).copy()
    omega = np.arange(DIM // 4, dtype=np.float32) / np.float32(DIM // 4 - 1)
    omega = (np.float32(1.0) / np.power(np.float32(10000.0), omega)).astype(np.float32)
    y, x = np.meshgrid(np.arange(HP, dtype=np.float32), np.arange(HP, dtype=np.float32), indexing="ij")
    y, x = y.reshape(-1)[:, None] * omega, x.reshape(-1)[:, None] * omega
    one = np.concatenate([np.zeros((2, DIM), np.float32), np.concatenate([np.sin(x), np.cos(x), np.sin(y), np.cos(y)], 1)], 0)
    pos = np.tile(one, (TILE_IMGS, 1)).astype(np.float32)
    s = np.arange(TROWS) % SEQ
    kinds = np.stack([s >= 2, s == 0, s == 1], 1).astype(np.float32)
    return {"k_ident": np.eye(128, dtype=np.float32), "k_head": head, "k_block": block,
            "k_causal": causal.reshape(128, 8 * SEQ), "k_upto": upto, "k_iota": iota, "k_ids": ids, "k_pos": pos, "k_kinds": kinds}


def rows(t):
    return min(TROWS, NTOK - t * TROWS)


def cols(t):
    return slice(t * TROWS, t * TROWS + rows(t))


def gcols(g):
    return slice(g * GCOLS, min((g + 1) * GCOLS, NTOK))


def bc(ap, axis, n):
    v = ap.unsqueeze(axis)
    shape = list(v.shape)
    shape[axis] = n
    return v.to_broadcast(shape)


PAIR, TILE = 10.0, 15.0
AFTER = {"tok": -70, "tokn": 8.53, "lns0": 9.44, "lnx0": 14, "lnt0": 20, "qk0": 2.93, "qk1": 3.61, "km": -9, "s": 0, "pt": 13.48,
         "vb": 8.58, "pv": 19.78, "ot": 32.87, "v": -4.85, "proj": 33.5, "lns": 0.1, "lnx": 4, "lnt": 9.84, "ffn": 13, "ffnr": 20,
         "log": 13, "cnt": 22.76, "scat": 24, "layer": 160}
LATER = {"dve": {},
         "act": {"vb": 3.77, "s": 5.43, "tokn": -1.59, "ot": -0.23, "pv": -2.01},
         "pool": {"log": 0.33, "pv": 3.99, "cnt": 4.41},
         "pe": {},
         "sp": {"pv": 1.1}}


def order(engine):
    at, A = [], AFTER
    last = lambda t: min((TILE_IMGS * t + TILE_IMGS - 1) // 2, PAIRS - 1)
    for t in range(TILES):
        b = TILE * t + A["tok"]
        at += [(b, "tok", 0, t), (b + A["tokn"], "tokn", 0, t), (b + A["lns0"], "lns", 0, t), (b + A["lnx0"], "lnx", 0, t), (b + A["lnt0"], "lnt", 0, t)]
    for g in range(GROUPS):
        at.append((TILE * min(2 * g + 1, TILES - 1) + A["tok"] + A["lnt0"] + A["qk0"], "qk", 0, g))
    for l in range(2):
        z = A["layer"] * l
        for p in range(PAIRS):
            at += [(z + PAIR * p + A[kind], kind, l, p) for kind in ("km", "s", "vb", "pt", "pv", "ot")]
        for t in range(TILES):
            b = z + PAIR * last(t) + A["proj"]
            at += [(z + PAIR * (TILE_IMGS * t // 2) + A["v"], "v", l, t), (b, "proj", l, t)]
            for after, norm in ((0, 1), (A["ffnr"], 2)) if l == 0 else ((0, 3),):
                at += [(b + after + A["lns"], "lns", norm, t), (b + after + A["lnx"], "lnx", norm, t), (b + after + A["lnt"], "lnt", norm, t)]
            at += [(b + A[kind], kind, 0, t) for kind in (("ffn", "ffnr") if l == 0 else ("log", "cnt", "scat"))]
        if l == 0:
            for g in range(GROUPS):
                at.append((PAIR * last(min(2 * g + 1, TILES - 1)) + A["proj"] + A["ffnr"] + A["lnt"] + A["qk1"], "qk", 1, g))
    at.sort(key=lambda a: a[0] + LATER[engine].get(a[1], 0))
    return [a[1:] for a in at]


def tower(nc, i, k, out):
    tasks = order("pe")
    uses = {}
    n = 0
    for task in tasks:
        if task[0] in ("tok", "lnt", "ot", "proj", "ffn", "log", "cnt", "v"):
            uses[task] = n
            n += 1
        elif task[0] == "qk":
            uses[task] = n
            n += 2
    rs_rank = {}
    for task in order("dve"):
        if task[0] in ("tok", "lns"):
            rs_rank[task] = len(rs_rank) + 1
    lnt_tasks = [task for task in tasks if task[0] == "lnt"]
    stats_of = [[task for task in order(engine) if task[0] in ("tok", "lns")] for engine in ("dve", "pool")]
    assert stats_of[0] == stats_of[1]
    for engine in LATER:
        mine = order(engine)
        for kind in {task[0] for task in tasks}:
            like = "lnt" if kind in ("lnx", "lns") and engine == "pe" else kind
            assert [task[1:] for task in mine if task[0] == kind] == [task[1:] for task in tasks if task[0] == like]
    xn_rank = {task[2]: m + 1 for m, task in enumerate(lnt_tasks) if task[1] == 2}
    use_xe = list(range(n, n + 6))
    xbuf = nc.dram_tensor("expert_in", [NTOK, ROW], F32, kind="Internal").ap()

    with ExitStack() as ctx:
        def sb(name, shape, dt=F32):
            return ctx.enter_context(nc.sbuf_tensor(name, shape, dt))

        def sem(name):
            return ctx.enter_context(nc.semaphore(name))

        def carve(arena, sizes):
            at, found = 0, []
            for s in sizes:
                found.append(arena[:, at:at + s])
                at += s
            return found

        XW = CH * PATCH * IMG
        early = sb("early", [128, 2 * XW + PC * NTOK + PC * DIM + 3 * KC * DIM])
        x0, xn0, xT_, tws_, temp_ = carve(early, [XW, XW, PC * NTOK, PC * DIM, 3 * KC * DIM])
        a1T, wT, fB = [v.rearrange("p (k n) -> p k n", k=KC) for v in carve(temp_, [KC * DIM] * 3)]
        xT = xT_.rearrange("p (k n) -> p k n", k=PC)
        tokWg = tws_.rearrange("p (f c n) -> p f c n", f=2, c=CH)
        slot = [early[:, 4096 * s:4096 * (s + 1)] for s in range(SLOTS)]
        w1s = [s[:, 0:2048].rearrange("p (k n) -> p k n", k=KC) for s in slot]
        w2s = [s[:, 2048:4096].rearrange("p (c n) -> p c n", c=HC) for s in slot]

        mid = sb("mid", [128, 14312])
        qT_, kT_, OT_, km_, P_, PTs_, Vb_, On_ = carve(mid, [KC * NTOK] * 3 + [2 * 2 * 8 * PCOLS, 2 * HEADS * SEQ, 2 * 6 * PROWS, 3 * 2 * HEADS * VW, 2 * DIM])
        qT, kT, OT = [v.rearrange("p (k n) -> p k n", k=KC) for v in (qT_, kT_, OT_)]
        km = km_.rearrange("p (b f h n) -> p b f h n", b=2, f=2, h=8)
        P = P_.rearrange("p (b h n) -> p b h n", b=2, h=HEADS)
        PTs = PTs_.rearrange("p (b j n) -> p b j n", b=2, j=6)
        Vb = Vb_.rearrange("p (b a h d) -> p b a h d", b=3, a=2, h=HEADS)
        On = On_.rearrange("p (b n) -> p b n", b=2)
        nat_, _ = carve(mid, [11 * KC * DIM, 0])
        attn_nat = nat_[:, 0:3 * KC * DIM].rearrange("p (o n) -> p o n", o=6)
        proj_nat = nat_[:, 3 * KC * DIM:4 * KC * DIM].rearrange("p (o n) -> p o n", o=KC)
        nat = {w: nat_[:, (4 + j) * KC * DIM:(5 + j) * KC * DIM].rearrange("p (o n) -> p o n", o=KC) for j, w in enumerate(WEIGHTS)}
        a2 = nat_[:, 10 * KC * DIM:11 * KC * DIM].rearrange("p (o n) -> p o n", o=KC)
        tokW = mid[:, 11 * KC * DIM:11 * KC * DIM + PC * DIM].rearrange("p (f c n) -> p f c n", f=2, c=CH)
        x1 = mid[:, 3 * KC * NTOK:3 * KC * NTOK + XW]
        at = 3 * KC * NTOK + XW
        clsB = mid[0:TROWS, at:at + 3 * DIM].rearrange("p (j n) -> p j n", j=3)
        l2bB = mid[0:TROWS, at + 3 * DIM:at + 4 * DIM]
        causf = mid[:, at + 4 * DIM:at + 4 * DIM + 8 * SEQ]
        at += 4 * DIM + 8 * SEQ
        empty = mid[0:TROWS, at:at + ROW]
        at += ROW
        b1n = mid[:, at:at + 128]
        xst_, xmv_, xrs_, xnb_ = carve(mid[0:96, at + 128:], [2 * HP * 2 * 6, 2 * HP * 2, 2 * HP, 2 * HP])
        xst = xst_.rearrange("p (u w f s) -> p u w f s", u=2, w=HP, f=2)
        xmv = xmv_.rearrange("p (u w s) -> p u w s", u=2, w=HP)
        xrs, xnb = [v.rearrange("p (u w) -> p u w", u=2) for v in (xrs_, xnb_)]
        xe_, xeT_, hT_, ysb_, b2B_ = carve(mid, [EXP * ROW, EXP * KC * ECOLS, 2 * HC * CAP, 2 * DIM, 2 * DIM])
        xe = xe_.rearrange("p (e n) -> p e n", e=EXP)
        xeT = xeT_.rearrange("p (e k n) -> p e k n", e=EXP, k=KC)
        hT = hT_.rearrange("p (b c n) -> p b c n", b=2, c=HC)
        ysb = ysb_.rearrange("p (b n) -> p b n", b=2)
        b2B = b2B_.rearrange("p (b n) -> p b n", b=2)

        tokens = sb("tokens", [TROWS, TILES, ROW])
        h, xnd = tokens[:, :, 0:DIM], tokens[:, :, DIM:2 * DIM]
        ids = sb("ids", [TROWS, TILES])
        xnT = sb("xnT", [128, KC, NTOK])
        vt = sb("vt", [TROWS, 2, DIM])
        v3 = sb("v3", [TROWS, 2 * TILE_IMGS, DIM])
        xn = sb("xn", [TROWS, XNB, DIM])
        fv = sb("fv", [TROWS, 2, DIM])
        qkvT = sb("qkvT", [128, KC, 3 * DIM])
        projT = sb("projT", [128, KC, DIM])
        ffnW = sb("ffnW", [128, KC, DIM])
        wqkvT = sb("wqkvT", [128, KC, 3 * DIM])
        woT = sb("woT", [128, KC, DIM])
        gateW = sb("gateW", [128, KC, EXP])
        b1T = sb("b1T", [128, EXP * HC])
        ident = sb("ident", [128, 128])
        ones = sb("ones", [128, 128])
        headm = sb("headm", [128, 8])
        blockm = sb("blockm", [TROWS, HEADS])
        causb = sb("causb", [128, 8 * SEQ], BF16)
        identb = sb("identb", [128, PROWS], BF16)
        upto = sb("upto", [TROWS, TROWS])
        iota = sb("iota", [TROWS, EXP])
        addA = sb("addA", [TROWS, DIM])
        kinds = sb("kinds", [TROWS, 3])
        g2B = sb("g2B", [TROWS, DIM])
        biasB = sb("biasB", [TROWS, DIM])
        fbB = sb("fbB", [TROWS, DIM])
        boB = sb("boB", [TROWS, DIM])
        bvB = sb("bvB", [PROWS, DIM])
        hmB = sb("hmB", [PROWS, HEADS])
        bgB = sb("bgB", [TROWS, EXP])
        bq = sb("bq", [128, KC])
        bk = sb("bk", [128, KC])
        g1 = sb("g1", [128, 2, CH])
        be1 = sb("be1", [128, 2, CH])
        mhalf = sb("mhalf", [128, 1])
        asum = sb("asum", [128, 2])
        qs = sb("qs", [128, 8])
        st = sb("st", [TROWS, 2, 6])
        mv = sb("mv", [TROWS, 5 * TILES, 2])
        rs = sb("rs", [TROWS, 5 * TILES, 1])
        mx = sb("mx", [PROWS, 2, HEADS])
        rec = sb("rec", [PROWS, 2, HEADS])
        lg = sb("lg", [TROWS, 2, EXP])
        top = sb("top", [TROWS, 2, 8])
        ti = sb("ti", [TROWS, 2, 8], U32)
        nmx = sb("nmx", [TROWS, 2])
        ex = sb("ex", [TROWS, EXP])
        se = sb("se", [TROWS, TILES])
        idf = sb("idf", [TROWS, TILES])
        oh = sb("oh", [TROWS, TILES, EXP])
        ohs = sb("ohs", [TROWS, 2, EXP])
        ohc = sb("ohc", [TROWS, EXP])
        pos = sb("pos", [TROWS, 1])
        drop = sb("drop", [TROWS, 1])
        slotf = sb("slotf", [TROWS, 1])
        sloti = sb("sloti", [TROWS, TILES], U32)
        idx = sb("idx", [CAP, 2], U32)

        bank = [ctx.enter_context(nc.psum_tensor(f"bank{b}", [128, 1024], F32)) for b in range(4)]
        Sp = bank[0][:, :].rearrange("p (f n) -> p f n", f=2)
        PTp = bank[1][:, :].rearrange("p (f n) -> p f n", f=2)
        Op = bank[2][:, 512:1024]
        G = [bank[3][:, 0:512], bank[3][:, 512:1024], bank[2][:, 0:512]]
        ring = [bank[b][:, 512 * f:512 * f + 512] for b in range(3) for f in range(2)]
        Hp = [bank[0][:, :].rearrange("p (f n) -> p f n", f=2), bank[1][:, :].rearrange("p (f n) -> p f n", f=2)]
        Yp = [G[2], Op]

        l_ident, l_tab, l_x, l_nat, l_tok, l_bias, l_zero = (
            sem("l_ident"), sem("l_tab"), [[sem(f"l_x{u}{c}") for c in range(CH)] for u in range(2)],
            [sem(f"l_nat{j}") for j in range(4)], sem("l_tok"), sem("l_bias"), sem("l_zero"))
        zeroed, consts, causal_ready, xstats, xrstd, xnorm_dve, xnorm_act = (
            sem("zeroed"), sem("consts"), sem("causal_ready"), sem("xstats"), sem("xrstd"), sem("xnorm_dve"), sem("xnorm_act"))
        ring_full = [sem(f"ring_full{b}") for b in range(6)]
        ring_free = [sem(f"ring_free{b}") for b in range(6)]
        asum_ready, quant_ready, tokw_ready, bias_ready, tables_ready, start_done = (
            sem("asum_ready"), sem("quant_ready"), sem("tokw_ready"), sem("bias_ready"), sem("tables_ready"), sem("start_done"))
        g_full, g_free = [sem(f"g_full{b}") for b in range(3)], [sem(f"g_free{b}") for b in range(3)]
        mv_ready, rs_ready, xn_ready = sem("mv_ready"), sem("rs_ready"), sem("xn_ready")
        km_ready, vb_ready = sem("km_ready"), sem("vb_ready")
        v_spread = [sem("v_spread0"), sem("v_spread1")]
        s_full, p_ready, p_exp, pt_full, pt_ready = sem("s_full"), sem("p_ready"), sem("p_exp"), sem("pt_full"), sem("pt_ready")
        o_full, on_ready = sem("o_full"), sem("on_ready")
        bo_added, tanh_ready, neg_ready, oh_ready, se_ready = (
            sem("bo_added"), sem("tanh_ready"), sem("neg_ready"), sem("oh_ready"), sem("se_ready"))
        slots_ready, scattered, pad_zero, ohs_ready = sem("slots_ready"), sem("scattered"), sem("pad_zero"), sem("ohs_ready")
        xe_loaded = [sem(f"xe_loaded{q}") for q in range(4)]
        w1_here, w2_here = [sem(f"w1_here{s}") for s in range(SLOTS)], [sem(f"w2_here{s}") for s in range(SLOTS)]
        w1_used = [sem(f"w1_used{s}") for s in range(SLOTS)]
        hid_full, hid_act, hid_dve = [[sem(f"{n}{b}") for b in range(2)] for n in ("hid_full", "hid_act", "hid_dve")]
        y_full, y_taken, r_ready, r_stored, b2_here = [[sem(f"{n}{b}") for b in range(2)] for n in ("y_full", "y_taken", "r_ready", "r_stored", "b2_here")]
        stored = sem("stored")
        dve_done, act_done, pool_done = sem("dve_done"), sem("act_done"), sem("pool_done")

        def chain(eng, s):
            count = [0]

            def link(ins):
                count[0] += 1
                ins.then_inc(s, 1)
                eng.wait_ge(s, count[0])
            return link

        def x_uses(half):
            return [("x", half, kc, w3) for w3 in range(2) for kc in range(PC)]
        start = ([("T", "qkv0"), ("T", "qkv1"), ("T", "qkv2"), ("T", "proj"), ("sum",)] + x_uses(0)
                 + [("T", WEIGHTS[1]), ("T", WEIGHTS[0]), ("T", WEIGHTS[2]), ("bias",)] + x_uses(1)
                 + [("T", WEIGHTS[3]), ("T", WEIGHTS[4]), ("T", WEIGHTS[5]), ("b1",), ("fB",), ("fW",)])
        x_first = [("x", half, 0, 0) for half in range(2)]
        start_at = {u: n for n, u in enumerate(start)}
        on_dve = {("T", "qkv1"), ("T", "proj"), ("sum",), ("T", WEIGHTS[2]), ("bias",), ("T", WEIGHTS[3]), ("T", WEIGHTS[5]), ("fB",)}
        ring_total = [len([1 for n in range(len(start)) if n % 6 == b]) for b in range(6)]

        T_dst = {"qkv0": qkvT[:, :, 0:DIM], "qkv1": qkvT[:, :, DIM:2 * DIM], "qkv2": qkvT[:, :, 2 * DIM:], "proj": projT[:, :, :],
                 WEIGHTS[1]: a1T, WEIGHTS[0]: wT, WEIGHTS[2]: wqkvT[:, :, 0:DIM], WEIGHTS[3]: wqkvT[:, :, DIM:2 * DIM],
                 WEIGHTS[4]: wqkvT[:, :, 2 * DIM:], WEIGHTS[5]: woT[:, :, :]}
        T_src = {"qkv0": attn_nat[:, 0:2, :], "qkv1": attn_nat[:, 2:4, :], "qkv2": attn_nat[:, 4:6, :], "proj": proj_nat, **nat}
        T_load = {"qkv0": 0, "qkv1": 0, "qkv2": 0, "proj": 0, WEIGHTS[0]: 1, WEIGHTS[1]: 1, WEIGHTS[2]: 2, WEIGHTS[3]: 2, WEIGHTS[4]: 3, WEIGHTS[5]: 3}
        T_count = [4 * 16, 3 * 16, 2 * 16, 2 * 16]
        xs = [x0, x1]
        xv = [v[0:96, :].rearrange("p (r w q) -> p r w q", r=CH * PATCH, w=HP) for v in xs]
        xnv = [v[0:96, :].rearrange("p (w n) -> p w n", w=HP) for v in (xn0, x0)]

        def empty_ring(eng, op, link, u):
            n = start_at[u]
            b = n % 6
            eng.wait_ge(ring_full[b], n // 6 + 1)
            if u[0] == "T":
                d = T_dst[u[1]]
                scale = 0.25 if u[1] == WEIGHTS[2] else 1.0
                ins = op(d, ring[b].rearrange("p (k n) -> p k n", k=KC), scale)
            elif u[0] == "b1":
                ins = op(b1T[:, :], ring[b][:, 0:128], 1.0)
            elif u[0] in ("fB", "fW"):
                ins = op(fB if u[0] == "fB" else ffnW[:, :, :], ring[b].rearrange("p (k n) -> p k n", k=KC), 1.0)
            elif u[0] == "x":
                _, half, kc, w3 = u
                d = xT[:, kc, half * 16 * SEQ:(half + 1) * 16 * SEQ].rearrange("p (b s) -> p b s", s=SEQ)[:, :, 2:SEQ]
                d = d.rearrange("p b (y w) -> p b y w", w=HP)[:, :, :, 3 * w3:3 * w3 + 3]
                ins = op(d, ring[b][:, 0:288].rearrange("p (w b y) -> p b y w", w=3, y=HP), 1.0)
            ins.then_inc(ring_free[b], 1)

        def v_spread_count(u):
            return sum(16 * 3 * (rows(v % TILES) // SEQ) for v in range(u % 2, u + 1, 2))

        def g_use(n):
            return n % 3, n // 3

        def emptied(eng, n):
            b, g = g_use(n)
            eng.wait_ge(g_free[b], g + 1)

        out_rows = out.rearrange("b s n -> (b s) n")
        block = ctx.enter_context(nc.Block())

        @block.sync
        def _(sp):
            sp.dma_start(ident[:, :], k["k_ident"]).then_inc(l_ident, 16)

            def images(u):
                for c in range(CH):
                    sp.dma_start(xs[u][0:96, c * PATCH * IMG:(c + 1) * PATCH * IMG],
                                 i["x"][16 * u:16 * u + 16, c].rearrange("b (y r) w -> b y (r w)", y=HP)).then_inc(l_x[u][c], 16)
            images(0)
            sp.dma_start(attn_nat, i["L0_attn_w_attn"].rearrange("(o p) n -> p o n", p=128)).then_inc(l_nat[0], 16)
            sp.dma_start(proj_nat, i["L0_attn_w_proj"].rearrange("(o p) n -> p o n", p=128)).then_inc(l_nat[0], 16)
            sp.dma_start(b1n, i["L1_ffn_b1"].rearrange("e (c p) -> (e c) p", p=128)).then_inc(l_nat[0], 16)
            sp.dma_start(causf, k["k_causal"]).then_inc(l_nat[0], 16)
            images(1)
            for j, names in ((1, ["L0_ffn_weight", "L0_ffn_aux_weight1", "L0_ffn_aux_weight2"]), (2, WEIGHTS[2:4]), (3, WEIGHTS[4:6])):
                for w in names:
                    sp.dma_start(a2 if w == "L0_ffn_aux_weight2" else nat[w], i[w].rearrange("(o p) n -> p o n", p=128)).then_inc(l_nat[j], 16)
            sp.wait_ge(zeroed, 1)
            sp.dma_start(xbuf[0:10 * TROWS, :].rearrange("(t p) n -> p t n", p=TROWS), bc(empty[:, :], 1, 10)).then_inc(l_zero, 16)
            sp.dma_start(xbuf[10 * TROWS:NTOK, :], empty[0:rows(10), :]).then_inc(l_zero, 16)
            pieces = 0
            for kind, l, n in order("sp"):
                if kind == "tok" and n == TILES - 1:
                    emptied(sp, uses[(kind, l, n)])
                    sp.wait_ge(start_done, 2)
                elif kind == "v":
                    m = l * TILES + n + 1
                    emptied(sp, uses[(kind, l, n)])
                    pairs = l * PAIRS + ((TILE_IMGS * (n - 1) - 1) // 2 + 1 if n >= 2 else 0)
                    if pairs:
                        sp.wait_ge(vb_ready, pairs)
                    for a in range(rows(n) // SEQ):
                        for j in range(3):
                            sp.dma_start(v3[j * SEQ:(j + 1) * SEQ, (TILE_IMGS * n + a) % (2 * TILE_IMGS), :], vt[a * SEQ:(a + 1) * SEQ, (m - 1) % 2, :]).then_inc(v_spread[(m - 1) % 2], 16)
                    if l == 1 and pieces < 2 * SLOTS:
                        s = pieces // 2
                        if pieces % 2 == 0:
                            sp.dma_start(w1s[s], i["L1_ffn_W1"][s].rearrange("(k p) n -> p k n", p=128)).then_inc(w1_here[s], 16)
                        else:
                            sp.dma_start(w2s[s], i["L1_ffn_W2"][s].rearrange("(c p) n -> p c n", p=128)).then_inc(w2_here[s], 16)
                        pieces += 1
            for t in range(TILES):
                emptied(sp, uses[("proj", 1, t)])
                sp.dma_start(out_rows[cols(t), :], h[0:rows(t), t, :]).then_inc(stored, 16)
            sp.wait_ge(scattered, 16 * TILES)
            for q in range(4):
                sp.dma_start(xe[0:CAP, 4 * q:4 * q + 4, :], xbuf[4 * q * CAP:(4 * q + 4) * CAP, :].rearrange("(e p) n -> p e n", p=CAP)).then_inc(xe_loaded[q], 16)
            with sp.Fori(1, EXP // SLOTS) as it:
                for s in range(SLOTS):
                    sp.wait_ge(w1_used[s], it)
                    sp.dma_start(w1s[s], i["L1_ffn_W1"][bass.ds(it * SLOTS + s, 1)].rearrange("e (k p) n -> p (e k) n", p=128)).then_inc(w1_here[s], 16)
                    sp.wait_ge(y_full[s % 2], it * (SLOTS // 2) + s // 2 - 1)
                    sp.dma_start(w2s[s], i["L1_ffn_W2"][bass.ds(it * SLOTS + s, 1)].rearrange("e (c p) n -> p (e c) n", p=128)).then_inc(w2_here[s], 16)

        @block.gpsimd
        def _(pool):
            link = chain(pool, pool_done)
            eng = nc.gpsimd
            eng.memset(mhalf[:, :], -0.5)
            eng.memset(ones[:, :], 1.0).then_inc(consts, 1)
            pool.dma_start(tokW.rearrange("p f c n -> p f (c n)"), i["L0_tok_W"].rearrange("(f p c) n -> p f (c n)", f=2, c=CH)).then_inc(l_tok, 16)
            with nc.allow_non_contiguous_dma(reason="small vectors laid over partitions"):
                for d, v in ((g1, "L0_tok_ln1_g"), (be1, "L0_tok_ln1_b")):
                    pool.dma_start(d[:, :, :], i[v].rearrange("(f p c) -> p f c", f=2, c=CH)).then_inc(l_tok, 16)
            link(eng.memset(empty[:, :], 0.0))
            eng.memset(empty[:, 2 * DIM:2 * DIM + 1], DROP).then_inc(zeroed, 1)
            eng.memset(ohs[:, 0, :], 0.0)
            link(eng.memset(xT.rearrange("p k (b s) -> p k b s", s=SEQ)[:, :, :, 0:2], 0.0))
            pool.wait_ge(l_tok, 48)
            eng.tensor_tensor(tokWg, tokW, bc(g1[:, :, :], 3, DIM), ALU.mult).then_inc(tokw_ready, 1)

            def patch_scales(u):
                pool.wait_ge(xstats, u + 1)
                link(eng.tensor_scalar(xrs[:, u, :], xmv[:, u, :, 1], EPS, None, ALU.add))
                link(eng.tensor_tensor(xrs[:, u, :], xrs[:, u, :], mhalf[0:96, :].to_broadcast([96, HP]), ALU.pow))
                link(eng.tensor_tensor(xnb[:, u, :], xrs[:, u, :], xmv[:, u, :, 0], ALU.mult))
                eng.tensor_scalar(xnb[:, u, :], xnb[:, u, :], -1.0, None, ALU.mult).then_inc(xrstd, 1)
            patch_scales(0)
            patch_scales(1)
            pool.wait_ge(l_bias, 16 * 21)
            link(eng.tensor_tensor(clsB[:, 1, :], clsB[:, 1, :], clsB[:, 2, :], ALU.add))
            for v, c in ((l2bB, 0), (clsB[:, 0, :], 1), (clsB[:, 1, :], 2)):
                link(eng.tensor_scalar(v, v, kinds[:, c:c + 1], None, ALU.mult))
                link(eng.tensor_tensor(addA[:, :], addA[:, :], v, ALU.add))
            link(eng.tensor_tensor(bvB[:, :].rearrange("p (h d) -> p h d", h=HEADS), bvB[:, :].rearrange("p (h d) -> p h d", h=HEADS),
                                   bc(hmB[:, :], 2, HD), ALU.mult))
            eng.tensor_copy(tokens[:, :, 2 * DIM:2 * DIM + 1], ids[:, :].unsqueeze(2))
            eng.tensor_scalar(bq[:, :], bq[:, :], 0.25, None, ALU.mult).then_inc(tables_ready, 1)

            counts = {"mv": 0, "km": 0}
            for kind, l, n in order("pool"):
                if kind in ("tok", "lns"):
                    r, j = rows(n), (n if kind == "tok" else (l + 1) * TILES + n)
                    counts["mv"] += 1
                    pool.wait_ge(mv_ready, counts["mv"])
                    link(eng.tensor_scalar(rs[0:r, j, :], mv[0:r, j, 1:2], EPS, None, ALU.add))
                    ins = eng.tensor_tensor(rs[0:r, j, :], rs[0:r, j, :], mhalf[0:r, :], ALU.pow)
                    if kind == "tok":
                        link(ins)
                        ins = eng.tensor_scalar(rs[0:r, j, :], rs[0:r, j, :], kinds[0:r, 0:1], None, ALU.mult)
                    ins.then_inc(rs_ready, 1)
                elif kind == "km":
                    emptied(pool, uses[("qk", l, 2 * n // GROUP_IMGS)] + 1)
                    counts["km"] += 1
                    if counts["km"] > 2:
                        pool.wait_ge(s_full, counts["km"] - 2)
                    for f in range(2):
                        ins = eng.tensor_tensor(km[:, n % 2, f], bc(kT[:, f, n * PCOLS:(n + 1) * PCOLS], 1, 8), bc(headm[:, :], 2, PCOLS), ALU.mult)
                    ins.then_inc(km_ready, 1)
                elif kind == "vb":
                    m = l * PAIRS + n + 1
                    t = l * TILES + (2 * n + 1) // TILE_IMGS
                    for u in (t - 1, t):
                        if u >= 0:
                            pool.wait_ge(v_spread[u % 2], v_spread_count(u))
                    if m > 3:
                        pool.wait_ge(o_full, m - 3)
                    else:
                        eng.tensor_copy(Vb[0:TROWS, (m - 1) % 3, :, :, HD:VW], bc(bc(blockm[:, :], 1, 2), 3, 1))
                    at = 2 * n % (2 * TILE_IMGS)
                    eng.tensor_tensor(Vb[0:TROWS, (m - 1) % 3, :, :, 0:HD], v3[:, at:at + 2, :].rearrange("p a (h d) -> p a h d", h=HEADS),
                                      bc(bc(blockm[:, :], 1, 2), 3, HD), ALU.mult).then_inc(vb_ready, 1)
                elif kind == "lnx" and l == 2:
                    pool.wait_ge(xn_ready, xn_rank[n])
                    eng.tensor_tensor(h[0:rows(n), n, :], h[0:rows(n), n, :], boB[0:rows(n), :], ALU.add).then_inc(bo_added, 1)
                elif kind == "cnt":
                    if n < TILES - 1:
                        pool.wait_ge(oh_ready, n + 1)
                        if n >= 2:
                            emptied(pool, uses[("cnt", 0, n - 1)])
                        if n:
                            pool.wait_ge(ohs_ready, n)
                        eng.tensor_tensor(ohs[:, (n + 1) % 2, :], ohs[:, n % 2, :], oh[:, n, :], ALU.add).then_inc(ohs_ready, 1)
                elif kind == "scat":
                    pool.wait_ge(slots_ready, n + 1)
                    pool.wait_ge(l_zero, 32)
                    eng.indirect_dma_start(out=xbuf, out_offset=bass.IndirectOffsetOnAxis(ap=sloti[0:rows(n), n:n + 1], axis=0),
                                           in_=tokens[0:rows(n), n, :], in_offset=None, bounds_check=NTOK - 1, oob_is_err=False).then_inc(scattered, 16)

            pool.wait_ge(scattered, 16 * TILES)
            eng.memset(xeT[:, :, :, CAP:ECOLS], 0.0).then_inc(pad_zero, 1)
            for b in range(2):
                pool.dma_start(b2B[0:CAP, b, :], i["L1_ffn_b2"][b, :].partition_broadcast(CAP)).then_inc(b2_here[b], 16)
            pool.wait_ge(stored, 16 * TILES)

            def results(b):
                eng.indirect_dma_start(out=out_rows, out_offset=bass.IndirectOffsetOnAxis(ap=idx[:, b:b + 1], axis=0), in_=ysb[0:CAP, b, :],
                                       in_offset=None, bounds_check=NTOK - 1, oob_is_err=False).then_inc(r_stored[b], 16)
            with pool.Fori(0, EXP // 2 - 1) as it:
                for b in range(2):
                    pool.wait_ge(r_ready[b], it + 1)
                    pool.dma_start(b2B[0:CAP, b, :], i["L1_ffn_b2"][bass.ds(it * 2 + b + 2, 1), :].rearrange("e n -> (e n)").partition_broadcast(CAP)
                                   ).then_inc(b2_here[b], 16)
                    results(b)
            for b in range(2):
                pool.wait_ge(r_ready[b], EXP // 2)
                results(b)
            for b in range(2):
                pool.wait_ge(r_stored[b], 16 * EXP // 2)

        @block.tensor
        def _(pe):
            mm, tr = nc.tensor.matmul, nc.tensor.transpose
            pe.wait_ge(l_ident, 16)
            for u in start:
                n = start_at[u]
                b = n % 6
                if n >= 6:
                    pe.wait_ge(ring_free[b], n // 6)
                if u[0] == "T":
                    pe.wait_ge(l_nat[T_load[u[1]]], T_count[T_load[u[1]]])
                    for kc in range(KC):
                        for oc in range(KC):
                            ins = tr(ring[b][:, kc * DIM + oc * 128:kc * DIM + oc * 128 + 128], T_src[u[1]][:, oc, kc * 128:kc * 128 + 128], ident[:, :])
                elif u[0] == "b1":
                    ins = tr(ring[b][:, 0:128], b1n, ident[:, :])
                elif u[0] == "sum":
                    pe.wait_ge(asum_ready, 1)
                    pe.wait_ge(consts, 1)
                    ins = mm(ring[b][:, 0:2], ones[:, :], asum[:, :], start=True, stop=True)
                elif u[0] == "fB":
                    pe.wait_ge(ring_free[start_at[("T", WEIGHTS[1])] % 6], start_at[("T", WEIGHTS[1])] // 6 + 1)
                    for ic in range(KC):
                        for kc in range(KC):
                            ins = mm(ring[b][:, ic * DIM:(ic + 1) * DIM], a1T[:, kc, ic * 128:ic * 128 + 128], a2[:, kc, :], start=kc == 0, stop=kc == KC - 1)
                elif u[0] == "fW":
                    for d in (("fB",), ("T", WEIGHTS[0])):
                        pe.wait_ge(ring_free[start_at[d] % 6], start_at[d] // 6 + 1)
                    for ic in range(KC):
                        for kc in range(KC):
                            ins = mm(ring[b][:, ic * DIM:(ic + 1) * DIM], wT[:, kc, ic * 128:ic * 128 + 128], fB[:, kc, :], start=kc == 0, stop=kc == KC - 1)
                elif u[0] == "bias":
                    pe.wait_ge(l_tok, 48)
                    for j in range(PC):
                        f, c = j % 2, j // 2
                        ins = mm(ring[b][0:TROWS, 0:DIM], be1[:, f, c:c + 1].to_broadcast([128, TROWS]), tokW[:, f, c, :], start=j == 0, stop=j == PC - 1)
                elif u[0] == "x":
                    _, half, kc, w3 = u
                    if half == 0:
                        pe.wait_ge(xnorm_dve, 2 if w3 == 0 else 3)
                        pe.wait_ge(xnorm_act, 1 if w3 == 0 else 3)
                    else:
                        pe.wait_ge(xnorm_dve, HP // 2 + 3 * w3 + 3)
                    for w in range(3):
                        ins = tr(ring[b][:, w * 96:(w + 1) * 96], xnv[half][:, 3 * w3 + w, kc * 128:kc * 128 + 128], ident[0:96, 0:96])
                ins.then_inc(ring_full[b], 1)

            def take(n):
                b, m = g_use(n)
                if m:
                    pe.wait_ge(g_free[b], m)
                elif b == 2:
                    pe.wait_ge(ring_free[4], ring_total[4])
                return G[b], g_full[b]

            done = {"v": 0, "s": 0, "pt": 0, "pv": 0, "ot": 0, "lnt": 0}
            for kind, l, n in order("pe"):
                done[kind] = done.get(kind, 0) + 1
                m = done[kind]
                if kind == "tok":
                    if n == 0:
                        pe.wait_ge(tokw_ready, 1)
                        for b in range(6):
                            at = [start_at[u] for u in x_uses(1) if start_at[u] % 6 == b][-1]
                            pe.wait_ge(ring_free[b], at // 6 + 1)
                    ps, full = take(uses[(kind, l, n)])
                    for j in range(PC):
                        mm_ = mm(ps[0:rows(n), 0:DIM], xT[:, j, cols(n)], tokWg[:, j % 2, j // 2, :], start=j == 0, stop=j == PC - 1)
                    mm_.then_inc(full, 1)
                elif kind == "lnt":
                    pe.wait_ge(xn_ready, m)
                    ps, full = take(uses[(kind, l, n)])
                    src = xnd[:, n, :] if l == 3 else xn[:, (m - 1) % XNB, :]
                    for kc in range(KC):
                        ins = tr(ps[:, kc * TROWS:kc * TROWS + rows(n)], src[0:rows(n), kc * 128:kc * 128 + 128], ident[0:rows(n), 0:rows(n)])
                    ins.then_inc(full, 1)
                elif kind == "qk":
                    for t in range(2 * n, min(2 * n + 2, TILES)):
                        emptied(pe, uses[("lnt", 2 * l, t)])
                    if m == 1:
                        pe.wait_ge(quant_ready, 1)
                    w = wqkvT if l else qkvT
                    width = gcols(n).stop - gcols(n).start
                    for j in range(2):
                        ps, full = take(uses[(kind, l, n)] + j)
                        for oc in range(KC):
                            for kc in range(KC):
                                ins = mm(ps[:, oc * width:(oc + 1) * width], w[:, kc, j * DIM + oc * 128:j * DIM + oc * 128 + 128], xnT[:, kc, gcols(n)],
                                         start=kc == 0, stop=kc == KC - 1)
                        ins.then_inc(full, 1)
                elif kind == "v":
                    emptied(pe, uses[("lnt", 2 * l, n)])
                    if m == 1:
                        pe.wait_ge(quant_ready, 1)
                    ps, full = take(uses[(kind, l, n)])
                    w = wqkvT if l else qkvT
                    for kc in range(KC):
                        ins = mm(ps[0:rows(n), 0:DIM], xnT[:, kc, cols(n)], w[:, kc, 2 * DIM:3 * DIM], start=kc == 0, stop=kc == KC - 1)
                    ins.then_inc(full, 1)
                elif kind == "s":
                    if m == 1:
                        for b in (0, 1):
                            pe.wait_ge(ring_free[b], ring_total[b])
                    pe.wait_ge(km_ready, m)
                    if m > 1:
                        pe.wait_ge(p_ready, m - 1)
                    if m == 1:
                        pe.wait_ge(causal_ready, 1)
                    for f in range(2):
                        o = Sp[:, f, 0:8 * SEQ]
                        if l == 0:
                            mm(o[0:PROWS, :], identb[:, :], causb[:, :], start=True, stop=False, skip_group_check=True)
                        at = n * PCOLS
                        mm(o[0:BROW, :], qT[:, f, at:at + BROW], km[:, n % 2, f, :, 0:SEQ], start=l == 1, stop=True, skip_group_check=True)
                        ins = mm(o[BROW:PROWS, :], qT[:, f, at + SEQ:at + PCOLS], km[:, n % 2, f, :, SEQ:PCOLS], start=l == 1, stop=True, skip_group_check=True)
                    ins.then_inc(s_full, 1)
                elif kind == "pt":
                    if m == 1:
                        for b in (2, 3):
                            pe.wait_ge(ring_free[b], ring_total[b])
                    pe.wait_ge(p_exp, m)
                    if m > 1:
                        pe.wait_ge(pt_ready, m - 1)
                    for j in range(6):
                        ins = tr(PTp[0:TROWS, j // 3, (j % 3) * PROWS:(j % 3 + 1) * PROWS], P[0:PROWS, n % 2, HSTART[j]:HSTART[j] + 3, :], ident[0:PROWS, 0:PROWS])
                    ins.then_inc(pt_full, 1)
                elif kind == "pv":
                    if m == 1:
                        for b in (5,):
                            pe.wait_ge(ring_free[b], ring_total[b])
                    pe.wait_ge(pt_ready, m)
                    pe.wait_ge(vb_ready, m)
                    if m > 1:
                        pe.wait_ge(on_ready, m - 1)
                    for j in range(6):
                        h0 = 3 * j
                        h1 = min(h0 + 3, HEADS)
                        for a, (r0, r1) in enumerate(((0, BROW), (BROW, PROWS))):
                            ins = mm(Op[r0:r1, h0 * VW:h1 * VW], PTs[0:TROWS, n % 2, j, r0:r1], Vb[0:TROWS, (m - 1) % 3, a, h0:h1, :], start=True, stop=True)
                    ins.then_inc(o_full, 1)
                elif kind == "ot":
                    pe.wait_ge(on_ready, m)
                    ps, full = take(uses[(kind, l, n)])
                    for f in range(2):
                        ins = tr(ps[:, f * PROWS:(f + 1) * PROWS], On[0:PROWS, n % 2, f * 128:f * 128 + 128], ident[0:PROWS, 0:PROWS])
                    ins.then_inc(full, 1)
                elif kind == "proj":
                    for p in range(TILE_IMGS * n // 2, min((TILE_IMGS * n + 2) // 2, PAIRS - 1) + 1):
                        emptied(pe, uses[("ot", l, p)])
                    ps, full = take(uses[(kind, l, n)])
                    w = woT if l else projT
                    for kc in range(KC):
                        ins = mm(ps[0:rows(n), 0:DIM], OT[:, kc, cols(n)], w[:, kc, :], start=kc == 0, stop=kc == KC - 1)
                    ins.then_inc(full, 1)
                elif kind in ("ffn", "log"):
                    emptied(pe, uses[("lnt", 1 if kind == "ffn" else 3, n)])
                    ps, full = take(uses[(kind, l, n)])
                    w, width = (ffnW, DIM) if kind == "ffn" else (gateW, EXP)
                    for kc in range(KC):
                        ins = mm(ps[0:rows(n), 0:width], xnT[:, kc, cols(n)], w[:, kc, :], start=kc == 0, stop=kc == KC - 1)
                    ins.then_inc(full, 1)
                elif kind == "cnt":
                    r = rows(n)
                    pe.wait_ge(oh_ready, n + 1)
                    ps, full = take(uses[(kind, l, n)])
                    ins = mm(ps[0:r, 0:EXP], upto[0:r, 0:r], oh[0:r, n, :], start=True, stop=n == 0)
                    if n:
                        pe.wait_ge(ohs_ready, n)
                        ins = mm(ps[0:r, 0:EXP], ones[0:TROWS, 0:r], ohs[:, n % 2, :], start=False, stop=True)
                    ins.then_inc(full, 1)

            for j in range(6):
                es = range(3 * j, min(3 * j + 3, EXP))
                ps, full = take(use_xe[j])
                for e in es:
                    pe.wait_ge(xe_loaded[e // 4], 16)
                    for kc in range(KC):
                        at = ((e - 3 * j) * KC + kc) * CAP
                        ins = tr(ps[:, at:at + CAP], xe[0:CAP, e, DIM + kc * 128:DIM + kc * 128 + 128], ident[0:CAP, 0:CAP])
                ins.then_inc(full, 1)
            for j in (3, 4, 5):
                emptied(pe, use_xe[j])
            pe.wait_ge(pad_zero, 1)
            def experts(it, first=False):
                for s in range(SLOTS):
                    b = s % 2
                    pe.wait_ge(w1_here[s], it * 16 + 16)
                    if not first or s >= 2:
                        pe.wait_ge(hid_act[b], it * 2 + s // 2)
                        pe.wait_ge(hid_dve[b], it * 2 + s // 2)
                    for c in range(HC):
                        for kc in range(KC):
                            ins = mm(Hp[b][:, c // 4, (c % 4) * ECOLS:(c % 4 + 1) * ECOLS], w1s[s][:, kc, c * 128:c * 128 + 128],
                                     xeT[:, bass.ds(it * SLOTS + s, 1), kc, :].rearrange("p e n -> p (e n)"), start=kc == 0, stop=kc == KC - 1)
                        if c == HC // 2 - 1:
                            ins.then_inc(hid_full[b], 1)
                    ins.then_inc(hid_full[b], 1)
                    pe.wait_ge(w2_here[s], it * 16 + 16)
                    if not first or s >= 2:
                        pe.wait_ge(y_taken[b], it * 2 + s // 2)
                    for c in range(HC):
                        if c == 0:
                            pe.wait_ge(hid_act[b], it * 2 + s // 2 + 1)
                        if c == HC // 2:
                            pe.wait_ge(hid_dve[b], it * 2 + s // 2 + 1)
                        ins = mm(Yp[b][0:CAP, 0:DIM], hT[:, b, c, :], w2s[s][:, c, :], start=c == 0, stop=c == HC - 1)
                        if c == 0:
                            ins.then_inc(w1_used[s], 1)
                    ins.then_inc(y_full[b], 1)

            experts(0, first=True)
            with pe.Fori(1, EXP // SLOTS) as it:
                experts(it)

        @block.scalar
        def _(act):
            link = chain(act, act_done)
            eng = nc.scalar
            for d, v in ((biasB[:, :], i["L0_tok_bias"]), (g2B[:, :], i["L0_tok_ln2_g"]), (l2bB, i["L0_tok_ln2_b"]),
                         (clsB[:, 0, :], i["cls_tok"].rearrange("a b n -> (a b n)")),
                         (clsB[:, 1, :], i["L0_tok_cls_token"].rearrange("a b n -> (a b n)")),
                         (clsB[:, 2, :], i["L0_tok_cls_pos_embedding"].rearrange("a b n -> (a b n)")),
                         (hmB[:, :], i["L1_attn_head_mask"]), (fbB[:, :], i["L0_ffn_bias"]), (boB[:, :], i["L1_attn_bo"]), (bvB[:, :], i["L1_attn_bv"]),
                         (bgB[:, :], i["L1_ffn_bg"])):
                act.dma_start(d, v.partition_broadcast(d.shape[0])).then_inc(l_bias, 16)
            for d, v in ((kinds, "k_kinds"), (addA, "k_pos"), (headm, "k_head"), (blockm, "k_block"), (upto, "k_upto"), (iota, "k_iota"), (ids, "k_ids")):
                act.dma_start(d[:, :], k[v]).then_inc(l_bias, 16)
            with nc.allow_non_contiguous_dma(reason="small vectors laid over partitions"):
                for d, v in ((bq, "L1_attn_bq"), (bk, "L1_attn_bk")):
                    act.dma_start(d[:, :], i[v].rearrange("(k p) -> p k", p=128)).then_inc(l_bias, 16)
            act.dma_start(gateW[:, :, :], i["L1_ffn_Wg"].rearrange("(k p) n -> p k n", p=128)).then_inc(l_bias, 16)

            def copy(d, s, scale):
                return eng.activation(d, s, ACT.Copy, scale=scale)

            for u in start:
                if u == x_first[0]:
                    act.wait_ge(xrstd, 1)
                    for w in range(1, HP, 2):
                        eng.activation(xnv[0][:, w, :].rearrange("p (r q) -> p r q", q=PATCH), xv[0][:, :, w, :], ACT.Identity,
                                       bias=xnb[:, 0, w:w + 1], scale=xrs[:, 0, w:w + 1]).then_inc(xnorm_act, 1)
                if u not in on_dve:
                    empty_ring(act, copy, link, u)
            act.wait_ge(ring_free[0], 1)
            eng.copy(nmx[0:1, 1:2], ident[0:1, 0:1]).then_inc(start_done, 1)
            done = {}
            act.wait_ge(tables_ready, 1)
            for kind, l, n in order("act"):
                done[kind] = done.get(kind, 0) + 1
                m = done[kind]
                if (kind, l, n) in uses:
                    b, g = g_use(uses[(kind, l, n)])
                if kind == "lnt":
                    act.wait_ge(g_full[b], g + 1)
                    eng.copy(xnT[:, :, cols(n)], G[b][:, 0:2 * TROWS].rearrange("p (k n) -> p k n", k=KC)[:, :, 0:rows(n)]).then_inc(g_free[b], 1)
                elif kind == "qk":
                    width = gcols(n).stop - gcols(n).start
                    for j, d in ((0, qT), (1, kT)):
                        b, g = g_use(uses[(kind, l, n)] + j)
                        act.wait_ge(g_full[b], g + 1)
                        if l == 0:
                            ins = eng.copy(d[:, :, gcols(n)], G[b][:, 0:2 * width].rearrange("p (k n) -> p k n", k=KC))
                        else:
                            for oc in range(KC):
                                ins = eng.activation(d[:, oc, gcols(n)], G[b][:, oc * width:(oc + 1) * width], ACT.Identity, bias=(bk if j else bq)[:, oc:oc + 1])
                        ins.then_inc(g_free[b], 1)
                elif kind == "v":
                    act.wait_ge(g_full[b], g + 1)
                    if m > 2:
                        act.wait_ge(v_spread[(m - 1) % 2], v_spread_count(m - 3))
                    eng.copy(vt[0:rows(n), (m - 1) % 2, :], G[b][0:rows(n), 0:DIM]).then_inc(g_free[b], 1)
                elif kind == "s":
                    act.wait_ge(p_ready, m)
                    eng.activation(P[0:PROWS, n % 2], P[0:PROWS, n % 2], ACT.Exp).then_inc(p_exp, 1)
                elif kind == "pt":
                    act.wait_ge(pt_full, m)
                    if m > 2:
                        act.wait_ge(o_full, m - 2)
                    eng.copy(PTs[0:TROWS, n % 2].rearrange("p (f j) n -> p f (j n)", f=2), PTp[0:TROWS, :, 0:3 * PROWS]).then_inc(pt_ready, 1)
                elif kind == "ot":
                    act.wait_ge(g_full[b], g + 1)
                    s = G[b][:, 0:2 * PROWS].rearrange("p (f n) -> p f n", f=2)
                    for a, r0 in ((0, 0), (1, BROW)):
                        ins = eng.copy(OT[:, :, n * PCOLS + a * SEQ:n * PCOLS + (a + 1) * SEQ], s[:, :, r0:r0 + SEQ])
                    ins.then_inc(g_free[b], 1)
                elif kind == "ffn":
                    emptied(act, uses[(kind, l, n)])
                    eng.activation(fv[0:rows(n), n % 2, :], fv[0:rows(n), n % 2, :], ACT.Tanh).then_inc(tanh_ready, 1)
                elif kind == "log":
                    act.wait_ge(neg_ready, n + 1)
                    eng.activation(ex[0:rows(n), :], lg[0:rows(n), n % 2, :], ACT.Exp, bias=nmx[0:rows(n), n % 2:n % 2 + 1],
                                   accum_out=se[0:rows(n), n:n + 1]).then_inc(se_ready, 1)
            for j in range(0, 6, 2):
                b, g = g_use(use_xe[j])
                act.wait_ge(g_full[b], g + 1)
                ne = min(3, EXP - 3 * j)
                eng.copy(xeT[:, 3 * j:3 * j + ne, :, 0:CAP], G[b][:, 0:ne * KC * CAP].rearrange("p (e k n) -> p e k n", k=KC, n=CAP)).then_inc(g_free[b], 1)

            def hidden(it, first=False):
                for b in range(2):
                    act.wait_ge(hid_full[b], it * 2 + 1)
                    if not first:
                        act.wait_ge(y_full[b], it)
                    for c in range(HC // 2):
                        ins = eng.activation(hT[:, b, c, :], Hp[b][:, 0, c * ECOLS:c * ECOLS + CAP], ACT.Relu, bias=b1T[:, bass.ds((it * 2 + b) * HC + c, 1)])
                    ins.then_inc(hid_act[b], 1)

            hidden(0, first=True)
            with act.Fori(1, EXP // 2) as it:
                hidden(it)

        @block.vector
        def _(dve):
            link = chain(dve, dve_done)
            eng = nc.vector

            def copy(d, s, scale):
                return eng.tensor_copy(d, s) if scale == 1.0 else eng.tensor_scalar(d, s, scale, None, ALU.mult)

            def patch_stats(u):
                for w in range(HP):
                    for f in range(2):
                        dve.wait_ge(l_x[u][1], 16)
                        if w == 0:
                            dve.wait_ge(l_x[u][0], 16)
                            dve.wait_ge(l_x[u][2], 16)
                        ins = eng.bn_stats(xst[:, u, w, f, :], xv[u][:, 24 * f:24 * f + 24, w, :])
                link(ins)
                for w in range(HP):
                    ins = eng.bn_aggr(xmv[:, u, w, :], xst[:, u, w].rearrange("p f s -> p (f s)"))
                ins.then_inc(xstats, 1)

            def quantise():
                for name in ("qkv0", "qkv1", "qkv2", "proj"):
                    n = start_at[("T", name)]
                    dve.wait_ge(ring_free[n % 6], n // 6 + 1)
                for w, inv in ((qkvT[:, :, :], 2), (projT[:, :, :], 3)):
                    ins = eng.tensor_scalar(w, w, qs[:, inv:inv + 1], MAGIC, ALU.mult, ALU.add)
                link(ins)
                for w in (qkvT[:, :, :], projT[:, :, :]):
                    ins = eng.tensor_scalar(w, w, MAGIC, -2.0, ALU.subtract, ALU.max)
                link(ins)
                for w, c in ((qkvT[:, :, 0:DIM], 4), (qkvT[:, :, DIM:], 0), (projT[:, :, :], 1)):
                    ins = eng.tensor_scalar(w, w, 2.0, qs[:, c:c + 1], ALU.min, ALU.mult)
                ins.then_inc(quant_ready, 1)

            patch_stats(0)
            dve.wait_ge(l_nat[0], 64)
            eng.tensor_copy(causb[:, :], causf)
            dve.wait_ge(l_ident, 16)
            eng.tensor_copy(identb[:, :], ident[:, 0:PROWS]).then_inc(causal_ready, 1)
            eng.tensor_reduce(asum[:, 0:1], attn_nat, AX.XY, ALU.add, apply_absolute_value=True)
            eng.tensor_reduce(asum[:, 1:2], proj_nat, AX.XY, ALU.add, apply_absolute_value=True).then_inc(asum_ready, 1)
            for u in start:
                if u in x_first:
                    half = u[1]
                    dve.wait_ge(xrstd, half + 1)
                    if half:
                        dve.wait_ge(xnorm_dve, HP // 2)
                        dve.wait_ge(xnorm_act, HP // 2)
                    for w in range(0, HP, 1 if half else 2):
                        eng.tensor_scalar(xnv[half][:, w, :].rearrange("p (r q) -> p r q", q=PATCH), xv[half][:, :, w, :], xmv[:, half, w, 0:1],
                                          xrs[:, half, w:w + 1], ALU.subtract, ALU.mult).then_inc(xnorm_dve, 1)
                    if half == 0:
                        patch_stats(1)
                    else:
                        quantise()
                if u[0] == "sum":
                    n = start_at[u]
                    b = n % 6
                    dve.wait_ge(ring_full[b], n // 6 + 1)
                    for c, size in ((0, 3 * DIM * DIM), (1, DIM * DIM)):
                        ins = eng.tensor_scalar(qs[:, c:c + 1], ring[b][:, c:c + 1], 1.0 / size, 1e-8, ALU.mult, ALU.max)
                    link(ins)
                    eng.tensor_scalar(qs[:, 4:5], qs[:, 0:1], 0.25, None, ALU.mult)
                    link(eng.reciprocal(qs[:, 2:4], qs[:, 0:2]))
                    eng.tensor_copy(qs[:, 6:8], ring[b][:, 0:2]).then_inc(ring_free[b], 1)
                elif u[0] == "bias":
                    n = start_at[u]
                    b = n % 6
                    dve.wait_ge(ring_full[b], n // 6 + 1)
                    dve.wait_ge(l_bias, 16 * 21)
                    eng.tensor_tensor(biasB[:, :], ring[b][0:TROWS, 0:DIM], biasB[:, :], ALU.add).then_inc(ring_free[b], 1)
                elif u in on_dve:
                    empty_ring(dve, copy, link, u)
            link(eng.memset(nmx[:, 0:1], 0.0))
            eng.tensor_copy(nmx[0:1, 0:1], nmx[0:1, 0:1]).then_inc(start_done, 1)
            dve.wait_ge(tables_ready, 1)
            dve.wait_ge(l_zero, 32)

            normed = [0]

            def stats(src, r, j):
                q = normed[0] % 2
                normed[0] += 1
                if normed[0] > 2:
                    dve.wait_ge(mv_ready, normed[0] - 2)
                link(eng.bn_stats(st[0:r, q, :], src))
                eng.bn_aggr(mv[0:r, j, :], st[0:r, q, :]).then_inc(mv_ready, 1)

            done = {}
            for kind, l, n in order("dve"):
                done[kind] = done.get(kind, 0) + 1
                m = done[kind]
                r = rows(n)
                if (kind, l, n) in uses:
                    b, g = g_use(uses[(kind, l, n)])
                if kind == "tok":
                    dve.wait_ge(g_full[b], g + 1)
                    eng.tensor_tensor(h[0:r, n, :], G[b][0:r, 0:DIM], biasB[0:r, :], ALU.add).then_inc(g_free[b], 1)
                    dve.wait_ge(g_free[b], g + 1)
                    stats(h[0:r, n, :], r, n)
                elif kind == "tokn":
                    dve.wait_ge(rs_ready, rs_rank[("tok", 0, n)])
                    link(eng.scalar_tensor_tensor(out=h[0:r, n, :], in0=h[0:r, n, :], scalar=mv[0:r, n, 0:1], in1=g2B[0:r, :], op0=ALU.subtract, op1=ALU.mult))
                    link(eng.scalar_tensor_tensor(out=h[0:r, n, :], in0=h[0:r, n, :], scalar=rs[0:r, n, :], in1=addA[0:r, :], op0=ALU.mult, op1=ALU.add))
                elif kind == "lns":
                    stats(h[0:r, n, :], r, (l + 1) * TILES + n)
                elif kind == "lnx":
                    dve.wait_ge(rs_ready, rs_rank[("lns", l, n)])
                    if m > XNB:
                        emptied(dve, uses[lnt_tasks[m - 1 - XNB]])
                    j = (l + 1) * TILES + n
                    d = xnd[0:r, n, :] if l == 3 else xn[0:r, (m - 1) % XNB, :]
                    eng.tensor_scalar(d, h[0:r, n, :], mv[0:r, j, 0:1], rs[0:r, j, :], ALU.subtract, ALU.mult).then_inc(xn_ready, 1)
                elif kind == "s":
                    dve.wait_ge(s_full, m)
                    sv = Sp[0:PROWS, :, 0:8 * SEQ].rearrange("p f (h n) -> p f h n", h=8)
                    mxv = mx[:, n % 2, :].rearrange("p (f h) -> p f h", f=2)
                    link(eng.tensor_reduce(mxv, sv, AX.X, ALU.max))
                    if m > 2:
                        dve.wait_ge(pt_full, m - 2)
                    eng.tensor_tensor(P[0:PROWS, n % 2].rearrange("p (f h) n -> p f h n", f=2), sv, bc(mxv, 3, SEQ), ALU.subtract).then_inc(p_ready, 1)
                elif kind == "pv":
                    dve.wait_ge(o_full, m)
                    if m > 2:
                        emptied(dve, uses[("ot",) + divmod(m - 3, PAIRS)])
                    ov = Op[0:PROWS, 0:HEADS * VW].rearrange("p (h d) -> p h d", h=HEADS)
                    link(eng.reciprocal(rec[:, n % 2, :], ov[:, :, HD]))
                    if l == 1:
                        link(eng.tensor_tensor(rec[:, n % 2, :], rec[:, n % 2, :], hmB[:, :], ALU.mult))
                    d = On[0:PROWS, n % 2, :]
                    ins = eng.tensor_tensor(d.rearrange("p (h d) -> p h d", h=HEADS), ov[:, :, 0:HD], bc(rec[:, n % 2, :], 2, HD), ALU.mult)
                    if l == 1:
                        link(ins)
                        ins = eng.tensor_tensor(d, d, bvB[:, :], ALU.add)
                    ins.then_inc(on_ready, 1)
                elif kind == "proj":
                    dve.wait_ge(g_full[b], g + 1)
                    if l == 1:
                        dve.wait_ge(bo_added, n + 1)
                    eng.tensor_tensor(h[0:r, n, :], h[0:r, n, :], G[b][0:r, 0:DIM], ALU.add).then_inc(g_free[b], 1)
                    dve.wait_ge(g_free[b], g + 1)
                elif kind == "ffn":
                    dve.wait_ge(g_full[b], g + 1)
                    eng.tensor_tensor(fv[0:r, n % 2, :], G[b][0:r, 0:DIM], fbB[0:r, :], ALU.add).then_inc(g_free[b], 1)
                elif kind == "ffnr":
                    dve.wait_ge(tanh_ready, n + 1)
                    link(eng.tensor_tensor(h[0:r, n, :], h[0:r, n, :], fv[0:r, n % 2, :], ALU.add))
                elif kind == "log":
                    q = n % 2
                    dve.wait_ge(g_full[b], g + 1)
                    if n >= 2:
                        dve.wait_ge(se_ready, n - 1)
                    eng.tensor_tensor(lg[0:r, q, :], G[b][0:r, 0:EXP], bgB[0:r, :], ALU.add).then_inc(g_free[b], 1)
                    dve.wait_ge(g_free[b], g + 1)
                    link(eng.max(top[0:r, q, :], lg[0:r, q, :]))
                    eng.tensor_scalar(nmx[0:r, q:q + 1], top[0:r, q, 0:1], -1.0, None, ALU.mult).then_inc(neg_ready, 1)
                    link(eng.max_index(ti[0:r, q, :], top[0:r, q, :], lg[0:r, q, :]))
                    link(eng.tensor_copy(idf[0:r, n:n + 1], ti[0:r, q, 0:1]))
                    eng.tensor_scalar(oh[0:r, n, :], iota[0:r, :], idf[0:r, n:n + 1], None, ALU.is_equal).then_inc(oh_ready, 1)
                elif kind == "cnt":
                    dve.wait_ge(g_full[b], g + 1)
                    dve.wait_ge(oh_ready, n + 1)
                    if n:
                        dve.wait_ge(slots_ready, n)
                    eng.tensor_tensor(ohc[0:r, :], oh[0:r, n, :], G[b][0:r, 0:EXP], ALU.mult).then_inc(g_free[b], 1)
                    dve.wait_ge(g_free[b], g + 1)
                    eng.tensor_scalar(slotf[0:r, :], idf[0:r, n:n + 1], float(CAP), -1.0, ALU.mult, ALU.add)
                    link(eng.tensor_reduce(pos[0:r, :], ohc[0:r, :], AX.X, ALU.add))
                    link(eng.tensor_scalar(drop[0:r, :], pos[0:r, :], CAP + 0.5, DROP, ALU.is_gt, ALU.mult))
                    link(eng.scalar_tensor_tensor(out=slotf[0:r, :], in0=pos[0:r, :], scalar=drop[0:r, :], in1=slotf[0:r, :], op0=ALU.add, op1=ALU.add))
                    dve.wait_ge(se_ready, n + 1)
                    link(eng.reciprocal(tokens[0:r, n, 2 * DIM + 1:ROW], se[0:r, n:n + 1]))
                    eng.tensor_copy(sloti[0:r, n:n + 1], slotf[0:r, :]).then_inc(slots_ready, 1)

            for j in range(1, 6, 2):
                b, g = g_use(use_xe[j])
                dve.wait_ge(g_full[b], g + 1)
                ne = min(3, EXP - 3 * j)
                eng.tensor_copy(xeT[:, 3 * j:3 * j + ne, :, 0:CAP], G[b][:, 0:ne * KC * CAP].rearrange("p (e k n) -> p e k n", k=KC, n=CAP)).then_inc(g_free[b], 1)

            def hidden(it, first=False):
                for b in range(2):
                    dve.wait_ge(hid_full[b], it * 2 + 2)
                    if not first:
                        dve.wait_ge(y_full[b], it)
                    for c in range(HC // 2, HC):
                        ins = eng.tensor_scalar(hT[:, b, c, :], Hp[b][:, 1, (c - 4) * ECOLS:(c - 4) * ECOLS + CAP], b1T[:, bass.ds((it * 2 + b) * HC + c, 1)], 0.0,
                                                ALU.add, ALU.max)
                    ins.then_inc(hid_dve[b], 1)
                    dve.wait_ge(y_full[b], it + 1)
                    dve.wait_ge(b2_here[b], it * 16 + 16)
                    if not first:
                        dve.wait_ge(r_stored[b], it * 16)
                    e = it * 2 + b
                    slots = xe[0:CAP, bass.ds(e, 1), :].rearrange("p e n -> p (e n)")
                    eng.tensor_tensor(ysb[0:CAP, b, :], Yp[b][0:CAP, 0:DIM], b2B[0:CAP, b, :], ALU.add).then_inc(y_taken[b], 1)
                    dve.wait_ge(y_taken[b], it + 1)
                    eng.scalar_tensor_tensor(out=ysb[0:CAP, b, :], in0=ysb[0:CAP, b, :], scalar=slots[:, 2 * DIM + 1:ROW], in1=slots[:, 0:DIM], op0=ALU.mult, op1=ALU.add)
                    eng.tensor_copy(idx[:, b:b + 1], slots[:, 2 * DIM:2 * DIM + 1]).then_inc(r_ready[b], 1)

            hidden(0, first=True)
            with dve.Fori(1, EXP // 2) as it:
                hidden(it)


def kernel(**inputs):
    import numpy as _np
    import concourse.bacc as _bacc
    from concourse.bass_utils import run_bass_kernel_spmd as _run

    nc = _bacc.Bacc("TRN2", target_bir_lowering=False, num_devices=1)
    arrays, args, tables = {}, {}, {}
    for name in INS:
        arrays[f"in_{name}"] = a = _np.ascontiguousarray(inputs[name])
        args[name] = nc.dram_tensor(f"in_{name}", a.shape, mybir.dt.from_np(a.dtype), kind="ExternalInput").ap()
    for name, a in constants().items():
        arrays[name] = a
        tables[name] = nc.dram_tensor(name, a.shape, mybir.dt.from_np(a.dtype), kind="ExternalInput").ap()
    out = nc.dram_tensor("out", (NIMG, SEQ, DIM), F32, kind="ExternalOutput").ap()
    tower(nc, args, tables, out)
    r = _run(nc, [arrays], core_ids=[0])
    return r.results[0]["out"]
```

```python
from contextlib import ExitStack

import numpy as np

import concourse.bass as bass
from concourse import mybir

F32 = mybir.dt.float32
BF16 = mybir.dt.bfloat16
U32 = mybir.dt.uint32
ALU = mybir.AluOpType
ACT = mybir.ActivationFunctionType
AX = mybir.AxisListType

NIMG, CH, IMG, PATCH, DIM = 32, 3, 96, 16, 256
HP = IMG // PATCH
SEQ = HP * HP + 2
NTOK = NIMG * SEQ
HEADS, HD = 16, 16
KC = DIM // 128
PC = CH * PATCH * PATCH // 128
TILE_IMGS = 3
TROWS = TILE_IMGS * SEQ
TILES = -(-NIMG // TILE_IMGS)
GROUP_IMGS = 6
GCOLS = GROUP_IMGS * SEQ
GROUPS = -(-NIMG // GROUP_IMGS)
PAIRS = NIMG // 2
PCOLS = 2 * SEQ
BROW = 64
PROWS = BROW + SEQ
HSTART = [0, 3, 6, 9, 12, 13]
VW = HD + 1
EXP, HID = 16, 1024
ROW = 2 * DIM + 2
HC = HID // 128
CAP = -(-NTOK // EXP)
ECOLS = 96
XNB = 3
XG = 3
SLOTS = 4
EPS = 1e-5
MAGIC = 12582912.0
NEG = -1.0e30
DROP = 65536.0

WEIGHTS = ["L0_ffn_weight", "L0_ffn_aux_weight1", "L1_attn_Wq", "L1_attn_Wk", "L1_attn_Wv", "L1_attn_Wo"]
INS = ["x", "cls_tok", "L0_tok_cls_token", "L0_tok_cls_pos_embedding", "L0_tok_ln1_g", "L0_tok_ln1_b",
       "L0_tok_W", "L0_tok_bias", "L0_tok_ln2_g", "L0_tok_ln2_b", "L0_attn_w_attn", "L0_attn_w_proj",
       "L0_ffn_weight", "L0_ffn_aux_weight1", "L0_ffn_aux_weight2", "L0_ffn_bias", "L1_attn_Wq",
       "L1_attn_bq", "L1_attn_Wk", "L1_attn_bk", "L1_attn_Wv", "L1_attn_bv", "L1_attn_Wo", "L1_attn_bo",
       "L1_attn_head_mask", "L1_ffn_Wg", "L1_ffn_bg", "L1_ffn_W1", "L1_ffn_b1", "L1_ffn_W2", "L1_ffn_b2"]


def constants():
    p = np.arange(128)
    head = np.zeros((128, 8), np.float32)
    head[p, p // HD] = 1.0
    block = np.zeros((TROWS, HEADS), np.float32)
    for h in range(HEADS):
        at = 2 if h == HEADS - 1 else h % 3
        block[at * SEQ:(at + 1) * SEQ, h] = 1.0
    causal = np.zeros((128, 8, SEQ), np.float32)
    q = np.where(p < SEQ, p, np.where((p >= BROW) & (p < PROWS), p - BROW, SEQ))
    for r in range(128):
        causal[r, :, :] = np.where(np.arange(SEQ) > q[r], NEG, 0.0)
    upto = (p[:TROWS, None] <= p[None, :TROWS]).astype(np.float32)
    ids = (np.arange(TILES)[None, :] * TROWS + p[:TROWS, None]).astype(np.float32)
    iota = np.broadcast_to(np.arange(EXP, dtype=np.float32), (TROWS, EXP)).copy()
    omega = np.arange(DIM // 4, dtype=np.float32) / np.float32(DIM // 4 - 1)
    omega = (np.float32(1.0) / np.power(np.float32(10000.0), omega)).astype(np.float32)
    y, x = np.meshgrid(np.arange(HP, dtype=np.float32), np.arange(HP, dtype=np.float32), indexing="ij")
    y, x = y.reshape(-1)[:, None] * omega, x.reshape(-1)[:, None] * omega
    one = np.concatenate([np.zeros((2, DIM), np.float32), np.concatenate([np.sin(x), np.cos(x), np.sin(y), np.cos(y)], 1)], 0)
    pos = np.tile(one, (TILE_IMGS, 1)).astype(np.float32)
    s = np.arange(TROWS) % SEQ
    kinds = np.stack([s >= 2, s == 0, s == 1], 1).astype(np.float32)
    return {"k_ident": np.eye(128, dtype=np.float32), "k_head": head, "k_block": block,
            "k_causal": causal.reshape(128, 8 * SEQ), "k_upto": upto, "k_iota": iota, "k_ids": ids, "k_pos": pos, "k_kinds": kinds}


def rows(t):
    return min(TROWS, NTOK - t * TROWS)


def cols(t):
    return slice(t * TROWS, t * TROWS + rows(t))


def gcols(g):
    return slice(g * GCOLS, min((g + 1) * GCOLS, NTOK))


def bc(ap, axis, n):
    v = ap.unsqueeze(axis)
    shape = list(v.shape)
    shape[axis] = n
    return v.to_broadcast(shape)


PAIR, TILE = 10.0, 15.0
AFTER = {"tok": -72.44, "tokn": 7.73, "lns0": 10.73, "lnx0": 14, "lnt0": 20, "qk0": 11.58, "qk1": 1.01, "km": -18.65, "s": 2.71,
         "pt": 13.48, "vb": 7.5, "pv": 18.37, "ot": 30.07, "v": -5.94, "proj": 33.75, "lns": 0.17, "lnx": 7.21, "lnt": 10.21, "ffn": 12.18,
         "ffnr": 20, "log": 15.55, "cnt": 21.51, "scat": 27.6, "layer": 160}
LATER = {"dve": {"km": 2.66, "ot": 5.83, "v": -1.47, "ffnr": -2.8, "log": 0.6, "ffn": 0.02, "pt": 4.14, "lnt": 5.08, "qk": -6.51},
         "act": {"vb": 3.77, "s": 3.74, "tokn": -10.67, "ot": -2.37, "pv": 5.17, "qk": 0.41, "cnt": 1.49, "ffnr": -1.42, "scat": 2.3,
                 "ffn": 1.13},
         "pool": {"log": -8.19, "pv": 3.99, "cnt": 4.41, "pt": 2.77, "proj": 3.7, "km": 3.67, "qk": -5.23, "lnt": 3.51, "ffn": 2.46,
                 "ffnr": 2.62, "s": 6.29},
         "pe": {},
         "sp": {"pv": 1.1, "ot": -1.02, "log": 2.91, "cnt": -7.38, "ffnr": 1.25, "tokn": -0.49, "v": 1.58, "km": -2.72, "qk": 2.29,
                 "s": 4.54}}


def order(engine):
    at, A = [], AFTER
    last = lambda t: min((TILE_IMGS * t + TILE_IMGS - 1) // 2, PAIRS - 1)
    for t in range(TILES):
        b = TILE * t + A["tok"]
        at += [(b, "tok", 0, t), (b + A["tokn"], "tokn", 0, t), (b + A["lns0"], "lns", 0, t), (b + A["lnx0"], "lnx", 0, t), (b + A["lnt0"], "lnt", 0, t)]
    for g in range(GROUPS):
        at.append((TILE * min(2 * g + 1, TILES - 1) + A["tok"] + A["lnt0"] + A["qk0"], "qk", 0, g))
    for l in range(2):
        z = A["layer"] * l
        for p in range(PAIRS):
            at += [(z + PAIR * p + A[kind], kind, l, p) for kind in ("km", "s", "vb", "pt", "pv", "ot")]
        for t in range(TILES):
            b = z + PAIR * last(t) + A["proj"]
            at += [(z + PAIR * (TILE_IMGS * t // 2) + A["v"], "v", l, t), (b, "proj", l, t)]
            for after, norm in ((0, 1), (A["ffnr"], 2)) if l == 0 else ((0, 3),):
                at += [(b + after + A["lns"], "lns", norm, t), (b + after + A["lnx"], "lnx", norm, t), (b + after + A["lnt"], "lnt", norm, t)]
            at += [(b + A[kind], kind, 0, t) for kind in (("ffn", "ffnr") if l == 0 else ("log", "cnt", "scat"))]
        if l == 0:
            for g in range(GROUPS):
                at.append((PAIR * last(min(2 * g + 1, TILES - 1)) + A["proj"] + A["ffnr"] + A["lnt"] + A["qk1"], "qk", 1, g))
    at.sort(key=lambda a: a[0] + LATER[engine].get(a[1], 0))
    return [a[1:] for a in at]


def tower(nc, i, k, out):
    tasks = order("pe")
    uses = {}
    n = 0
    for task in tasks:
        if task[0] in ("tok", "lnt", "ot", "proj", "ffn", "log", "cnt", "v"):
            uses[task] = n
            n += 1
        elif task[0] == "qk":
            uses[task] = n
            n += 2
    rs_rank = {}
    for task in order("dve"):
        if task[0] in ("tok", "lns"):
            rs_rank[task] = len(rs_rank) + 1
    lnt_tasks = [task for task in tasks if task[0] == "lnt"]
    stats_of = [[task for task in order(engine) if task[0] in ("tok", "lns")] for engine in ("dve", "pool")]
    assert stats_of[0] == stats_of[1]
    for engine in LATER:
        mine = order(engine)
        for kind in {task[0] for task in tasks}:
            like = "lnt" if kind in ("lnx", "lns") and engine == "pe" else kind
            assert [task[1:] for task in mine if task[0] == kind] == [task[1:] for task in tasks if task[0] == like]
    xn_rank = {task[2]: m + 1 for m, task in enumerate(lnt_tasks) if task[1] == 2}
    last_uses = range(n - 3, n)
    xbuf = nc.dram_tensor("expert_in", [NTOK, ROW], F32, kind="Internal").ap()

    with ExitStack() as ctx:
        def sb(name, shape, dt=F32):
            return ctx.enter_context(nc.sbuf_tensor(name, shape, dt))

        def sem(name):
            return ctx.enter_context(nc.semaphore(name))

        def carve(arena, sizes):
            at, found = 0, []
            for s in sizes:
                found.append(arena[:, at:at + s])
                at += s
            return found

        XW = CH * PATCH * IMG
        early = sb("early", [128, 2 * XW + PC * NTOK + PC * DIM + 3 * KC * DIM])
        x0, xn0, xT_, tws_, temp_ = carve(early, [XW, XW, PC * NTOK, PC * DIM, 3 * KC * DIM])
        a1T, wT, fB = [v.rearrange("p (k n) -> p k n", k=KC) for v in carve(temp_, [KC * DIM] * 3)]
        xT = xT_.rearrange("p (k n) -> p k n", k=PC)
        tokWg = tws_.rearrange("p (f c n) -> p f c n", f=2, c=CH)
        slot = [early[:, 4096 * s:4096 * (s + 1)] for s in range(SLOTS)]
        w1s = [s[:, 0:2048].rearrange("p (k n) -> p k n", k=KC) for s in slot]
        w2s = [s[:, 2048:4096].rearrange("p (c n) -> p c n", c=HC) for s in slot]

        mid = sb("mid", [128, 14312])
        qT_, kT_, OT_, km_, P_, PTs_, Vb_, On_ = carve(mid, [KC * NTOK] * 3 + [2 * 2 * 8 * PCOLS, 2 * HEADS * SEQ, 2 * 6 * PROWS, 3 * 2 * HEADS * VW, 2 * DIM])
        qT, kT, OT = [v.rearrange("p (k n) -> p k n", k=KC) for v in (qT_, kT_, OT_)]
        km = km_.rearrange("p (b f h n) -> p b f h n", b=2, f=2, h=8)
        P = P_.rearrange("p (b h n) -> p b h n", b=2, h=HEADS)
        PTs = PTs_.rearrange("p (b j n) -> p b j n", b=2, j=6)
        Vb = Vb_.rearrange("p (b a h d) -> p b a h d", b=3, a=2, h=HEADS)
        On = On_.rearrange("p (b n) -> p b n", b=2)
        nat_, _ = carve(mid, [11 * KC * DIM, 0])
        attn_nat = nat_[:, 0:3 * KC * DIM].rearrange("p (o n) -> p o n", o=6)
        proj_nat = nat_[:, 3 * KC * DIM:4 * KC * DIM].rearrange("p (o n) -> p o n", o=KC)
        nat = {w: nat_[:, (4 + j) * KC * DIM:(5 + j) * KC * DIM].rearrange("p (o n) -> p o n", o=KC) for j, w in enumerate(WEIGHTS)}
        a2 = nat_[:, 10 * KC * DIM:11 * KC * DIM].rearrange("p (o n) -> p o n", o=KC)
        tokW = mid[:, 11 * KC * DIM:11 * KC * DIM + PC * DIM].rearrange("p (f c n) -> p f c n", f=2, c=CH)
        x1 = mid[:, 3 * KC * NTOK:3 * KC * NTOK + XW]
        at = 3 * KC * NTOK + XW
        clsB = mid[0:TROWS, at:at + 3 * DIM].rearrange("p (j n) -> p j n", j=3)
        l2bB = mid[0:TROWS, at + 3 * DIM:at + 4 * DIM]
        causf = mid[:, at + 4 * DIM:at + 4 * DIM + 8 * SEQ]
        at += 4 * DIM + 8 * SEQ
        empty = mid[0:TROWS, at:at + ROW]
        at += ROW
        b1n = mid[:, at:at + 128]
        xst_, xmv_, xrs_, xnb_ = carve(mid[0:96, at + 128:], [2 * HP * 2 * 6, 2 * HP * 2, 2 * HP, 2 * HP])
        xst = xst_.rearrange("p (u w f s) -> p u w f s", u=2, w=HP, f=2)
        xmv = xmv_.rearrange("p (u w s) -> p u w s", u=2, w=HP)
        xrs, xnb = [v.rearrange("p (u w) -> p u w", u=2) for v in (xrs_, xnb_)]
        xe_, xeT_, hT_, ysb_, b2B_ = carve(mid, [EXP * ROW, EXP * KC * ECOLS, 2 * HC * CAP, 2 * DIM, 2 * DIM])
        xe = xe_.rearrange("p (e n) -> p e n", e=EXP)
        xeT = xeT_.rearrange("p (e k n) -> p e k n", e=EXP, k=KC)
        hT = hT_.rearrange("p (b c n) -> p b c n", b=2, c=HC)
        ysb = ysb_.rearrange("p (b n) -> p b n", b=2)
        b2B = b2B_.rearrange("p (b n) -> p b n", b=2)

        tokens = sb("tokens", [TROWS, TILES, ROW])
        h, xnd = tokens[:, :, 0:DIM], tokens[:, :, DIM:2 * DIM]
        ids = sb("ids", [TROWS, TILES])
        xnT = sb("xnT", [128, KC, NTOK])
        vt = sb("vt", [TROWS, 2, DIM])
        v3 = sb("v3", [TROWS, 2 * TILE_IMGS, DIM])
        xn = sb("xn", [TROWS, XNB, DIM])
        fv = sb("fv", [TROWS, 2, DIM])
        qkvT = sb("qkvT", [128, KC, 3 * DIM])
        projT = sb("projT", [128, KC, DIM])
        ffnW = sb("ffnW", [128, KC, DIM])
        wqkvT = sb("wqkvT", [128, KC, 3 * DIM])
        woT = sb("woT", [128, KC, DIM])
        gateW = sb("gateW", [128, KC, EXP])
        b1T = sb("b1T", [128, EXP * HC])
        ident = sb("ident", [128, 128])
        ones = sb("ones", [128, 128])
        headm = sb("headm", [128, 8])
        blockm = sb("blockm", [TROWS, HEADS])
        causb = sb("causb", [128, 8 * SEQ], BF16)
        identb = sb("identb", [128, PROWS], BF16)
        upto = sb("upto", [TROWS, TROWS])
        iota = sb("iota", [TROWS, EXP])
        addA = sb("addA", [TROWS, DIM])
        kinds = sb("kinds", [TROWS, 3])
        g2B = sb("g2B", [TROWS, DIM])
        biasB = sb("biasB", [TROWS, DIM])
        fbB = sb("fbB", [TROWS, DIM])
        boB = sb("boB", [TROWS, DIM])
        bv = sb("bv", [128, KC])
        hmB = sb("hmB", [128, HEADS])
        hm = sb("hm", [128, KC])
        hmh = sb("hmh", [128, KC, HEADS // KC])
        bgB = sb("bgB", [TROWS, EXP])
        bq = sb("bq", [128, KC])
        bk = sb("bk", [128, KC])
        g1 = sb("g1", [128, 2, CH])
        be1 = sb("be1", [128, 2, CH])
        mhalf = sb("mhalf", [128, 1])
        asum = sb("asum", [128, 2])
        qs = sb("qs", [128, 8])
        st = sb("st", [TROWS, 2, 6])
        mv = sb("mv", [TROWS, 5 * TILES, 2])
        rs = sb("rs", [TROWS, 5 * TILES, 1])
        mx = sb("mx", [PROWS, 2, HEADS])
        rec = sb("rec", [PROWS, 2, HEADS])
        lg = sb("lg", [TROWS, 2, EXP])
        top = sb("top", [TROWS, 2, 8])
        ti = sb("ti", [TROWS, 2, 8], U32)
        nmx = sb("nmx", [TROWS, 2])
        ex = sb("ex", [TROWS, EXP])
        se = sb("se", [TROWS, TILES])
        idf = sb("idf", [TROWS, TILES])
        oh = sb("oh", [TROWS, TILES, EXP])
        ohs = sb("ohs", [TROWS, 2, EXP])
        ohc = sb("ohc", [TROWS, EXP])
        pos = sb("pos", [TROWS, 2])
        drop = sb("drop", [TROWS, 1])
        slotf = sb("slotf", [TROWS, 1])
        sloti = sb("sloti", [TROWS, TILES], U32)
        idx = sb("idx", [CAP, 2], U32)

        bank = [ctx.enter_context(nc.psum_tensor(f"bank{b}", [128, 1024], F32)) for b in range(4)]
        Sp = bank[0][:, :].rearrange("p (f n) -> p f n", f=2)
        PTp = bank[1][:, :].rearrange("p (f n) -> p f n", f=2)
        Op = bank[2][:, 512:1024]
        G = [bank[3][:, 0:512], bank[3][:, 512:1024], bank[2][:, 0:512]]
        ring = [bank[b][:, 512 * f:512 * f + 512] for b in range(3) for f in range(2)]
        Hp = [bank[0][:, :].rearrange("p (f n) -> p f n", f=2), bank[1][:, :].rearrange("p (f n) -> p f n", f=2)]
        Yp = [G[2], Op]

        l_ident, l_x, l_nat, l_tok, l_bias, l_zero = (
            sem("l_ident"), [[sem(f"l_x{u}{c}") for c in range(CH)] for u in range(2)],
            [sem(f"l_nat{j}") for j in range(4)], sem("l_tok"), sem("l_bias"), sem("l_zero"))
        zeroed, consts, causal_ready, xstats, xrstd, xnorm_dve, xnorm_act = (
            sem("zeroed"), sem("consts"), sem("causal_ready"), sem("xstats"), sem("xrstd"), sem("xnorm_dve"), sem("xnorm_act"))
        ring_full = [sem(f"ring_full{b}") for b in range(6)]
        ring_free = [sem(f"ring_free{b}") for b in range(6)]
        asum_ready, quant_ready, tokw_ready, tables_ready = (
            sem("asum_ready"), sem("quant_ready"), sem("tokw_ready"), sem("tables_ready"))
        g_full, g_free = [sem(f"g_full{b}") for b in range(3)], [sem(f"g_free{b}") for b in range(3)]
        mv_ready, rs_ready, xn_ready = sem("mv_ready"), sem("rs_ready"), sem("xn_ready")
        km_ready, km2_ready, vb_ready = sem("km_ready"), sem("km2_ready"), sem("vb_ready")
        v_spread = [sem("v_spread0"), sem("v_spread1")]
        s_full, p_ready, p_exp, pt_full, pt_ready = sem("s_full"), sem("p_ready"), sem("p_exp"), sem("pt_full"), sem("pt_ready")
        o_full, on_ready = sem("o_full"), sem("on_ready")
        bo_added, tanh_ready, neg_ready, oh_ready, se_ready = (
            sem("bo_added"), sem("tanh_ready"), sem("neg_ready"), sem("oh_ready"), sem("se_ready"))
        slots_ready, pos_ready, scattered, pad_zero, ohs_ready = sem("slots_ready"), sem("pos_ready"), sem("scattered"), sem("pad_zero"), sem("ohs_ready")
        xe_loaded, rest_loaded = [sem(f"xe_loaded{j}") for j in range(-(-EXP // XG))], sem("rest_loaded")
        xe_full, xe_free = [sem("xe_full0"), sem("xe_full1")], [sem("xe_free0"), sem("xe_free1")]
        w1_here, w2_here = [sem(f"w1_here{s}") for s in range(SLOTS)], [sem(f"w2_here{s}") for s in range(SLOTS)]
        w1_used = [sem(f"w1_used{s}") for s in range(SLOTS)]
        hid_full, hid_act, hid_dve = [[sem(f"{n}{b}") for b in range(2)] for n in ("hid_full", "hid_act", "hid_dve")]
        y_full, y_taken, r_ready, r_stored, b2_here = [[sem(f"{n}{b}") for b in range(2)] for n in ("y_full", "y_taken", "r_ready", "r_stored", "b2_here")]
        stored = sem("stored")
        dve_done, pool_done = sem("dve_done"), sem("pool_done")

        def chain(eng, s):
            count = [0]

            def link(ins):
                count[0] += 1
                ins.then_inc(s, 1)
                eng.wait_ge(s, count[0])
            return link

        def x_uses(half):
            return [("x", half, kc, w3) for w3 in range(2) for kc in range(PC)]
        start = ([("T", "qkv0"), ("T", "qkv1"), ("T", "qkv2"), ("T", "proj")] + x_uses(0)
                 + [("T", WEIGHTS[1]), ("T", WEIGHTS[0]), ("T", WEIGHTS[2]), ("sum",), ("T", WEIGHTS[3]), ("T", WEIGHTS[4])] + x_uses(1)
                 + [("T", WEIGHTS[5]), ("bias",), ("b1",), ("fB",), ("bo",), ("fW",)])
        dve_cols, act_cols = [(0, 2, 4), (0, 2, 3, 4)], [(1, 3, 5), (1, 5)]
        x_first = [("x", half, 0, 0) for half in range(2)]
        start_at = {u: n for n, u in enumerate(start)}
        on_dve = {("T", "qkv1"), ("T", "proj"), ("sum",), ("T", WEIGHTS[2]), ("bias",), ("T", WEIGHTS[5]), ("fB",), ("bo",)}
        ring_total = [len([1 for n in range(len(start)) if n % 6 == b]) for b in range(6)]

        T_dst = {"qkv0": qkvT[:, :, 0:DIM], "qkv1": qkvT[:, :, DIM:2 * DIM], "qkv2": qkvT[:, :, 2 * DIM:], "proj": projT[:, :, :],
                 WEIGHTS[1]: a1T, WEIGHTS[0]: wT, WEIGHTS[2]: wqkvT[:, :, 0:DIM], WEIGHTS[3]: wqkvT[:, :, DIM:2 * DIM],
                 WEIGHTS[4]: wqkvT[:, :, 2 * DIM:], WEIGHTS[5]: woT[:, :, :]}
        T_src = {"qkv0": attn_nat[:, 0:2, :], "qkv1": attn_nat[:, 2:4, :], "qkv2": attn_nat[:, 4:6, :], "proj": proj_nat, **nat}
        T_load = {"qkv0": 0, "qkv1": 0, "qkv2": 0, "proj": 0, WEIGHTS[0]: 1, WEIGHTS[1]: 1, WEIGHTS[2]: 2, WEIGHTS[3]: 2, WEIGHTS[4]: 3, WEIGHTS[5]: 3}
        T_count = [4 * 16, 3 * 16, 2 * 16, 2 * 16]
        xs = [x0, x1]
        xv = [v[0:96, :].rearrange("p (r w q) -> p r w q", r=CH * PATCH, w=HP) for v in xs]
        xnv = [v[0:96, :].rearrange("p (w n) -> p w n", w=HP) for v in (xn0, x0)]

        def empty_ring(eng, op, u):
            n = start_at[u]
            b = n % 6
            eng.wait_ge(ring_full[b], n // 6 + 1)
            if u[0] == "T":
                d = T_dst[u[1]]
                scale = 0.25 if u[1] == WEIGHTS[2] else 1.0
                ins = op(d, ring[b].rearrange("p (k n) -> p k n", k=KC), scale)
            elif u[0] == "b1":
                ins = op(b1T[:, :], ring[b][:, 0:128], 1.0)
            elif u[0] in ("fB", "fW"):
                ins = op(fB if u[0] == "fB" else ffnW[:, :, :], ring[b].rearrange("p (k n) -> p k n", k=KC), 1.0)
            elif u[0] == "x":
                _, half, kc, w3 = u
                d = xT[:, kc, half * 16 * SEQ:(half + 1) * 16 * SEQ].rearrange("p (b s) -> p b s", s=SEQ)[:, :, 2:SEQ]
                d = d.rearrange("p b (y w) -> p b y w", w=HP)[:, :, :, 3 * w3:3 * w3 + 3]
                ins = op(d, ring[b][:, 0:288].rearrange("p (w b y) -> p b y w", w=3, y=HP), 1.0)
            ins.then_inc(ring_free[b], 1)

        def v_spread_count(u):
            return sum(16 * 3 * (rows(v % TILES) // SEQ) for v in range(u % 2, u + 1, 2))

        def g_use(n):
            return n % 3, n // 3

        def emptied(eng, n):
            b, g = g_use(n)
            eng.wait_ge(g_free[b], g + 1)

        out_rows = out.rearrange("b s n -> (b s) n")
        row_loads = [(biasB[:, :], i["L0_tok_bias"]), (g2B[:, :], i["L0_tok_ln2_g"]), (l2bB, i["L0_tok_ln2_b"]),
                     (clsB[:, 0, :], i["cls_tok"].rearrange("a b n -> (a b n)")),
                     (clsB[:, 1, :], i["L0_tok_cls_token"].rearrange("a b n -> (a b n)")),
                     (clsB[:, 2, :], i["L0_tok_cls_pos_embedding"].rearrange("a b n -> (a b n)")),
                     (hmB[:, :], i["L1_attn_head_mask"]), (fbB[:, :], i["L0_ffn_bias"]), (boB[:, :], i["L1_attn_bo"]), (bgB[:, :], i["L1_ffn_bg"])]
        table_loads = [(kinds, "k_kinds"), (addA, "k_pos"), (headm, "k_head"), (blockm, "k_block"), (upto, "k_upto"), (iota, "k_iota"), (ids, "k_ids")]
        column_loads = [(bq, "L1_attn_bq"), (bk, "L1_attn_bk"), (bv, "L1_attn_bv")]
        small_loads = 16 * (len(row_loads) + len(table_loads) + len(column_loads) + 1)
        block = ctx.enter_context(nc.Block())

        @block.sync
        def _(sp):
            sp.dma_start(ident[:, :], k["k_ident"]).then_inc(l_ident, 16)

            def images(u):
                for c in range(CH):
                    sp.dma_start(xs[u][0:96, c * PATCH * IMG:(c + 1) * PATCH * IMG],
                                 i["x"][16 * u:16 * u + 16, c].rearrange("b (y r) w -> b y (r w)", y=HP)).then_inc(l_x[u][c], 16)
            images(0)
            sp.dma_start(attn_nat, i["L0_attn_w_attn"].rearrange("(o p) n -> p o n", p=128)).then_inc(l_nat[0], 16)
            sp.dma_start(proj_nat, i["L0_attn_w_proj"].rearrange("(o p) n -> p o n", p=128)).then_inc(l_nat[0], 16)
            sp.dma_start(b1n, i["L1_ffn_b1"].rearrange("e (c p) -> (e c) p", p=128)).then_inc(l_nat[0], 16)
            sp.dma_start(causf, k["k_causal"]).then_inc(l_nat[0], 16)
            images(1)
            for j, names in ((1, ["L0_ffn_weight", "L0_ffn_aux_weight1", "L0_ffn_aux_weight2"]), (2, WEIGHTS[2:4]), (3, WEIGHTS[4:6])):
                for w in names:
                    sp.dma_start(a2 if w == "L0_ffn_aux_weight2" else nat[w], i[w].rearrange("(o p) n -> p o n", p=128)).then_inc(l_nat[j], 16)
            sp.wait_ge(zeroed, 1)
            sp.dma_start(xbuf[0:10 * TROWS, :].rearrange("(t p) n -> p t n", p=TROWS), bc(empty[:, :], 1, 10)).then_inc(l_zero, 16)
            sp.dma_start(xbuf[10 * TROWS:NTOK, :], empty[0:rows(10), :]).then_inc(l_zero, 16)

            def half_w1(s, e, half):
                sp.dma_start(w1s[s][:, half, :], i["L1_ffn_W1"][e, half * 128:(half + 1) * 128, :].rearrange("e p n -> p (e n)")).then_inc(w1_here[s], 16)

            def half_w2(s, e, half):
                at = slice(half * HC // 2, (half + 1) * HC // 2)
                sp.dma_start(w2s[s][:, at, :], i["L1_ffn_W2"][e, half * HID // 2:(half + 1) * HID // 2, :].rearrange("e (c p) n -> p (e c) n", p=128)).then_inc(w2_here[s], 16)

            first_loads = [(load, s, half) for s in range(SLOTS) for load in (half_w1, half_w2) for half in range(2)]
            slots_free = False
            for kind, l, n in order("sp"):
                if kind == "tok" and n == TILES - 1:
                    emptied(sp, uses[(kind, l, n)])
                    slots_free = True
                elif kind == "v":
                    m = l * TILES + n + 1
                    emptied(sp, uses[(kind, l, n)])
                    pairs = l * PAIRS + ((TILE_IMGS * (n - 1) - 1) // 2 + 1 if n >= 2 else 0)
                    if pairs:
                        sp.wait_ge(vb_ready, pairs)
                    for a in range(rows(n) // SEQ):
                        for j in range(3):
                            sp.dma_start(v3[j * SEQ:(j + 1) * SEQ, (TILE_IMGS * n + a) % (2 * TILE_IMGS), :], vt[a * SEQ:(a + 1) * SEQ, (m - 1) % 2, :]).then_inc(v_spread[(m - 1) % 2], 16)
                    if slots_free and first_loads:
                        load, s, half = first_loads.pop(0)
                        load(s, slice(s, s + 1), half)
            for load, s, half in first_loads:
                load(s, slice(s, s + 1), half)
            for t in range(TILES):
                emptied(sp, uses[("proj", 1, t)])
                sp.dma_start(out_rows[cols(t), :], h[0:rows(t), t, :]).then_inc(stored, 16)
            sp.wait_ge(scattered, 16 * TILES)
            for j in range(-(-EXP // XG)):
                e0, e1 = XG * j, min(XG * j + XG, EXP)
                sp.dma_start(xe[0:CAP, e0:e1, DIM:2 * DIM], xbuf[e0 * CAP:e1 * CAP, DIM:2 * DIM].rearrange("(e p) n -> p e n", p=CAP)).then_inc(xe_loaded[j], 16)
            with nc.allow_non_contiguous_dma(reason="two words of each token's row"):
                for part in (slice(0, DIM), slice(2 * DIM, ROW)):
                    sp.dma_start(xe[0:CAP, :, part], xbuf[:, part].rearrange("(e p) n -> p e n", p=CAP)).then_inc(rest_loaded, 16)
            with sp.Fori(1, EXP // SLOTS) as it:
                for s in range(SLOTS):
                    sp.wait_ge(w1_used[s], it)
                    for half in range(2):
                        half_w1(s, bass.ds(it * SLOTS + s, 1), half)
                    sp.wait_ge(y_full[s % 2], it * (SLOTS // 2) + s // 2 - 1)
                    for half in range(2):
                        half_w2(s, bass.ds(it * SLOTS + s, 1), half)

        @block.gpsimd
        def _(pool):
            link = chain(pool, pool_done)
            eng = nc.gpsimd
            eng.memset(mhalf[:, :], -0.5)
            eng.memset(ones[:, :], 1.0).then_inc(consts, 1)
            pool.dma_start(tokW.rearrange("p f c n -> p f (c n)"), i["L0_tok_W"].rearrange("(f p c) n -> p f (c n)", f=2, c=CH)).then_inc(l_tok, 16)
            with nc.allow_non_contiguous_dma(reason="small vectors laid over partitions"):
                for d, v in ((g1, "L0_tok_ln1_g"), (be1, "L0_tok_ln1_b")):
                    pool.dma_start(d[:, :, :], i[v].rearrange("(f p c) -> p f c", f=2, c=CH)).then_inc(l_tok, 16)
            link(eng.memset(empty[:, :], 0.0))
            eng.memset(empty[:, 2 * DIM:2 * DIM + 1], DROP).then_inc(zeroed, 1)
            eng.memset(ohs[:, 0, :], 0.0)
            link(eng.memset(xT.rearrange("p k (b s) -> p k b s", s=SEQ)[:, :, :, 0:2], 0.0))
            pool.wait_ge(l_tok, 48)
            eng.tensor_tensor(tokWg, tokW, bc(g1[:, :, :], 3, DIM), ALU.mult).then_inc(tokw_ready, 1)

            def patch_scales(u):
                pool.wait_ge(xstats, u + 1)
                link(eng.tensor_scalar(xrs[:, u, :], xmv[:, u, :, 1], EPS, None, ALU.add))
                link(eng.tensor_tensor(xrs[:, u, :], xrs[:, u, :], mhalf[0:96, :].to_broadcast([96, HP]), ALU.pow))
                link(eng.tensor_tensor(xnb[:, u, :], xrs[:, u, :], xmv[:, u, :, 0], ALU.mult))
                eng.tensor_scalar(xnb[:, u, :], xnb[:, u, :], -1.0, None, ALU.mult).then_inc(xrstd, 1)
            patch_scales(0)
            patch_scales(1)
            pool.wait_ge(l_bias, small_loads)
            link(eng.tensor_tensor(clsB[:, 1, :], clsB[:, 1, :], clsB[:, 2, :], ALU.add))
            for v, c in ((l2bB, 0), (clsB[:, 0, :], 1), (clsB[:, 1, :], 2)):
                link(eng.tensor_scalar(v, v, kinds[:, c:c + 1], None, ALU.mult))
                link(eng.tensor_tensor(addA[:, :], addA[:, :], v, ALU.add))
            eng.tensor_scalar(g2B[:, :], g2B[:, :], kinds[:, 0:1], None, ALU.mult)
            eng.tensor_copy(tokens[:, :, 2 * DIM:2 * DIM + 1], ids[:, :].unsqueeze(2))
            eng.tensor_scalar(bq[:, :], bq[:, :], 0.25, None, ALU.mult).then_inc(tables_ready, 1)

            counts = {"mv": 0, "km": 0}
            for kind, l, n in order("pool"):
                if kind in ("tok", "lns"):
                    r, j = rows(n), (n if kind == "tok" else (l + 1) * TILES + n)
                    counts["mv"] += 1
                    pool.wait_ge(mv_ready, counts["mv"])
                    link(eng.tensor_scalar(rs[0:r, j, :], mv[0:r, j, 1:2], EPS, None, ALU.add))
                    ins = eng.tensor_tensor(rs[0:r, j, :], rs[0:r, j, :], mhalf[0:r, :], ALU.pow)
                    ins.then_inc(rs_ready, 1)
                elif kind == "km":
                    emptied(pool, uses[("qk", l, 2 * n // GROUP_IMGS)] + 1)
                    counts["km"] += 1
                    if counts["km"] > 2:
                        pool.wait_ge(s_full, counts["km"] - 2)
                    for f in range(2 if l == 0 else 1):
                        ins = eng.tensor_tensor(km[:, n % 2, f], bc(kT[:, f, n * PCOLS:(n + 1) * PCOLS], 1, 8), bc(headm[:, :], 2, PCOLS), ALU.mult)
                    ins.then_inc(km_ready, 1)
                elif kind == "vb":
                    m = l * PAIRS + n + 1
                    t = l * TILES + (2 * n + 1) // TILE_IMGS
                    for u in (t - 1, t):
                        if u >= 0:
                            pool.wait_ge(v_spread[u % 2], v_spread_count(u))
                    if m > 3:
                        pool.wait_ge(o_full, m - 3)
                    at = 2 * n % (2 * TILE_IMGS)
                    if m <= 3:
                        eng.tensor_copy(Vb[0:TROWS, (m - 1) % 3, :, :, HD:VW], bc(bc(blockm[:, :], 1, 2), 3, 1))
                    eng.tensor_tensor(Vb[0:TROWS, (m - 1) % 3, :, :, 0:HD], v3[:, at:at + 2, :].rearrange("p a (h d) -> p a h d", h=HEADS),
                                      bc(bc(blockm[:, :], 1, 2), 3, HD), ALU.mult).then_inc(vb_ready, 1)
                elif kind == "lnx" and l == 2:
                    pool.wait_ge(xn_ready, xn_rank[n])
                    eng.tensor_tensor(h[0:rows(n), n, :], h[0:rows(n), n, :], boB[0:rows(n), :], ALU.add).then_inc(bo_added, 1)
                elif kind == "cnt":
                    if n < TILES - 1:
                        pool.wait_ge(oh_ready, n + 1)
                        if n >= 2:
                            emptied(pool, uses[("cnt", 0, n - 1)])
                        if n:
                            pool.wait_ge(ohs_ready, n)
                        eng.tensor_tensor(ohs[:, (n + 1) % 2, :], ohs[:, n % 2, :], oh[:, n, :], ALU.add).then_inc(ohs_ready, 1)
                elif kind == "scat":
                    r = rows(n)
                    p = pos[0:r, n % 2:n % 2 + 1]
                    pool.wait_ge(pos_ready, n + 1)
                    eng.tensor_scalar(slotf[0:r, :], idf[0:r, n:n + 1], float(CAP), -1.0, ALU.mult, ALU.add)
                    link(eng.tensor_scalar(drop[0:r, :], p, CAP + 0.5, DROP, ALU.is_gt, ALU.mult))
                    link(eng.tensor_tensor(slotf[0:r, :], slotf[0:r, :], p, ALU.add))
                    link(eng.tensor_tensor(slotf[0:r, :], slotf[0:r, :], drop[0:r, :], ALU.add))
                    eng.tensor_copy(sloti[0:r, n:n + 1], slotf[0:r, :]).then_inc(slots_ready, 1)
                    pool.wait_ge(slots_ready, n + 1)
                    pool.wait_ge(l_zero, 32)
                    eng.indirect_dma_start(out=xbuf, out_offset=bass.IndirectOffsetOnAxis(ap=sloti[0:rows(n), n:n + 1], axis=0),
                                           in_=tokens[0:rows(n), n, :], in_offset=None, bounds_check=NTOK - 1, oob_is_err=False).then_inc(scattered, 16)

            pool.wait_ge(scattered, 16 * TILES)
            eng.memset(xeT[:, :, :, CAP:ECOLS], 0.0).then_inc(pad_zero, 1)
            for b in range(2):
                pool.dma_start(b2B[0:CAP, b, :], i["L1_ffn_b2"][b, :].partition_broadcast(CAP)).then_inc(b2_here[b], 16)
            pool.wait_ge(stored, 16 * TILES)

            def results(b):
                eng.indirect_dma_start(out=out_rows, out_offset=bass.IndirectOffsetOnAxis(ap=idx[:, b:b + 1], axis=0), in_=ysb[0:CAP, b, :],
                                       in_offset=None, bounds_check=NTOK - 1, oob_is_err=False).then_inc(r_stored[b], 16)
            with pool.Fori(0, EXP // 2 - 1) as it:
                for b in range(2):
                    pool.wait_ge(r_ready[b], it + 1)
                    pool.dma_start(b2B[0:CAP, b, :], i["L1_ffn_b2"][bass.ds(it * 2 + b + 2, 1), :].rearrange("e n -> (e n)").partition_broadcast(CAP)
                                   ).then_inc(b2_here[b], 16)
                    results(b)
            for b in range(2):
                pool.wait_ge(r_ready[b], EXP // 2)
                results(b)
            for b in range(2):
                pool.wait_ge(r_stored[b], 16 * EXP // 2)

        @block.tensor
        def _(pe):
            mm, tr = nc.tensor.matmul, nc.tensor.transpose
            pe.wait_ge(l_ident, 16)
            for u in start:
                n = start_at[u]
                b = n % 6
                if n >= 6:
                    pe.wait_ge(ring_free[b], n // 6)
                if u[0] == "T":
                    pe.wait_ge(l_nat[T_load[u[1]]], T_count[T_load[u[1]]])
                    for kc in range(KC):
                        for oc in range(KC):
                            ins = tr(ring[b][:, kc * DIM + oc * 128:kc * DIM + oc * 128 + 128], T_src[u[1]][:, oc, kc * 128:kc * 128 + 128], ident[:, :])
                elif u[0] == "b1":
                    ins = tr(ring[b][:, 0:128], b1n, ident[:, :])
                elif u[0] == "sum":
                    pe.wait_ge(asum_ready, 1)
                    pe.wait_ge(consts, 1)
                    ins = mm(ring[b][:, 0:2], ones[:, :], asum[:, :], start=True, stop=True)
                elif u[0] == "fB":
                    pe.wait_ge(ring_free[start_at[("T", WEIGHTS[1])] % 6], start_at[("T", WEIGHTS[1])] // 6 + 1)
                    for ic in range(KC):
                        for kc in range(KC):
                            ins = mm(ring[b][:, ic * DIM:(ic + 1) * DIM], a1T[:, kc, ic * 128:ic * 128 + 128], a2[:, kc, :], start=kc == 0, stop=kc == KC - 1)
                elif u[0] == "fW":
                    for d in (("fB",), ("T", WEIGHTS[0])):
                        pe.wait_ge(ring_free[start_at[d] % 6], start_at[d] // 6 + 1)
                    for ic in range(KC):
                        for kc in range(KC):
                            ins = mm(ring[b][:, ic * DIM:(ic + 1) * DIM], wT[:, kc, ic * 128:ic * 128 + 128], fB[:, kc, :], start=kc == 0, stop=kc == KC - 1)
                elif u[0] == "bias":
                    pe.wait_ge(l_tok, 48)
                    for j in range(PC):
                        f, c = j % 2, j // 2
                        ins = mm(ring[b][0:TROWS, 0:DIM], be1[:, f, c:c + 1].to_broadcast([128, TROWS]), tokW[:, f, c, :], start=j == 0, stop=j == PC - 1)
                elif u[0] == "bo":
                    pe.wait_ge(ring_free[start_at[("T", WEIGHTS[5])] % 6], start_at[("T", WEIGHTS[5])] // 6 + 1)
                    for kc in range(KC):
                        ins = mm(ring[b][0:TROWS, 0:DIM], bv[:, kc:kc + 1].to_broadcast([128, TROWS]), woT[:, kc, :], start=kc == 0, stop=kc == KC - 1)
                elif u[0] == "x":
                    _, half, kc, w3 = u
                    for ready, columns in ((xnorm_dve, dve_cols), (xnorm_act, act_cols)):
                        pe.wait_ge(ready, half * len(columns[0]) + len([w for w in columns[half] if w < 3 * w3 + 3]))
                    for w in range(3):
                        ins = tr(ring[b][:, w * 96:(w + 1) * 96], xnv[half][:, 3 * w3 + w, kc * 128:kc * 128 + 128], ident[0:96, 0:96])
                ins.then_inc(ring_full[b], 1)

            def take(n):
                b, m = g_use(n)
                if m:
                    pe.wait_ge(g_free[b], m)
                elif b == 2:
                    pe.wait_ge(ring_free[4], ring_total[4])
                return G[b], g_full[b]

            done = {}
            for kind, l, n in order("pe"):
                done[kind] = done.get(kind, 0) + 1
                m = done[kind]
                if kind == "tok":
                    if n == 0:
                        pe.wait_ge(tokw_ready, 1)
                        for b in range(6):
                            at = [start_at[u] for u in x_uses(1) if start_at[u] % 6 == b][-1]
                            pe.wait_ge(ring_free[b], at // 6 + 1)
                    ps, full = take(uses[(kind, l, n)])
                    for j in range(PC):
                        mm_ = mm(ps[0:rows(n), 0:DIM], xT[:, j, cols(n)], tokWg[:, j % 2, j // 2, :], start=j == 0, stop=j == PC - 1)
                    mm_.then_inc(full, 1)
                elif kind == "lnt":
                    pe.wait_ge(xn_ready, m)
                    ps, full = take(uses[(kind, l, n)])
                    src = xnd[:, n, :] if l == 3 else xn[:, (m - 1) % XNB, :]
                    for kc in range(KC):
                        ins = tr(ps[:, kc * TROWS:kc * TROWS + rows(n)], src[0:rows(n), kc * 128:kc * 128 + 128], ident[0:rows(n), 0:rows(n)])
                    ins.then_inc(full, 1)
                elif kind == "qk":
                    for t in range(2 * n, min(2 * n + 2, TILES)):
                        emptied(pe, uses[("lnt", 2 * l, t)])
                    if m == 1:
                        pe.wait_ge(quant_ready, 1)
                    w = wqkvT if l else qkvT
                    width = gcols(n).stop - gcols(n).start
                    for j in range(2):
                        ps, full = take(uses[(kind, l, n)] + j)
                        for oc in range(KC):
                            for kc in range(KC):
                                ins = mm(ps[:, oc * width:(oc + 1) * width], w[:, kc, j * DIM + oc * 128:j * DIM + oc * 128 + 128], xnT[:, kc, gcols(n)],
                                         start=kc == 0, stop=kc == KC - 1)
                        ins.then_inc(full, 1)
                elif kind == "v":
                    emptied(pe, uses[("lnt", 2 * l, n)])
                    if m == 1:
                        pe.wait_ge(quant_ready, 1)
                    ps, full = take(uses[(kind, l, n)])
                    w = wqkvT if l else qkvT
                    for kc in range(KC):
                        ins = mm(ps[0:rows(n), 0:DIM], xnT[:, kc, cols(n)], w[:, kc, 2 * DIM:3 * DIM], start=kc == 0, stop=kc == KC - 1)
                    ins.then_inc(full, 1)
                elif kind == "s":
                    if m == 1:
                        for b in (0, 1):
                            pe.wait_ge(ring_free[b], ring_total[b])
                    pe.wait_ge(km_ready, m)
                    if l == 1:
                        pe.wait_ge(km2_ready, n + 1)
                    if m > 1:
                        pe.wait_ge(p_ready, m - 1)
                    if m == 1:
                        pe.wait_ge(causal_ready, 1)
                    for f in range(2):
                        o = Sp[:, f, 0:8 * SEQ]
                        if l == 0:
                            mm(o[0:PROWS, :], identb[:, :], causb[:, :], start=True, stop=False, skip_group_check=True)
                        at = n * PCOLS
                        mm(o[0:BROW, :], qT[:, f, at:at + BROW], km[:, n % 2, f, :, 0:SEQ], start=l == 1, stop=True, skip_group_check=True)
                        ins = mm(o[BROW:PROWS, :], qT[:, f, at + SEQ:at + PCOLS], km[:, n % 2, f, :, SEQ:PCOLS], start=l == 1, stop=True, skip_group_check=True)
                    ins.then_inc(s_full, 1)
                elif kind == "pt":
                    if m == 1:
                        for b in (2, 3):
                            pe.wait_ge(ring_free[b], ring_total[b])
                    pe.wait_ge(p_exp, m)
                    if m > 1:
                        pe.wait_ge(pt_ready, m - 1)
                    for j in range(6):
                        ins = tr(PTp[0:TROWS, j // 3, (j % 3) * PROWS:(j % 3 + 1) * PROWS], P[0:PROWS, n % 2, HSTART[j]:HSTART[j] + 3, :], ident[0:PROWS, 0:PROWS])
                    ins.then_inc(pt_full, 1)
                elif kind == "pv":
                    if m == 1:
                        for b in (5,):
                            pe.wait_ge(ring_free[b], ring_total[b])
                    pe.wait_ge(pt_ready, m)
                    pe.wait_ge(vb_ready, m)
                    if m > 1:
                        pe.wait_ge(on_ready, m - 1)
                    for j in range(6):
                        h0 = 3 * j
                        h1 = min(h0 + 3, HEADS)
                        for a, (r0, r1) in enumerate(((0, BROW), (BROW, PROWS))):
                            ins = mm(Op[r0:r1, h0 * VW:h1 * VW], PTs[0:TROWS, n % 2, j, r0:r1], Vb[0:TROWS, (m - 1) % 3, a, h0:h1, :], start=True, stop=True)
                    ins.then_inc(o_full, 1)
                elif kind == "ot":
                    pe.wait_ge(on_ready, m)
                    ps, full = take(uses[(kind, l, n)])
                    for f in range(2):
                        ins = tr(ps[:, f * PROWS:(f + 1) * PROWS], On[0:PROWS, n % 2, f * 128:f * 128 + 128], ident[0:PROWS, 0:PROWS])
                    ins.then_inc(full, 1)
                elif kind == "proj":
                    for p in range(TILE_IMGS * n // 2, min((TILE_IMGS * n + 2) // 2, PAIRS - 1) + 1):
                        emptied(pe, uses[("ot", l, p)])
                    ps, full = take(uses[(kind, l, n)])
                    w = woT if l else projT
                    for kc in range(KC):
                        ins = mm(ps[0:rows(n), 0:DIM], OT[:, kc, cols(n)], w[:, kc, :], start=kc == 0, stop=kc == KC - 1)
                    ins.then_inc(full, 1)
                elif kind in ("ffn", "log"):
                    emptied(pe, uses[("lnt", 1 if kind == "ffn" else 3, n)])
                    ps, full = take(uses[(kind, l, n)])
                    w, width = (ffnW, DIM) if kind == "ffn" else (gateW, EXP)
                    for kc in range(KC):
                        ins = mm(ps[0:rows(n), 0:width], xnT[:, kc, cols(n)], w[:, kc, :], start=kc == 0, stop=kc == KC - 1)
                    ins.then_inc(full, 1)
                elif kind == "cnt":
                    r = rows(n)
                    pe.wait_ge(oh_ready, n + 1)
                    ps, full = take(uses[(kind, l, n)])
                    ins = mm(ps[0:r, 0:EXP], upto[0:r, 0:r], oh[0:r, n, :], start=True, stop=n == 0)
                    if n:
                        pe.wait_ge(ohs_ready, n)
                        ins = mm(ps[0:r, 0:EXP], ones[0:TROWS, 0:r], ohs[:, n % 2, :], start=False, stop=True)
                    ins.then_inc(full, 1)

            def transpose(j):
                pe.wait_ge(xe_loaded[j], 16)
                if j >= 2:
                    pe.wait_ge(xe_free[j % 2], j // 2)
                for e in range(XG * j, min(XG * j + XG, EXP)):
                    for kc in range(KC):
                        at = ((e - XG * j) * KC + kc) * CAP
                        ins = tr(G[j % 2][:, at:at + CAP], xe[0:CAP, e, DIM + kc * 128:DIM + kc * 128 + 128], ident[0:CAP, 0:CAP])
                ins.then_inc(xe_full[j % 2], 1)

            def transposed(j):
                pe.wait_ge(xe_free[j % 2], j // 2 + 1)

            for use in last_uses:
                emptied(pe, use)
            transpose(0)
            transpose(1)
            pe.wait_ge(pad_zero, 1)

            def experts(it, first=False):
                for s in range(SLOTS):
                    b = s % 2
                    if first and s % XG == 0:
                        transposed(s // XG)
                    pe.wait_ge(w1_here[s], it * 32 + 32)
                    if not first or s >= 2:
                        pe.wait_ge(hid_act[b], it * 2 + s // 2)
                        pe.wait_ge(hid_dve[b], it * 2 + s // 2)
                    for c in range(HC):
                        for kc in range(KC):
                            ins = mm(Hp[b][:, c // 4, (c % 4) * ECOLS:(c % 4 + 1) * ECOLS], w1s[s][:, kc, c * 128:c * 128 + 128],
                                     xeT[:, bass.ds(it * SLOTS + s, 1), kc, :].rearrange("p e n -> p (e n)"), start=kc == 0, stop=kc == KC - 1)
                        if c == HC // 2 - 1:
                            ins.then_inc(hid_full[b], 1)
                    ins.then_inc(hid_full[b], 1)
                    pe.wait_ge(w2_here[s], it * 32 + 32)
                    if not first or s >= 2:
                        pe.wait_ge(y_taken[b], it * 2 + s // 2)
                    for c in range(HC):
                        if c == 0:
                            pe.wait_ge(hid_act[b], it * 2 + s // 2 + 1)
                        if c == HC // 2:
                            pe.wait_ge(hid_dve[b], it * 2 + s // 2 + 1)
                        ins = mm(Yp[b][0:CAP, 0:DIM], hT[:, b, c, :], w2s[s][:, c, :], start=c == 0, stop=c == HC - 1)
                        if c == 0:
                            ins.then_inc(w1_used[s], 1)
                    ins.then_inc(y_full[b], 1)
                    if first and s < 2:
                        transpose(2 * s + 2)
                        transpose(2 * s + 3)

            experts(0, first=True)
            for j in range(2, 6):
                transposed(j)
            with pe.Fori(1, EXP // SLOTS) as it:
                experts(it)

        @block.scalar
        def _(act):
            eng = nc.scalar
            for d, v in row_loads:
                act.dma_start(d, v.partition_broadcast(d.shape[0])).then_inc(l_bias, 16)
            for d, v in table_loads:
                act.dma_start(d[:, :], k[v]).then_inc(l_bias, 16)
            with nc.allow_non_contiguous_dma(reason="small vectors laid over partitions"):
                for d, v in column_loads:
                    act.dma_start(d[:, :], i[v].rearrange("(k p) -> p k", p=128)).then_inc(l_bias, 16)
            act.dma_start(gateW[:, :, :], i["L1_ffn_Wg"].rearrange("(k p) n -> p k n", p=128)).then_inc(l_bias, 16)

            def copy(d, s, scale):
                return eng.activation(d, s, ACT.Copy, scale=scale)

            for u in start:
                if u in x_first:
                    half = u[1]
                    act.wait_ge(xrstd, half + 1)
                    if half:
                        act.wait_ge(xnorm_dve, len(dve_cols[0]))
                        act.wait_ge(xnorm_act, len(act_cols[0]))
                    for w in act_cols[half]:
                        eng.activation(xnv[half][:, w, :].rearrange("p (r q) -> p r q", q=PATCH), xv[half][:, :, w, :], ACT.Identity,
                                       bias=xnb[:, half, w:w + 1], scale=xrs[:, half, w:w + 1]).then_inc(xnorm_act, 1)
                if u not in on_dve:
                    empty_ring(act, copy, u)
            done = {}
            act.wait_ge(tables_ready, 1)
            for kind, l, n in order("act"):
                done[kind] = done.get(kind, 0) + 1
                m = done[kind]
                if (kind, l, n) in uses:
                    b, g = g_use(uses[(kind, l, n)])
                if kind == "lnt":
                    act.wait_ge(g_full[b], g + 1)
                    eng.copy(xnT[:, :, cols(n)], G[b][:, 0:2 * TROWS].rearrange("p (k n) -> p k n", k=KC)[:, :, 0:rows(n)]).then_inc(g_free[b], 1)
                elif kind == "qk":
                    width = gcols(n).stop - gcols(n).start
                    for j, d in ((0, qT), (1, kT)):
                        b, g = g_use(uses[(kind, l, n)] + j)
                        act.wait_ge(g_full[b], g + 1)
                        if l == 0:
                            ins = eng.copy(d[:, :, gcols(n)], G[b][:, 0:2 * width].rearrange("p (k n) -> p k n", k=KC))
                        else:
                            for oc in range(KC):
                                ins = eng.activation(d[:, oc, gcols(n)], G[b][:, oc * width:(oc + 1) * width], ACT.Identity, bias=(bk if j else bq)[:, oc:oc + 1])
                        ins.then_inc(g_free[b], 1)
                elif kind == "v":
                    act.wait_ge(g_full[b], g + 1)
                    if m > 2:
                        act.wait_ge(v_spread[(m - 1) % 2], v_spread_count(m - 3))
                    eng.copy(vt[0:rows(n), (m - 1) % 2, :], G[b][0:rows(n), 0:DIM]).then_inc(g_free[b], 1)
                elif kind == "s":
                    act.wait_ge(p_ready, m)
                    eng.activation(P[0:PROWS, n % 2], P[0:PROWS, n % 2], ACT.Exp).then_inc(p_exp, 1)
                elif kind == "pt":
                    act.wait_ge(pt_full, m)
                    if m > 2:
                        act.wait_ge(o_full, m - 2)
                    eng.copy(PTs[0:TROWS, n % 2].rearrange("p (f j) n -> p f (j n)", f=2), PTp[0:TROWS, :, 0:3 * PROWS]).then_inc(pt_ready, 1)
                elif kind == "ot":
                    act.wait_ge(g_full[b], g + 1)
                    s = G[b][:, 0:2 * PROWS].rearrange("p (f n) -> p f n", f=2)
                    for a, r0 in ((0, 0), (1, BROW)):
                        ins = eng.copy(OT[:, :, n * PCOLS + a * SEQ:n * PCOLS + (a + 1) * SEQ], s[:, :, r0:r0 + SEQ])
                    ins.then_inc(g_free[b], 1)
                elif kind == "ffn":
                    emptied(act, uses[(kind, l, n)])
                    eng.activation(fv[0:rows(n), n % 2, :], fv[0:rows(n), n % 2, :], ACT.Tanh).then_inc(tanh_ready, 1)
                elif kind == "log":
                    act.wait_ge(neg_ready, n + 1)
                    eng.activation(ex[0:rows(n), :], lg[0:rows(n), n % 2, :], ACT.Exp, bias=nmx[0:rows(n), n % 2:n % 2 + 1],
                                   accum_out=se[0:rows(n), n:n + 1]).then_inc(se_ready, 1)
            def empty_group(j):
                act.wait_ge(xe_full[j % 2], j // 2 + 1)
                ne = min(XG, EXP - XG * j)
                eng.copy(xeT[:, XG * j:XG * j + ne, :, 0:CAP], G[j % 2][:, 0:ne * KC * CAP].rearrange("p (e k n) -> p e k n", k=KC, n=CAP)).then_inc(xe_free[j % 2], 1)

            empty_group(0)

            def hidden(it, first=False):
                for b in range(2):
                    act.wait_ge(hid_full[b], it * 2 + 1)
                    if not first:
                        act.wait_ge(y_full[b], it)
                    for c in range(HC // 2):
                        ins = eng.activation(hT[:, b, c, :], Hp[b][:, 0, c * ECOLS:c * ECOLS + CAP], ACT.Relu, bias=b1T[:, bass.ds((it * 2 + b) * HC + c, 1)])
                    ins.then_inc(hid_act[b], 1)
                    if first:
                        empty_group(2 * b + 2)

            hidden(0, first=True)
            with act.Fori(1, EXP // 2) as it:
                hidden(it)

        @block.vector
        def _(dve):
            link = chain(dve, dve_done)
            eng = nc.vector

            def copy(d, s, scale):
                return eng.tensor_copy(d, s) if scale == 1.0 else eng.tensor_scalar(d, s, scale, None, ALU.mult)

            def patch_stats(u):
                for f in range(2):
                    for c in range(CH) if f else range(CH - 1):
                        dve.wait_ge(l_x[u][c], 16)
                    for w in range(HP):
                        ins = eng.bn_stats(xst[:, u, w, f, :], xv[u][:, 24 * f:24 * f + 24, w, :])
                link(ins)
                for w in range(HP):
                    ins = eng.bn_aggr(xmv[:, u, w, :], xst[:, u, w].rearrange("p f s -> p (f s)"))
                ins.then_inc(xstats, 1)

            def normalise(half):
                dve.wait_ge(xrstd, half + 1)
                if half:
                    dve.wait_ge(xnorm_dve, len(dve_cols[0]))
                    dve.wait_ge(xnorm_act, len(act_cols[0]))
                for w in dve_cols[half]:
                    eng.tensor_scalar(xnv[half][:, w, :].rearrange("p (r q) -> p r q", q=PATCH), xv[half][:, :, w, :], xmv[:, half, w, 0:1],
                                      xrs[:, half, w:w + 1], ALU.subtract, ALU.mult).then_inc(xnorm_dve, 1)

            def quantise():
                for name in ("qkv0", "qkv1", "qkv2", "proj"):
                    n = start_at[("T", name)]
                    dve.wait_ge(ring_free[n % 6], n // 6 + 1)
                for w, inv in ((qkvT[:, :, :], 2), (projT[:, :, :], 3)):
                    ins = eng.tensor_scalar(w, w, qs[:, inv:inv + 1], MAGIC, ALU.mult, ALU.add)
                link(ins)
                for w in (qkvT[:, :, :], projT[:, :, :]):
                    ins = eng.tensor_scalar(w, w, MAGIC, -2.0, ALU.subtract, ALU.max)
                link(ins)
                for w, c in ((qkvT[:, :, 0:DIM], 4), (qkvT[:, :, DIM:], 0), (projT[:, :, :], 1)):
                    ins = eng.tensor_scalar(w, w, 2.0, qs[:, c:c + 1], ALU.min, ALU.mult)
                ins.then_inc(quant_ready, 1)

            patch_stats(0)
            normalise(0)
            dve.wait_ge(l_nat[0], 64)
            eng.tensor_copy(causb[:, :], causf)
            dve.wait_ge(l_ident, 16)
            eng.tensor_copy(identb[:, :], ident[:, 0:PROWS]).then_inc(causal_ready, 1)
            for u in start:
                if u == x_first[0]:
                    patch_stats(1)
                    eng.tensor_reduce(asum[:, 0:1], attn_nat, AX.XY, ALU.add, apply_absolute_value=True)
                    eng.tensor_reduce(asum[:, 1:2], proj_nat, AX.XY, ALU.add, apply_absolute_value=True).then_inc(asum_ready, 1)
                elif u == x_first[1]:
                    normalise(1)
                    quantise()
                if u[0] == "sum":
                    n = start_at[u]
                    b = n % 6
                    dve.wait_ge(ring_full[b], n // 6 + 1)
                    for c, size in ((0, 3 * DIM * DIM), (1, DIM * DIM)):
                        ins = eng.tensor_scalar(qs[:, c:c + 1], ring[b][:, c:c + 1], 1.0 / size, 1e-8, ALU.mult, ALU.max)
                    link(ins)
                    eng.tensor_scalar(qs[:, 4:5], qs[:, 0:1], 0.25, None, ALU.mult)
                    link(eng.reciprocal(qs[:, 2:4], qs[:, 0:2]))
                    eng.tensor_copy(qs[:, 6:8], ring[b][:, 0:2]).then_inc(ring_free[b], 1)
                elif u[0] == "bias":
                    n = start_at[u]
                    b = n % 6
                    dve.wait_ge(ring_full[b], n // 6 + 1)
                    dve.wait_ge(l_bias, small_loads)
                    eng.tensor_tensor(biasB[:, :], ring[b][0:TROWS, 0:DIM], biasB[:, :], ALU.add).then_inc(ring_free[b], 1)
                elif u[0] == "bo":
                    n = start_at[u]
                    b = n % 6
                    dve.wait_ge(ring_full[b], n // 6 + 1)
                    eng.tensor_tensor(boB[:, :], ring[b][0:TROWS, 0:DIM], boB[:, :], ALU.add).then_inc(ring_free[b], 1)
                elif u == ("T", WEIGHTS[5]):
                    n = start_at[u]
                    b = n % 6
                    dve.wait_ge(l_bias, small_loads)
                    link(eng.tensor_tensor(hmh[:, :, :], bc(headm[:, :], 1, KC), hmB[:, :].rearrange("p (k a) -> p k a", k=KC), ALU.mult))
                    link(eng.tensor_reduce(hm[:, :], hmh[:, :, :], AX.X, ALU.add))
                    dve.wait_ge(ring_full[b], n // 6 + 1)
                    for kc in range(KC):
                        ins = eng.tensor_scalar(woT[:, kc, :], ring[b][:, kc * DIM:(kc + 1) * DIM], hm[:, kc:kc + 1], None, ALU.mult)
                    ins.then_inc(ring_free[b], 1)
                elif u in on_dve:
                    empty_ring(dve, copy, u)
            dve.wait_ge(tables_ready, 1)
            dve.wait_ge(l_zero, 32)

            normed = [0]

            def stats(src, r, j):
                q = normed[0] % 2
                normed[0] += 1
                if normed[0] > 2:
                    dve.wait_ge(mv_ready, normed[0] - 2)
                link(eng.bn_stats(st[0:r, q, :], src))
                eng.bn_aggr(mv[0:r, j, :], st[0:r, q, :]).then_inc(mv_ready, 1)

            done = {}
            for kind, l, n in order("dve"):
                done[kind] = done.get(kind, 0) + 1
                m = done[kind]
                r = rows(n)
                if (kind, l, n) in uses:
                    b, g = g_use(uses[(kind, l, n)])
                if kind == "tok":
                    dve.wait_ge(g_full[b], g + 1)
                    eng.tensor_tensor(h[0:r, n, :], G[b][0:r, 0:DIM], biasB[0:r, :], ALU.add).then_inc(g_free[b], 1)
                    dve.wait_ge(g_free[b], g + 1)
                    stats(h[0:r, n, :], r, n)
                elif kind == "tokn":
                    dve.wait_ge(rs_ready, rs_rank[("tok", 0, n)])
                    link(eng.scalar_tensor_tensor(out=h[0:r, n, :], in0=h[0:r, n, :], scalar=mv[0:r, n, 0:1], in1=g2B[0:r, :], op0=ALU.subtract, op1=ALU.mult))
                    link(eng.scalar_tensor_tensor(out=h[0:r, n, :], in0=h[0:r, n, :], scalar=rs[0:r, n, :], in1=addA[0:r, :], op0=ALU.mult, op1=ALU.add))
                elif kind == "km" and l == 1:
                    emptied(dve, uses[("qk", l, 2 * n // GROUP_IMGS)] + 1)
                    if m > 2:
                        dve.wait_ge(s_full, m - 2)
                    eng.tensor_tensor(km[:, n % 2, 1], bc(kT[:, 1, n * PCOLS:(n + 1) * PCOLS], 1, 8), bc(headm[:, :], 2, PCOLS), ALU.mult).then_inc(km2_ready, 1)
                elif kind == "lns":
                    stats(h[0:r, n, :], r, (l + 1) * TILES + n)
                elif kind == "lnx":
                    dve.wait_ge(rs_ready, rs_rank[("lns", l, n)])
                    if m > XNB:
                        emptied(dve, uses[lnt_tasks[m - 1 - XNB]])
                    j = (l + 1) * TILES + n
                    d = xnd[0:r, n, :] if l == 3 else xn[0:r, (m - 1) % XNB, :]
                    eng.tensor_scalar(d, h[0:r, n, :], mv[0:r, j, 0:1], rs[0:r, j, :], ALU.subtract, ALU.mult).then_inc(xn_ready, 1)
                elif kind == "s":
                    dve.wait_ge(s_full, m)
                    sv = Sp[0:PROWS, :, 0:8 * SEQ].rearrange("p f (h n) -> p f h n", h=8)
                    mxv = mx[:, n % 2, :].rearrange("p (f h) -> p f h", f=2)
                    link(eng.tensor_reduce(mxv, sv, AX.X, ALU.max))
                    if m > 2:
                        dve.wait_ge(pt_full, m - 2)
                    eng.tensor_tensor(P[0:PROWS, n % 2].rearrange("p (f h) n -> p f h n", f=2), sv, bc(mxv, 3, SEQ), ALU.subtract).then_inc(p_ready, 1)
                elif kind == "pv":
                    dve.wait_ge(o_full, m)
                    if m > 2:
                        emptied(dve, uses[("ot",) + divmod(m - 3, PAIRS)])
                    ov = Op[0:PROWS, 0:HEADS * VW].rearrange("p (h d) -> p h d", h=HEADS)
                    link(eng.reciprocal(rec[:, n % 2, :], ov[:, :, HD]))
                    eng.tensor_tensor(On[0:PROWS, n % 2, :].rearrange("p (h d) -> p h d", h=HEADS), ov[:, :, 0:HD], bc(rec[:, n % 2, :], 2, HD),
                                      ALU.mult).then_inc(on_ready, 1)
                elif kind == "proj":
                    dve.wait_ge(g_full[b], g + 1)
                    if l == 1:
                        dve.wait_ge(bo_added, n + 1)
                    eng.tensor_tensor(h[0:r, n, :], h[0:r, n, :], G[b][0:r, 0:DIM], ALU.add).then_inc(g_free[b], 1)
                    dve.wait_ge(g_free[b], g + 1)
                elif kind == "ffn":
                    dve.wait_ge(g_full[b], g + 1)
                    eng.tensor_tensor(fv[0:r, n % 2, :], G[b][0:r, 0:DIM], fbB[0:r, :], ALU.add).then_inc(g_free[b], 1)
                elif kind == "ffnr":
                    dve.wait_ge(tanh_ready, n + 1)
                    link(eng.tensor_tensor(h[0:r, n, :], h[0:r, n, :], fv[0:r, n % 2, :], ALU.add))
                elif kind == "log":
                    q = n % 2
                    dve.wait_ge(g_full[b], g + 1)
                    if n >= 2:
                        dve.wait_ge(se_ready, n - 1)
                    eng.tensor_tensor(lg[0:r, q, :], G[b][0:r, 0:EXP], bgB[0:r, :], ALU.add).then_inc(g_free[b], 1)
                    dve.wait_ge(g_free[b], g + 1)
                    link(eng.max(top[0:r, q, :], lg[0:r, q, :]))
                    eng.tensor_scalar(nmx[0:r, q:q + 1], top[0:r, q, 0:1], -1.0, None, ALU.mult).then_inc(neg_ready, 1)
                    link(eng.max_index(ti[0:r, q, :], top[0:r, q, :], lg[0:r, q, :]))
                    link(eng.tensor_copy(idf[0:r, n:n + 1], ti[0:r, q, 0:1]))
                    eng.tensor_scalar(oh[0:r, n, :], iota[0:r, :], idf[0:r, n:n + 1], None, ALU.is_equal).then_inc(oh_ready, 1)
                elif kind == "cnt":
                    dve.wait_ge(g_full[b], g + 1)
                    dve.wait_ge(oh_ready, n + 1)
                    if n:
                        dve.wait_ge(pos_ready, n)
                    if n >= 2:
                        dve.wait_ge(slots_ready, n - 1)
                    eng.tensor_tensor(ohc[0:r, :], oh[0:r, n, :], G[b][0:r, 0:EXP], ALU.mult).then_inc(g_free[b], 1)
                    dve.wait_ge(g_free[b], g + 1)
                    eng.tensor_reduce(pos[0:r, n % 2:n % 2 + 1], ohc[0:r, :], AX.X, ALU.add)
                    dve.wait_ge(se_ready, n + 1)
                    eng.reciprocal(tokens[0:r, n, 2 * DIM + 1:ROW], se[0:r, n:n + 1]).then_inc(pos_ready, 1)

            def empty_group(j):
                dve.wait_ge(xe_full[j % 2], j // 2 + 1)
                ne = min(XG, EXP - XG * j)
                eng.tensor_copy(xeT[:, XG * j:XG * j + ne, :, 0:CAP], G[j % 2][:, 0:ne * KC * CAP].rearrange("p (e k n) -> p e k n", k=KC, n=CAP)).then_inc(xe_free[j % 2], 1)

            empty_group(1)

            def hidden(it, first=False):
                for b in range(2):
                    dve.wait_ge(hid_full[b], it * 2 + 2)
                    if not first:
                        dve.wait_ge(y_full[b], it)
                    for c in range(HC // 2, HC):
                        ins = eng.tensor_scalar(hT[:, b, c, :], Hp[b][:, 1, (c - 4) * ECOLS:(c - 4) * ECOLS + CAP], b1T[:, bass.ds((it * 2 + b) * HC + c, 1)], 0.0,
                                                ALU.add, ALU.max)
                    ins.then_inc(hid_dve[b], 1)
                    dve.wait_ge(y_full[b], it + 1)
                    dve.wait_ge(b2_here[b], it * 16 + 16)
                    if not first:
                        dve.wait_ge(r_stored[b], it * 16)
                    e = it * 2 + b
                    slots = xe[0:CAP, bass.ds(e, 1), :].rearrange("p e n -> p (e n)")
                    eng.tensor_tensor(ysb[0:CAP, b, :], Yp[b][0:CAP, 0:DIM], b2B[0:CAP, b, :], ALU.add).then_inc(y_taken[b], 1)
                    dve.wait_ge(y_taken[b], it + 1)
                    if first:
                        dve.wait_ge(rest_loaded, 32)
                    eng.scalar_tensor_tensor(out=ysb[0:CAP, b, :], in0=ysb[0:CAP, b, :], scalar=slots[:, 2 * DIM + 1:ROW], in1=slots[:, 0:DIM], op0=ALU.mult, op1=ALU.add)
                    eng.tensor_copy(idx[:, b:b + 1], slots[:, 2 * DIM:2 * DIM + 1]).then_inc(r_ready[b], 1)
                    if first:
                        empty_group(2 * b + 3)

            hidden(0, first=True)
            with dve.Fori(1, EXP // 2) as it:
                hidden(it)


def kernel(**inputs):
    import numpy as _np
    import concourse.bacc as _bacc
    from concourse.bass_utils import run_bass_kernel_spmd as _run

    nc = _bacc.Bacc("TRN2", target_bir_lowering=False, num_devices=1)
    arrays, args, tables = {}, {}, {}
    for name in INS:
        arrays[f"in_{name}"] = a = _np.ascontiguousarray(inputs[name])
        args[name] = nc.dram_tensor(f"in_{name}", a.shape, mybir.dt.from_np(a.dtype), kind="ExternalInput").ap()
    for name, a in constants().items():
        arrays[name] = a
        tables[name] = nc.dram_tensor(name, a.shape, mybir.dt.from_np(a.dtype), kind="ExternalInput").ap()
    out = nc.dram_tensor("out", (NIMG, SEQ, DIM), F32, kind="ExternalOutput").ap()
    tower(nc, args, tables, out)
    r = _run(nc, [arrays], core_ids=[0])
    return r.results[0]["out"]
```
